# Optimizing a Trainium2 kernel written in Bass

```python
import numpy as np
import jax
import jax.numpy as jnp

def _softmax(x, axis=-1):
    return jax.nn.softmax(x, axis=axis)

def _gelu(x):
    return jax.nn.gelu(x, approximate=True)

def _silu(x):
    return jax.nn.silu(x)

def _sigmoid(x):
    return jax.nn.sigmoid(x)

def _layernorm(x, axis=-1, eps=1e-05):
    m = jnp.mean(x, axis=axis, keepdims=True)
    v = jnp.var(x, axis=axis, keepdims=True)
    return (x - m) / jnp.sqrt(v + eps)

def _scatter_add(tgt, idx, src, axis=0):
    return tgt.at[idx].add(src)

def _segment_sum(src, seg, n):
    return jax.ops.segment_sum(src, seg, n)
kernel_name = 'mk_prb_d1_jaxref_r8_ab3474'

def setup_inputs(seed: int=0):
    np.random.seed(seed)
    _w = jnp.asarray

    def _L0_attn_setup():
        import jax, jax.numpy as jnp
        import numpy as np
        HEADS = 8
        CHUNK = 32

        def _gammas(heads):
            betas = jnp.linspace(np.log2(1.0 / 32.0), np.log2(1.0 / 512.0), heads)
            return 1.0 - jnp.exp2(betas)
        key = jax.random.key(seed)
        ks = jax.random.split(key, 4)
        H = 256
        x = jax.random.normal(ks[0], (4, 512, H), dtype=jnp.float32)
        sc = 1.0 / np.sqrt(H)
        Wq = jax.random.normal(ks[1], (H, H), dtype=jnp.float32) * sc
        Wk = jax.random.normal(ks[2], (H, H), dtype=jnp.float32) * sc
        Wv = jax.random.normal(ks[3], (H, H), dtype=jnp.float32) * sc
        z = jnp.zeros((H,), dtype=jnp.float32)
        return {'x': x, 'Wq': Wq, 'bq': z, 'Wk': Wk, 'bk': z, 'Wv': Wv, 'bv': z}
    _L0_attn_in = _L0_attn_setup()

    def _L0_ffn_setup():
        import jax, jax.numpy as jnp
        import numpy as np
        HIDDEN = 256
        FFN = 176
        N_EXPERTS = 64
        TOP_K = 6
        N_SHARED = 2
        SHARED_FFN = FFN * N_SHARED
        ROUTED_SCALING = 1.0
        EPS = 1e-20

        def _moe_forward(x, gate_w, w_gate_up, w_down, ws_gate_up, ws_down):
            T = x.shape[0]
            logits = jnp.einsum('th,eh->te', x.astype(jnp.float32), gate_w.astype(jnp.float32))
            scores = jax.nn.softmax(logits, axis=-1)
            topk_w, topk_ids = jax.lax.top_k(scores, TOP_K)
            topk_w = topk_w / (jnp.sum(topk_w, axis=-1, keepdims=True) + EPS)
            topk_w = topk_w * ROUTED_SCALING
            comb = jnp.zeros((T, N_EXPERTS), dtype=x.dtype)
            comb = comb.at[jnp.arange(T)[:, None], topk_ids].add(topk_w.astype(x.dtype))
            gu = jnp.einsum('th,efh->tef', x, w_gate_up)
            g, u = (gu[..., :FFN], gu[..., FFN:])
            act = jax.nn.silu(g) * u
            act = act * comb[:, :, None]
            routed = jnp.einsum('tef,ehf->th', act, w_down)
            sgu = jnp.einsum('th,fh->tf', x, ws_gate_up)
            sg, su = (sgu[..., :SHARED_FFN], sgu[..., SHARED_FFN:])
            shared = jnp.einsum('tf,hf->th', jax.nn.silu(sg) * su, ws_down)
            return routed + shared
        key = jax.random.key(seed)
        k0, k1, k2, k3, k4, k5 = jax.random.split(key, 6)
        hidden_states = jax.random.normal(k0, (1, 32, HIDDEN), dtype=jnp.float32)
        gate_w = jax.random.normal(k1, (N_EXPERTS, HIDDEN), dtype=jnp.float32) * 0.05
        w_gate_up = jax.random.normal(k2, (N_EXPERTS, 2 * FFN, HIDDEN), dtype=jnp.float32) * 0.02
        w_down = jax.random.normal(k3, (N_EXPERTS, HIDDEN, FFN), dtype=jnp.float32) * 0.02
        ws_gate_up = jax.random.normal(k4, (2 * SHARED_FFN, HIDDEN), dtype=jnp.float32) * 0.02
        ws_down = jax.random.normal(k5, (HIDDEN, SHARED_FFN), dtype=jnp.float32) * 0.02
        return {'hidden_states': hidden_states, 'gate_w': gate_w, 'w_gate_up': w_gate_up, 'w_down': w_down, 'ws_gate_up': ws_gate_up, 'ws_down': ws_down}
    _L0_ffn_in = _L0_ffn_setup()
    _d = {'L0_attn_x': _L0_attn_in['x'], 'L0_attn_Wq': _L0_attn_in['Wq'], 'L0_attn_bq': _L0_attn_in['bq'], 'L0_attn_Wk': _L0_attn_in['Wk'], 'L0_attn_bk': _L0_attn_in['bk'], 'L0_attn_Wv': _L0_attn_in['Wv'], 'L0_attn_bv': _L0_attn_in['bv'], 'L0_ffn_gate_w': _L0_ffn_in['gate_w'], 'L0_ffn_w_gate_up': _L0_ffn_in['w_gate_up'], 'L0_ffn_w_down': _L0_ffn_in['w_down'], 'L0_ffn_ws_gate_up': _L0_ffn_in['ws_gate_up'], 'L0_ffn_ws_down': _L0_ffn_in['ws_down']}
    _x0 = _d['L0_attn_x']
    _d['L0_attn_x'] = jax.random.normal(jax.random.fold_in(jax.random.key(seed), 1), (2, 512, 256), dtype=_x0.dtype)
    del _x0
    return _d

def reference(L0_attn_x, L0_attn_Wq, L0_attn_bq, L0_attn_Wk, L0_attn_bk, L0_attn_Wv, L0_attn_bv, L0_ffn_gate_w, L0_ffn_w_gate_up, L0_ffn_w_down, L0_ffn_ws_gate_up, L0_ffn_ws_down):

    def _L0_attn_ref(x, Wq, bq, Wk, bk, Wv, bv):
        import jax, jax.numpy as jnp
        import numpy as np
        HEADS = 8
        CHUNK = 32

        def _gammas(heads):
            betas = jnp.linspace(np.log2(1.0 / 32.0), np.log2(1.0 / 512.0), heads)
            return 1.0 - jnp.exp2(betas)
        B, S, H = x.shape
        h, C = (HEADS, CHUNK)
        d = H // h
        N = S // C
        g = _gammas(h)
        q = x @ Wq + bq
        k = x @ Wk + bk
        v = x @ Wv + bv

        def split(t):
            return t.reshape(B, N, C, h, d).transpose(1, 0, 3, 2, 4)
        qc, kc, vc = (split(q), split(k), split(v))
        idx = jnp.arange(C)
        i, j = (idx[:, None], idx[None, :])
        D = jnp.where(i >= j, g[:, None, None] ** (i - j).astype(jnp.float32), 0.0)
        cross_scale = g[:, None] ** (idx + 1).astype(jnp.float32)
        kv_scale = g[:, None] ** (C - 1 - idx).astype(jnp.float32)
        chunk_decay = g ** C

        def step(Sstate, qkv):
            qi, ki, vi = qkv
            attn = jnp.einsum('bhid,bhjd->bhij', qi, ki) * D
            inner = jnp.einsum('bhij,bhjd->bhid', attn, vi)
            cross = jnp.einsum('bhid,bhde->bhie', qi * cross_scale[:, :, None], Sstate)
            S_new = chunk_decay[:, None, None] * Sstate + jnp.einsum('bhjd,bhje->bhde', ki * kv_scale[:, :, None], vi)
            return (S_new, inner + cross)
        S0 = jnp.zeros((B, h, d, d), dtype=x.dtype)
        _, outs = jax.lax.scan(step, S0, (qc, kc, vc))
        return outs.transpose(1, 0, 3, 2, 4).reshape(B, S, H)

    def _L0_ffn_ref(hidden_states, gate_w, w_gate_up, w_down, ws_gate_up, ws_down):
        import jax, jax.numpy as jnp
        import numpy as np
        HIDDEN = 256
        FFN = 176
        N_EXPERTS = 64
        TOP_K = 6
        N_SHARED = 2
        SHARED_FFN = FFN * N_SHARED
        ROUTED_SCALING = 1.0
        EPS = 1e-20

        def _moe_forward(x, gate_w, w_gate_up, w_down, ws_gate_up, ws_down):
            T = x.shape[0]
            logits = jnp.einsum('th,eh->te', x.astype(jnp.float32), gate_w.astype(jnp.float32))
            scores = jax.nn.softmax(logits, axis=-1)
            topk_w, topk_ids = jax.lax.top_k(scores, TOP_K)
            topk_w = topk_w / (jnp.sum(topk_w, axis=-1, keepdims=True) + EPS)
            topk_w = topk_w * ROUTED_SCALING
            comb = jnp.zeros((T, N_EXPERTS), dtype=x.dtype)
            comb = comb.at[jnp.arange(T)[:, None], topk_ids].add(topk_w.astype(x.dtype))
            gu = jnp.einsum('th,efh->tef', x, w_gate_up)
            g, u = (gu[..., :FFN], gu[..., FFN:])
            act = jax.nn.silu(g) * u
            act = act * comb[:, :, None]
            routed = jnp.einsum('tef,ehf->th', act, w_down)
            sgu = jnp.einsum('th,fh->tf', x, ws_gate_up)
            sg, su = (sgu[..., :SHARED_FFN], sgu[..., SHARED_FFN:])
            shared = jnp.einsum('tf,hf->th', jax.nn.silu(sg) * su, ws_down)
            return routed + shared
        B, S, H = hidden_states.shape
        x = hidden_states.reshape(-1, H)
        out = _moe_forward(x, gate_w, w_gate_up, w_down, ws_gate_up, ws_down)
        return out.reshape(B, S, H)
    x = L0_attn_x
    xn = _layernorm(x, axis=-1)
    x = x + _L0_attn_ref(xn, L0_attn_Wq, L0_attn_bq, L0_attn_Wk, L0_attn_bk, L0_attn_Wv, L0_attn_bv) + _L0_ffn_ref(xn, L0_ffn_gate_w, L0_ffn_w_gate_up, L0_ffn_w_down, L0_ffn_ws_gate_up, L0_ffn_ws_down)
    return x

_drawn_inputs = setup_inputs


def setup_inputs(seed=0):
    import zlib

    import numpy as np

    out = dict(_drawn_inputs(seed))
    spreads = {'L0_attn_bq': (0.0, 0.1), 'L0_attn_bk': (0.0, 0.1), 'L0_attn_bv': (0.0, 0.1)}
    factors = {'L0_ffn_gate_w': 8.0,
     'L0_ffn_w_gate_up': 8.0,
     'L0_ffn_w_down': 8.0,
     'L0_ffn_ws_gate_up': 8.0,
     'L0_ffn_ws_down': 8.0}
    for name, (base, spread) in spreads.items():
        noise = np.random.default_rng([zlib.crc32(name.encode()), seed]).standard_normal(out[name].shape)
        drawn = base * np.exp(spread * noise) if base else spread * noise
        out[name] = jnp.asarray(drawn.astype(out[name].dtype))
    for name, factor in factors.items():
        out[name] = (out[name] * factor).astype(out[name].dtype)
    return out
```

```python
from contextlib import ExitStack

import concourse.bass as bass
from concourse import mybir

P = 128
T, H = 1024, 256
NC = T // P
E, TOPK, F = 64, 6, 176
FS = 352
HEADS, D = 8, 32
HG = P // D
NG = H // P
SEQ_CHUNKS = 4
ROW = H + E
RING = 16
F1 = P
F2 = F - F1
W1C = 2 * 2 * F + H
ACC_ROWS = T + P
BIG = 3.0e38
UNCHOSEN = 4096.0
SKIP = 4096

C32 = {}
_at = 0
for _n, _w in (("ident", P), ("mask8", 8), ("padrow", 1), ("iota_e", E), ("iota_s", P), ("hmask", HG),
               ("gc", NG), ("bdmask", P), ("kscale", H), ("qscale", NG * P), ("decay", HEADS * P)):
    C32[_n] = (_at, _at + _w)
    _at += _w
C32W = _at
C16 = {}
_at = 0
for _n, _w in (("tri", P), ("ones", P), ("place", 240), ("tok", NC * E), ("tokc", NC)):
    C16[_n] = (_at, _at + _w)
    _at += _w
C16W = _at


def build(nc, x, wq, wkv, bq, bkv, gate, sgu, sdn, w1, w2, c32, c16, out):
    f32, f16, i32 = mybir.dt.float32, mybir.dt.float16, mybir.dt.int32
    ALU = mybir.AluOpType
    ACT = mybir.ActivationFunctionType
    AX = mybir.AxisListType.X

    table = nc.dram_tensor("table", [T, ROW], f32, kind="Internal").ap()
    acc = [nc.dram_tensor(f"acc{k}", [ACC_ROWS, H], f32, kind="Internal").ap() for k in range(2)]

    with ExitStack() as ctx:
        def sb(name, shape, dt=f32):
            return ctx.enter_context(nc.sbuf_tensor(name, shape, dt))

        def sem(name):
            return ctx.enter_context(nc.semaphore(name))

        k32 = sb("k32", [P, C32W])
        k16 = sb("k16", [P, C16W], f16)

        def c_32(n):
            return k32[:, C32[n][0]:C32[n][1]]

        def c_16(n):
            return k16[:, C16[n][0]:C16[n][1]]

        ident = c_32("ident")

        def slab(name, words):
            return sb(name, [P, words])

        def view(s, at, *dims, dt=f32):
            n = 1
            for d in dims:
                n *= d
            v = s[:, at:at + n * mybir.dt.size(dt) // 4]
            if dt != f32:
                v = v.bitcast(dt)
            names = "abcd"[:len(dims)]
            return v.rearrange(f"p ({' '.join(names)}) -> p {' '.join(names)}", **dict(zip(names, dims)))

        tab_slab = slab("tab_slab", NC * ROW)
        tab = view(tab_slab, 0, NC, ROW)
        x_again = view(tab_slab, 0, NC, H)
        x_slab = slab("x_slab", NC * H)
        x_sb = view(x_slab, 0, NC, H)
        qT = view(x_slab, 0, NG, T)
        xnT = sb("xnT", [P, NG, T])
        stats = sb("stats", [P, NC, 6])
        mv = sb("mv", [P, NC, 2])
        rs = sb("rs", [P, 4, NC])
        gate_sb = sb("gate_sb", [P, NG, E])
        wq_sb = sb("wq_sb", [P, NG, H])
        wkv_sb = sb("wkv_sb", [P, NG, 2 * H])
        bq_sb = sb("bq_sb", [P, NG])
        bkv_sb = sb("bkv_sb", [P, 2 * H])
        sdn_sb = sb("sdn_sb", [P, 3, H])
        LG = NC * (E + 2)
        NE = NC * E
        route = slab("route", 2 * LG + 2 * NE)
        lg = view(route, 0, NC, E + 2)
        lgm = view(route, LG, NC, E + 2)
        ex = view(route, 2 * LG, NC, E)
        exm = view(route, 2 * LG + NE, NC, E)
        rank_i = view(route, 0, NE, dt=i32)
        lo_i = view(route, NE, NE, dt=i32)
        hi_i = view(route, 2 * NE, NE, dt=i32)
        lo_h = view(route, 3 * NE, NE, dt=f16)
        hi_h = view(route, 3 * NE + NE // 2, NE, dt=f16)
        ov_sel = view(route, NE, NC, E)
        ov_hot = view(route, 2 * NE, NC, P, dt=f16)
        rank_f = sb("rank_f", [P, NE])
        top8 = sb("top8", [P, NC, 8])
        sm = sb("sm", [P, 4, NC])
        chosen = sb("chosen", [P, NC, E], f16)
        early = slab("early", 24 * NE // 2)
        zero = view(early, 0, ACC_ROWS // P, H)
        lo_hot = view(early, 0, NC * 8, 16, 8, dt=f16)
        hi_hot = view(early, 16 * NE // 2, 8, NC, E, dt=f16)
        acc_sb = [view(early, 0, NC, H), view(early, NC * H, NC, H)]
        sgu_sb = view(early, 2 * NC * H, NG, 2 * FS)
        res = view(early, 2 * NC * H + NG * 2 * FS, 2, H)
        diag = sb("diag", [P, 8, 8, 8], f16)
        slot_t = sb("slot_t", [P, 2, E])
        gidx = sb("gidx", [P, E], i32)
        sidx = sb("sidx", [P, E], i32)
        ov = sb("ov", [P, 5, E])
        ov_ones = sb("ov_ones", [P, E])
        ov_n = sb("ov_n", [1, 1], i32)
        ov_e = sb("ov_e", [1, 1], i32)
        ov_j = sb("ov_j", [P, 1])
        ov_s = sb("ov_s", [P, 8])
        ov_rank = sb("ov_rank", [P, NC])
        ov_adj = sb("ov_adj", [P, NC])
        ov_idx = sb("ov_idx", [P, 2], i32)
        ov_t = sb("ov_t", [P, 2])
        ov_comb = sb("ov_comb", [P, E])
        w1_slab = slab("w1_slab", RING * W1C)
        w1_sb = view(w1_slab, 0, RING, W1C)
        qbd = view(w1_slab, 0, NG, NC * HG, P)
        qsT = view(w1_slab, NG * NC * HG * P, NG, T)
        kT = view(w1_slab, NG * NC * HG * P + NG * T, NG, T)
        sact = view(w1_slab, NG * NC * HG * P + 2 * NG * T, 3, T)
        w2_slab = slab("w2_slab", RING * H)
        w2_sb = view(w2_slab, 0, RING, H)[0:F2]
        ks = view(w2_slab, 0, NC, H)
        stmp = view(w2_slab, NC * H, 2, 512)
        pT = view(w2_slab, NC * H + 1024, 2, HG * P)
        gcol = sb("gcol", [P, 4], i32)
        scol = sb("scol", [P, 4], i32)
        rows = sb("rows", [P, 4, ROW])
        xT = sb("xT", [P, 2, H])
        sg = sb("sg", [P, 2, F])
        act = sb("act", [P, 2, 2 * P])
        aT = sb("aT", [P, 2, 2 * P])
        y = sb("y", [P, 4, H])
        kv = sb("kv", [P, NC, 2 * H])
        state = sb("state", [P, 2, NG, P])
        st_t = sb("st_t", [P, P])

        ps = [ctx.enter_context(nc.psum_tensor(f"ps{b}", [P, 512], f32)) for b in range(8)]

        x_in = [sem(f"x_in{n}") for n in range(4)]
        ident_in = sem("ident_in")
        c16_in = sem("c16_in")
        c32_in = sem("c32_in")
        gate_in = sem("gate_in")
        wq_in = sem("wq_in")
        wkv_in = sem("wkv_in")
        bias_in = sem("bias_in")
        shared_in = sem("shared_in")
        w_in = [sem(f"w_in{s}") for s in range(RING)]
        dve_step = sem("dve_step")
        pool_step = sem("pool_step")
        var_ready, std_ready = sem("var_ready"), sem("std_ready")
        xn_ready = sem("xn_ready")
        xnT_ps, xnT_a, xnT_v = sem("xnT_ps"), sem("xnT_a"), sem("xnT_v")
        logits_ps = sem("logits_ps")
        shifted_ready, ex_ready = sem("shifted_ready"), sem("ex_ready")
        comb_ready, table_out = sem("comb_ready"), sem("table_out")
        chosen_ready, rank_ps = sem("chosen_ready"), sem("rank_ps")
        hot_ready, diag_ps, diag_ready, slot_ps = sem("hot_ready"), sem("diag_ps"), sem("diag_ready"), sem("slot_ps")
        ov_ready = sem("ov_ready")
        zero_ready = sem("zero_ready")
        q_ps, q_sb = sem("q_ps"), sem("q_sb")
        kv_ps, kv_sb = sem("kv_ps"), sem("kv_sb")
        rows_in = [sem(f"rows_in{r}") for r in range(4)]
        gcol_ready, scol_ready = sem("gcol_ready"), sem("scol_ready")
        xT_ps, xT_sb = sem("xT_ps"), sem("xT_sb")
        gu_ps, sg_sb, act_sb = sem("gu_ps"), sem("sg_sb"), sem("act_sb")
        aT_ps, aT_sb = sem("aT_ps"), sem("aT_sb")
        y_ps, y_sb = sem("y_ps"), sem("y_sb")
        acc_done = [sem("acc_done0"), sem("acc_done1")]
        act_zero = sem("act_zero")
        ov_hot_ready, ov_list_ps, ov_idx_ready, ov_expert_ready = (
            sem("ov_hot_ready"), sem("ov_list_ps"), sem("ov_idx_ready"), sem("ov_expert_ready"))
        ov_rows_in, ov_w_in = sem("ov_rows_in"), sem("ov_w_in")
        ov_comb_ready = sem("ov_comb_ready")
        acc_in, x_again_in = sem("acc_in"), sem("x_again_in")
        sgu_ps, stmp_sb, sact_sb = sem("sgu_ps"), sem("stmp_sb"), sem("sact_sb")
        kvb_ready, qbd_ready, qs_ready, ks_ready = sem("kvb_ready"), sem("qbd_ready"), sem("qs_ready"), sem("ks_ready")
        kT_ps, kT_a, kT_v = sem("kT_ps"), sem("kT_a"), sem("kT_v")
        s_ps, p_sb = sem("s_ps"), sem("p_sb")
        o_ps, st_ps, st_sb = sem("o_ps"), sem("st_ps"), sem("st_sb")
        xab_ready, res_sb = sem("xab_ready"), sem("res_sb")
        out_done = [sem("out_done0"), sem("out_done1")]
        sp_waited, pool_waited = sem("sp_waited"), sem("pool_waited")

        x_v = x.rearrange("(c p) h -> p c h", p=P)
        out_v = out.rearrange("(c p) h -> p c h", p=P)
        table_v = table.rearrange("(c p) h -> p c h", p=P)
        acc_v = [a.rearrange("(c p) h -> p c h", p=P) for a in acc]

        def bc(ap, shape):
            return ap.unsqueeze(2).to_broadcast(shape)

        block = ctx.enter_context(nc.Block())

        @block.sync
        def _(sp):
            for n in range(4):
                sp.dma_start(x_sb[:, 2 * n:2 * n + 2, :], x_v[:, 2 * n:2 * n + 2, :]).then_inc(x_in[n], 16)
            sp.dma_start(k32[:, 0:P], c32[:, 0:P]).then_inc(ident_in, 16)
            sp.dma_start(gate_sb[:], gate).then_inc(gate_in, 16)
            sp.dma_start(wq_sb[:], wq).then_inc(wq_in, 16)
            sp.dma_start(bq_sb[:], bq).then_inc(bias_in, 16)
            sp.dma_start(bkv_sb[:], bkv.partition_broadcast(P)).then_inc(bias_in, 16)
            sp.dma_start(k16[:], c16).then_inc(c16_in, 16)
            sp.dma_start(wkv_sb[:], wkv).then_inc(wkv_in, 16)
            sp.dma_start(k32[:, P:C32W], c32[:, P:C32W]).then_inc(c32_in, 16)

            def load_expert(slot, e):
                sp.dma_start(w1_sb[:, slot, :], w1[e, :, :]).then_inc(w_in[slot], 16)
                sp.dma_start(w2_sb[:, slot, :], w2[e, :, :]).then_inc(w_in[slot], 16)

            for s in range(RING):
                load_expert(s, s)
            with sp.Fori(0, E // RING - 1) as i:
                for s in range(RING):
                    sp.wait_ge(y_ps, i * RING + (s + 1))
                    e = i * RING + (RING + s)
                    sp.dma_start(w1_sb[:, s, :], w1[bass.ds(e, 1), :, :].rearrange("a p c -> p (a c)"))\
                        .then_inc(w_in[s], 16)
                    sp.dma_start(w2_sb[:, s, :], w2[bass.ds(e, 1), :, :].rearrange("a p c -> p (a c)"))\
                        .then_inc(w_in[s], 16)
            sp.wait_ge(table_out, 16)
            sp.dma_start(x_again, x_v).then_inc(x_again_in, 16)
            sp.dma_start(sgu_sb[:], sgu).then_inc(shared_in, 16)
            sp.dma_start(sdn_sb[:, 0:2, :], sdn[0:2 * P, :].rearrange("(c p) h -> p c h", p=P)).then_inc(shared_in, 16)
            sp.dma_start(sdn_sb[0:FS - 2 * P, 2, :], sdn[2 * P:FS, :]).then_inc(shared_in, 16)

            sp.wait_ge(ov_ready, 1)
            n_ov = sp.value_load(ov_n[0:1, 0:1], min_val=0, max_val=E - 1)
            with sp.If(n_ov > 0):
                with sp.Fori(0, n_ov) as j:
                    sp.wait_ge(y_ps, j + E)
                    sp.sem_inc(sp_waited, 1)
                    sp.wait_ge(ov_expert_ready, j + 1)
                    sp.sem_inc(sp_waited, 1)
                    e = sp.value_load(ov_e[0:1, 0:1], min_val=0, max_val=E - 1)
                    sp.dma_start(w1_sb[:, 0, :], w1[bass.ds(e, 1), :, :].rearrange("a p c -> p (a c)"))\
                        .then_inc(ov_w_in, 16)
                    sp.dma_start(w2_sb[:, 0, :], w2[bass.ds(e, 1), :, :].rearrange("a p c -> p (a c)"))\
                        .then_inc(ov_w_in, 16)

            sp.wait_ge(acc_done[0], n_ov * 16 + 16 * (E // 2 + 1))
            sp.wait_ge(acc_done[1], 16 * (E // 2 + 1))
            for k in range(2):
                sp.dma_start(acc_sb[k], acc_v[k][:, 0:NC, :]).then_inc(acc_in, 16)
            for c in range(NC):
                sp.wait_ge(res_sb, c + 1)
                sp.dma_start(out_v[:, c, :], res[:, c % 2, :]).then_inc(out_done[c % 2], 16)
            for k in range(2):
                sp.wait_ge(out_done[k], 16 * (NC // 2))

        @block.gpsimd
        def _(pool):
            nc.gpsimd.memset(zero, 0.0).then_inc(zero_ready, 1)
            nc.gpsimd.memset(rows[:], 0.0).then_inc(zero_ready, 1)
            nc.gpsimd.memset(act[:], 0.0).then_inc(act_zero, 1)
            pool.wait_ge(zero_ready, 2)
            for k in range(2):
                pool.dma_start(acc_v[k], zero).then_inc(acc_done[k], 16)
            pool.wait_ge(comb_ready, 1)
            pool.dma_start(table_v, tab).then_inc(table_out, 16)
            pool.wait_ge(table_out, 16)

            def gather(r):
                pool.indirect_dma_start(
                    out=rows[:, r, :], out_offset=None, in_=table,
                    in_offset=bass.IndirectOffsetOnAxis(ap=gcol[:, r:r + 1], axis=0),
                    bounds_check=T - 1, oob_is_err=False).then_inc(rows_in[r], 16)

            def scatter(k, r):
                pool.indirect_dma_start(
                    out=acc[k], out_offset=bass.IndirectOffsetOnAxis(ap=scol[:, r:r + 1], axis=0),
                    in_=y[:, r, :], in_offset=None, compute_op=ALU.add).then_inc(acc_done[k], 16)

            pool.wait_ge(gcol_ready, 1)
            for r in range(4):
                gather(r)
            def expert_pool(t, k, last):
                if not last:
                    pool.wait_ge(gcol_ready, t + 2)
                    pool.sem_inc(pool_waited, 1)
                    gather(k % 4)
                pool.wait_ge(y_sb, t + 1)
                pool.wait_ge(scol_ready, t + 1)
                prev = (t - k) * 8 + 16 * (k // 2 + 1)
                pool.wait_ge(acc_done[k % 2], prev)
                pool.sem_inc(pool_waited, 1)
                scatter(k % 2, k % 4)

            with pool.Fori(0, E // RING - 1) as i:
                for k in range(RING):
                    expert_pool(i * RING + k, k, False)
            for k in range(RING):
                expert_pool(E - RING + k, k, k >= RING - 4)

            pool.wait_ge(ov_ready, 1)
            n_ov = pool.value_load(ov_n[0:1, 0:1], min_val=0, max_val=E - 1)
            with pool.If(n_ov > 0):
                with pool.Fori(0, n_ov) as j:
                    pool.wait_ge(ov_idx_ready, j + 1)
                    pool.sem_inc(pool_waited, 1)
                    pool.indirect_dma_start(
                        out=rows[:, 0, :], out_offset=None, in_=table,
                        in_offset=bass.IndirectOffsetOnAxis(ap=ov_idx[:, 0:1], axis=0),
                        bounds_check=T - 1, oob_is_err=False).then_inc(ov_rows_in, 16)
                    pool.wait_ge(y_sb, j + (E + 1))
                    pool.wait_ge(acc_done[0], j * 16 + 16 * (E // 2 + 1))
                    pool.sem_inc(pool_waited, 1)
                    pool.indirect_dma_start(
                        out=acc[0], out_offset=bass.IndirectOffsetOnAxis(ap=ov_idx[:, 1:2], axis=0),
                        in_=y[:, 0, :], in_offset=None, compute_op=ALU.add).then_inc(acc_done[0], 16)
            pool.wait_ge(acc_in, 32)
            nc.gpsimd.tensor_tensor(acc_sb[1], acc_sb[1], acc_sb[0], ALU.add).then_inc(pool_step, 1)
            pool.wait_ge(pool_step, 1)
            pool.wait_ge(x_again_in, 16)
            nc.gpsimd.tensor_tensor(acc_sb[1], acc_sb[1], x_again, ALU.add).then_inc(xab_ready, 1)

        @block.scalar
        def _(act_e):
            act_e.wait_ge(var_ready, 1)
            nc.scalar.activation(rs[:, 1, :], rs[:, 0, :], ACT.Sqrt).then_inc(std_ready, 1)
            for n in range(2):
                act_e.wait_ge(xnT_ps, n + 1)
                nc.scalar.copy(xnT[:, 0, n * 512:(n + 1) * 512], ps[n][:]).then_inc(xnT_a, 1)
            act_e.wait_ge(shifted_ready, 1)
            nc.scalar.activation(ex[:], ex[:], ACT.Exp).then_inc(ex_ready, 1)
            act_e.wait_ge(bias_in, 32)
            for n in range(4):
                act_e.wait_ge(q_ps, n + 1)
                nc.scalar.activation(qT[:, n // 2, (n % 2) * 512:(n % 2 + 1) * 512], ps[n % 2][:], ACT.Identity,
                                     bias=bq_sb[:, n // 2:n // 2 + 1]).then_inc(q_sb, 1)
            for c in range(NC):
                act_e.wait_ge(kv_ps, c + 1)
                nc.scalar.copy(kv[:, c, :], ps[c % 4][:]).then_inc(kv_sb, 1)

            def evac_xT(t, k):
                act_e.wait_ge(xT_ps, t + 1)
                if not (isinstance(t, int) and t < 2):
                    act_e.wait_ge(gu_ps, t - 1)
                nc.scalar.copy(xT[:, k % 2, :], ps[k % 2][:, 0:H]).then_inc(xT_sb, 1)

            def silu(t, k):
                act_e.wait_ge(gu_ps, t + 1)
                nc.scalar.activation(sg[:, k % 2, :], ps[2 + k % 2][:, 0:F], ACT.Silu).then_inc(sg_sb, 1)

            def evac_y(t, k, first):
                act_e.wait_ge(y_ps, t + 1)
                if not first:
                    act_e.wait_ge(acc_done[k % 2], (t - k) * 8 + 16 * (k // 2))
                nc.scalar.copy(y[:, k % 4, :], ps[6 + k % 2][:, 0:H]).then_inc(y_sb, 1)

            evac_xT(0, 0)
            silu(0, 0)
            evac_xT(1, 1)

            def expert_act(t, k, first=False, ahead=2):
                if ahead >= 2:
                    evac_xT(t + 2, k)
                if ahead >= 1:
                    silu(t + 1, k + 1)
                evac_y(t, k, first)

            for k in range(4):
                expert_act(k, k, first=True)
            with act_e.Fori(0, E // RING - 1) as i:
                for k in range(4, RING + 4):
                    expert_act(i * RING + k, k)
            for k in range(4, RING):
                expert_act(E - RING + k, k, ahead=min(2, RING - 1 - k))

            act_e.wait_ge(ov_ready, 1)
            n_ov = act_e.value_load(ov_n[0:1, 0:1], min_val=0, max_val=E - 1)
            with act_e.If(n_ov > 0):
                with act_e.Fori(0, n_ov) as j:
                    act_e.wait_ge(xT_ps, j + (E + 1))
                    nc.scalar.copy(xT[:, 0, :], ps[0][:, 0:H]).then_inc(xT_sb, 1)
                    act_e.wait_ge(gu_ps, j + (E + 1))
                    nc.scalar.activation(sg[:, 0, :], ps[2][:, 0:F], ACT.Silu).then_inc(sg_sb, 1)
                    act_e.wait_ge(y_ps, j + (E + 1))
                    act_e.wait_ge(acc_done[0], j * 16 + 16 * (E // 2 + 1))
                    nc.scalar.copy(y[:, 0, :], ps[6][:, 0:H]).then_inc(y_sb, 1)

            for n in range(6):
                act_e.wait_ge(sgu_ps, n + 1)
                if n >= 2:
                    act_e.wait_ge(sact_sb, n - 1)
                rows_n = P if n % 3 < 2 else FS - 2 * P
                nc.scalar.activation(stmp[0:rows_n, n % 2, :], ps[(n % 2) * 2][0:rows_n, :], ACT.Silu)\
                    .then_inc(stmp_sb, 1)
            for n in range(2):
                act_e.wait_ge(kT_ps, n + 1)
                nc.scalar.copy(kT[:, 0, n * 512:(n + 1) * 512], ps[4 + n][:]).then_inc(kT_a, 1)

        @block.vector
        def _(dve):
            step = [0]

            def link(ins):
                step[0] += 1
                ins.then_inc(dve_step, 1)
                dve.wait_ge(dve_step, step[0])

            V = nc.vector
            for c in range(NC):
                if c % 2 == 0:
                    dve.wait_ge(x_in[c // 2], 16)
                ins = V.bn_stats(stats[:, c, :], x_sb[:, c, :])
            link(ins)
            for c in range(NC):
                ins = V.bn_aggr(mv[:, c, :], stats[:, c, :])
            link(ins)
            V.tensor_scalar(rs[:, 0, :], mv[:, :, 1], 1e-5, None, ALU.add).then_inc(var_ready, 1)
            dve.wait_ge(std_ready, 1)
            link(V.reciprocal(rs[:, 2, :], rs[:, 1, :]))
            link(V.tensor_tensor(rs[:, 3, :], rs[:, 2, :], rs[:, 2, :], ALU.mult))
            link(V.scalar_tensor_tensor(rs[:, 3, :], rs[:, 3, :], -0.5, rs[:, 0, :], ALU.mult, ALU.mult))
            link(V.scalar_tensor_tensor(rs[:, 2, :], rs[:, 3, :], 1.5, rs[:, 2, :], ALU.add, ALU.mult))
            for c in range(NC):
                V.tensor_scalar(tab[:, c, 0:H], x_sb[:, c, :], mv[:, c, 0:1], rs[:, 2, c:c + 1],
                                ALU.subtract, ALU.mult).then_inc(xn_ready, 1)
            V.memset(lg[:, :, E:E + 2], BIG)
            V.memset(ov_ones[:], 1.0)
            V.memset(ov_j[:], 0.0)
            for n in range(2):
                dve.wait_ge(xnT_ps, n + 1)
                V.tensor_copy(xnT[:, 1, n * 512:(n + 1) * 512], ps[2 + n][:]).then_inc(xnT_v, 1)

            dve.wait_ge(logits_ps, 1)
            link(V.tensor_copy(lg[:, :, 0:E], ps[4][:].rearrange("p (c e) -> p c e", e=E)))
            for c in range(NC):
                ins = V.max(top8[:, c, :], lg[:, c, 0:E])
            link(ins)
            V.tensor_tensor(ex[:], lg[:, :, 0:E], top8[:, :, 0:1].to_broadcast([P, NC, E]), ALU.subtract)\
                .then_inc(shifted_ready, 1)
            link(V.memset(top8[:, :, TOPK:8], BIG))
            for c in range(NC):
                ins = V.match_replace(lgm[:, c, :], top8[:, c, :], lg[:, c, :], -BIG)
            link(ins)
            V.tensor_tensor(chosen[:], lg[:, :, 0:E], lgm[:, :, 0:E], ALU.not_equal).then_inc(chosen_ready, 1)
            dve.wait_ge(chosen_ready, 1)
            dve.wait_ge(ex_ready, 1)
            V.tensor_reduce(sm[:, 0, :], ex[:], AX, ALU.add)
            link(V.tensor_tensor(exm[:], ex[:], chosen[:], ALU.mult))
            V.tensor_reduce(sm[:, 1, :], exm[:], AX, ALU.add)
            link(V.reciprocal(sm[:, 2, :], sm[:, 0, :]))
            link(V.tensor_tensor(sm[:, 1, :], sm[:, 1, :], sm[:, 2, :], ALU.mult))
            link(V.tensor_scalar(sm[:, 1, :], sm[:, 1, :], 1e-20, None, ALU.add))
            link(V.reciprocal(sm[:, 3, :], sm[:, 1, :]))
            link(V.tensor_tensor(sm[:, 3, :], sm[:, 3, :], sm[:, 2, :], ALU.mult))
            V.tensor_tensor(tab[:, :, H:ROW], exm[:], bc(sm[:, 3, :], [P, NC, E]), ALU.mult).then_inc(comb_ready, 1)

            dve.wait_ge(rank_ps, 1)
            link(V.scalar_tensor_tensor(rank_i[:], chosen[:].rearrange("p c e -> p (c e)"), -UNCHOSEN, ps[5][:],
                                        ALU.mult, ALU.add))
            V.tensor_scalar(lo_i[:], rank_i[:], 15, None, ALU.bitwise_and)
            link(V.tensor_scalar(hi_i[:], rank_i[:], 4, None, ALU.arith_shift_right))
            V.tensor_copy(lo_h[:], lo_i[:])
            link(V.tensor_copy(hi_h[:], hi_i[:]))
            dve.wait_ge(c16_in, 16)
            dve.wait_ge(acc_done[0], 16)
            dve.wait_ge(acc_done[1], 16)
            for a in range(16):
                V.tensor_scalar(lo_hot[:, :, a, :], lo_h.rearrange("p (n e) -> p n e", e=8), float(a), None,
                                ALU.is_equal)
            for b in range(8):
                ins = V.scalar_tensor_tensor(hi_hot[:, b, :, :].rearrange("p c e -> p (c e)"), hi_h[:],
                                             float(b) - UNCHOSEN / 16, c_16("tok"), ALU.is_equal, ALU.mult)
            ins.then_inc(hot_ready, 1)
            V.tensor_copy(rank_f[:], rank_i[:])
            link(V.tensor_scalar(ov[:, 0, :], ps[6][:, 0:E], float(P), None, ALU.is_gt))
            for j in range(2, T // P):
                link(V.scalar_tensor_tensor(ov[:, 0, :], ps[6][:, 0:E], float(P * j), ov[:, 0, :],
                                            ALU.is_gt, ALU.add))
            link(V.tensor_tensor_scan(ov[:, 1, :], ov_ones[:], ov[:, 0, :], 0.0, ALU.mult, ALU.add))
            V.tensor_copy(ov_n[:], ov[0:1, 1, E - 1:E]).then_inc(ov_ready, 1)
            link(V.tensor_tensor(ov[:, 2, :], ov[:, 1, :], ov[:, 0, :], ALU.subtract))
            dve.wait_ge(c32_in, 16)
            dve.wait_ge(diag_ps, 1)
            V.tensor_tensor(diag[:].rearrange("p g b e -> p (g b) e"), ps[7][:].rearrange("p (gb e) -> p gb e", e=8),
                            c_32("mask8").unsqueeze(1).to_broadcast([P, 64, 8]), ALU.mult).then_inc(diag_ready, 1)
            dve.wait_ge(slot_ps, 1)

            def indices(lst, tmp, g_out, s_out):
                V.tensor_scalar(tmp[0], lst, 0.0, float(SKIP + 1), ALU.is_equal, ALU.mult)
                link(V.tensor_scalar(tmp[1], lst, 0.0, c_32("padrow"), ALU.is_equal, ALU.mult))
                V.scalar_tensor_tensor(g_out, lst, -1.0, tmp[0], ALU.add, ALU.add)
                return V.scalar_tensor_tensor(s_out, lst, -1.0, tmp[1], ALU.add, ALU.add)

            link(indices(ps[4][:, 0:E], (slot_t[:, 0, :], slot_t[:, 1, :]), gidx[:], sidx[:]))
            V.tensor_copy(gcol[:], gidx[:, 0:4]).then_inc(gcol_ready, 1)

            def gate_up(t, k, comb):
                dve.wait_ge(sg_sb, t + 1)
                if not (isinstance(t, int) and t < 2):
                    dve.wait_ge(aT_ps, t - 1)
                V.scalar_tensor_tensor(act[:, k % 2, 0:F], ps[2 + k % 2][:, F:2 * F], comb, sg[:, k % 2, :],
                                       ALU.mult, ALU.mult).then_inc(act_sb, 1)

            dve.wait_ge(act_zero, 1)
            gate_up(0, 0, rows[:, 0, H:H + 1])

            def expert_dve(t, k, first=False, last=False):
                if not first:
                    dve.wait_ge(acc_done[k % 2], (t - k) * 8 + 16 * (k // 2))
                V.tensor_copy(scol[:, k % 4:k % 4 + 1], sidx[:, bass.ds(t, 1)]).then_inc(scol_ready, 1)
                if not (last and k >= RING - 4):
                    V.tensor_copy(gcol[:, k % 4:k % 4 + 1], gidx[:, bass.ds(t + 4, 1)]).then_inc(gcol_ready, 1)
                dve.wait_ge(aT_ps, t + 1)
                if not (isinstance(t, int) and t < 2):
                    dve.wait_ge(y_ps, t - 1)
                V.tensor_copy(aT[:, k % 2, :], ps[4 + k % 2][:, 0:2 * P]).then_inc(aT_sb, 1)
                if not (last and k == RING - 1):
                    gate_up(t + 1, k + 1, rows[:, (k + 1) % 4, bass.ds(t + (H + 1), 1)])

            for k in range(4):
                expert_dve(k, k, first=True)
            with dve.Fori(0, E // RING - 1) as i:
                for k in range(4, RING + 4):
                    expert_dve(i * RING + k, k)
            for k in range(4, RING):
                expert_dve(E - RING + k, k, last=True)

            n_ov = dve.value_load(ov_n[0:1, 0:1], min_val=0, max_val=E - 1)
            ov_steps = sem("ov_steps")
            per_tile = [0]

            def ov_body(j):
                count = [0]

                def olink(ins):
                    count[0] += 1
                    ins.then_inc(ov_steps, 1)
                    dve.wait_ge(ov_steps, j * OV_LINKS + count[0])

                olink(V.tensor_scalar(ov[:, 3, :], ov[:, 1, :], ov_j[:], None, ALU.is_gt))
                olink(V.scalar_tensor_tensor(ov[:, 3, :], ov[:, 2, :], ov_j[:], ov[:, 3, :], ALU.is_le, ALU.mult))
                olink(V.tensor_tensor(ov[:, 4, :], ov[:, 3, :], c_32("iota_e"), ALU.mult))
                olink(V.tensor_reduce(ov_s[:, 0:1], ov[:, 4, :], AX, ALU.add))
                V.tensor_copy(ov_e[:], ov_s[0:1, 0:1]).then_inc(ov_expert_ready, 1)
                olink(V.tensor_tensor(ov[:, 4, :], ov[:, 3, :], ov[:, 2, :], ALU.mult))
                olink(V.tensor_reduce(ov_s[:, 1:2], ov[:, 4, :], AX, ALU.add))
                olink(V.tensor_tensor(ov_s[:, 2:3], ov_j[:], ov_s[:, 1:2], ALU.subtract))
                olink(V.tensor_scalar(ov_s[:, 3:4], ov_s[:, 2:3], float(P), float(P) - UNCHOSEN, ALU.mult, ALU.add))
                olink(V.tensor_tensor(ov_sel[:], rank_f[:].rearrange("p (c e) -> p c e", e=E),
                                      ov[:, 3, :].unsqueeze(1).to_broadcast([P, NC, E]), ALU.mult))
                olink(V.tensor_reduce(ov_rank[:], ov_sel[:], AX, ALU.add))
                olink(V.tensor_scalar(ov_adj[:], ov_rank[:], ov_s[:, 3:4], None, ALU.subtract))
                for c in range(NC):
                    ins = V.tensor_scalar(ov_hot[:, c, :], c_32("iota_s"), ov_adj[:, c:c + 1], None, ALU.is_equal)
                ins.then_inc(ov_hot_ready, 1)
                dve.wait_ge(ov_list_ps, j + 1)
                count[0] += 1
                V.tensor_scalar(ov_t[:, 0:1], ps[7][:, 0:1], 0.0, float(SKIP + 1), ALU.is_equal, ALU.mult)
                V.tensor_scalar(ov_t[:, 1:2], ps[7][:, 0:1], 0.0, c_32("padrow"), ALU.is_equal, ALU.mult)\
                    .then_inc(ov_steps, 1)
                dve.wait_ge(ov_steps, j * OV_LINKS + count[0])
                dve.wait_ge(acc_done[0], j * 16 + 16 * (E // 2 + 1))
                V.scalar_tensor_tensor(ov_idx[:, 0:1], ps[7][:, 0:1], -1.0, ov_t[:, 0:1], ALU.add, ALU.add)
                V.scalar_tensor_tensor(ov_idx[:, 1:2], ps[7][:, 0:1], -1.0, ov_t[:, 1:2], ALU.add, ALU.add)\
                    .then_inc(ov_idx_ready, 1)
                dve.wait_ge(ov_rows_in, j * 16 + 16)
                olink(V.tensor_tensor(ov_comb[:], rows[:, 0, H:ROW], ov[:, 3, :], ALU.mult))
                olink(V.tensor_reduce(ov_s[:, 4:5], ov_comb[:], AX, ALU.add))
                dve.wait_ge(sg_sb, j + (E + 1))
                V.scalar_tensor_tensor(act[:, 0, 0:F], ps[2][:, F:2 * F], ov_s[:, 4:5], sg[:, 0, :],
                                       ALU.mult, ALU.mult).then_inc(act_sb, 1)
                olink(V.tensor_scalar(ov_j[:], ov_j[:], 1.0, None, ALU.add))
                dve.wait_ge(aT_ps, j + (E + 1))
                V.tensor_copy(aT[:, 0, :], ps[4][:, 0:2 * P]).then_inc(aT_sb, 1)
                assert count[0] == OV_LINKS, count

            OV_LINKS = 15
            with dve.If(n_ov > 0):
                with dve.Fori(0, n_ov) as j:
                    ov_body(j)

            def bias_kv(c):
                V.tensor_tensor(kv[:, c, :], kv[:, c, :], bkv_sb[:], ALU.add).then_inc(kvb_ready, 1)

            def split_heads(g, h):
                V.tensor_scalar(qbd[:, g, h::HG, :], qT[:, g, :].rearrange("p (c i) -> p c i", i=P),
                                c_32("hmask")[:, h:h + 1], None, ALU.mult).then_inc(qbd_ready, 1)

            dve.wait_ge(kv_sb, NC)
            dve.wait_ge(q_sb, 4)
            dve.wait_ge(y_ps, n_ov + E)
            extra = [lambda c=c: bias_kv(c) for c in range(NC)]
            heads = [lambda g=g, h=h: split_heads(g, h) for g in range(NG) for h in range(HG)]
            for f in extra[0:4]:
                f()
            for n in range(6):
                rows_n = P if n % 3 < 2 else FS - 2 * P
                dve.wait_ge(stmp_sb, n + 1)
                V.tensor_tensor(sact[0:rows_n, n % 3, (n // 3) * 512:(n // 3 + 1) * 512],
                                ps[(n % 2) * 2 + 1][0:rows_n, :], stmp[0:rows_n, n % 2, :], ALU.mult)\
                    .then_inc(sact_sb, 1)
                if n < 2:
                    for f in extra[4 + 2 * n:6 + 2 * n]:
                        f()
                    if n == 1:
                        dve.wait_ge(kvb_ready, NC)
                        for c in range(NC):
                            V.tensor_tensor(ks[:, c, :], kv[:, c, 0:H], c_32("kscale"), ALU.mult).then_inc(ks_ready, 1)
                elif n < 4:
                    for f in heads[4 * (n - 2):4 * (n - 1)]:
                        f()
                elif n == 4:
                    for g in range(NG):
                        V.tensor_tensor(qsT[:, g, :].rearrange("p (c i) -> p c i", i=P),
                                        qT[:, g, :].rearrange("p (c i) -> p c i", i=P),
                                        c_32("qscale")[:, g * P:(g + 1) * P].unsqueeze(1).to_broadcast([P, NC, P]),
                                        ALU.mult).then_inc(qs_ready, 1)
            for n in range(2):
                dve.wait_ge(kT_ps, n + 1)
                V.tensor_copy(kT[:, 1, n * 512:(n + 1) * 512], ps[6 + n][:]).then_inc(kT_v, 1)

            n_state = 0
            for u in range(2 * NC):
                c, g = u // 2, u % 2
                dve.wait_ge(s_ps, u + 1)
                if u >= 2:
                    dve.wait_ge(o_ps, u - 1)
                V.tensor_tensor(pT[:, u % 2, :], ps[u % 2][:],
                                c_32("decay")[:, g * HG * P:(g + 1) * HG * P], ALU.mult).then_inc(p_sb, 1)
                if u >= 2 and u % 2 == 0:
                    finish = c - 1
                    if finish == 0:
                        dve.wait_ge(xab_ready, 1)
                    dve.wait_ge(o_ps, 2 * (finish + 1))
                    if finish >= 2:
                        dve.wait_ge(out_done[finish % 2], 16 * (finish // 2))
                    V.tensor_tensor(res[:, finish % 2, :], ps[4 + finish % 2][:, 0:H], acc_sb[1][:, finish, :],
                                    ALU.add).then_inc(res_sb, 1)
                if c % SEQ_CHUNKS < SEQ_CHUNKS - 1:
                    m = c % SEQ_CHUNKS
                    n_state += 1
                    dve.wait_ge(st_ps, n_state)
                    if m == 0:
                        V.tensor_tensor(state[:, 0, g, :], ps[6 + n_state % 2][:, 0:P], c_32("bdmask"), ALU.mult)\
                            .then_inc(st_sb, 1)
                    else:
                        dve.wait_ge(st_sb, n_state - 1)
                        link(V.tensor_tensor(st_t[:], ps[6 + n_state % 2][:, 0:P], c_32("bdmask"), ALU.mult))
                        V.scalar_tensor_tensor(state[:, m % 2, g, :], state[:, (m - 1) % 2, g, :],
                                               c_32("gc")[:, g:g + 1], st_t[:], ALU.mult, ALU.add).then_inc(st_sb, 1)
            dve.wait_ge(o_ps, 2 * NC)
            dve.wait_ge(out_done[(NC - 1) % 2], 16 * ((NC - 1) // 2))
            V.tensor_tensor(res[:, (NC - 1) % 2, :], ps[4 + (NC - 1) % 2][:, 0:H], acc_sb[1][:, NC - 1, :],
                            ALU.add).then_inc(res_sb, 1)

        @block.tensor
        def _(pe):
            mm = nc.tensor.matmul
            pe.wait_ge(ident_in, 16)
            for c in range(NC):
                pe.wait_ge(xn_ready, c + 1)
                for k in range(NG):
                    ins = nc.tensor.transpose(ps[2 * k + c // 4][:, (c % 4) * P:(c % 4 + 1) * P],
                                              tab[:, c, k * P:(k + 1) * P], ident)
                if c % 4 == 3:
                    ins.then_inc(xnT_ps, 1)
            pe.wait_ge(gate_in, 16)
            for c in range(NC):
                pe.wait_ge(xnT_a, c // 4 + 1)
                pe.wait_ge(xnT_v, c // 4 + 1)
                for k in range(NG):
                    ins = mm(ps[4][:, c * E:(c + 1) * E], xnT[:, k, c * P:(c + 1) * P], gate_sb[:, k, :],
                             start=(k == 0), stop=(k == NG - 1))
            ins.then_inc(logits_ps, 1)
            pe.wait_ge(wq_in, 16)
            for m in range(4):
                g, n = m // 2, m % 2
                if m >= 2:
                    pe.wait_ge(q_sb, m - 1)
                for k in range(NG):
                    ins = mm(ps[m % 2][:], wq_sb[:, k, g * P:(g + 1) * P], xnT[:, k, n * 512:(n + 1) * 512],
                             start=(k == 0), stop=(k == NG - 1))
                ins.then_inc(q_ps, 1)
            pe.wait_ge(c16_in, 16)
            pe.wait_ge(chosen_ready, 1)
            mm(ps[5][:], c_16("tri"), chosen[:].rearrange("p c e -> p (c e)"), start=True, stop=False)
            for c in range(NC - 1):
                mm(ps[5][:, (c + 1) * E:].rearrange("p (c e) -> p c e", e=E), c_16("ones"),
                   chosen[:, c:c + 1, :].to_broadcast([P, NC - 1 - c, E]), start=False, stop=(c == NC - 2))
            for c in range(NC):
                ins = mm(ps[6][:, 0:E], c_16("ones"), chosen[:, c, :], start=(c == 0), stop=(c == NC - 1))
            ins.then_inc(rank_ps, 1)
            pe.wait_ge(wkv_in, 16)
            pe.wait_ge(q_sb, 4)
            for c in range(NC):
                if c >= 4:
                    pe.wait_ge(kv_sb, c - 3)
                for k in range(NG):
                    ins = mm(ps[c % 4][:], xnT[:, k, c * P:(c + 1) * P], wkv_sb[:, k, :],
                             start=(k == 0), stop=(k == NG - 1))
                ins.then_inc(kv_ps, 1)
            pe.wait_ge(hot_ready, 1)
            for g in range(8):
                for c in range(NC):
                    ins = mm(ps[7][:, g * 64:(g + 1) * 64], lo_hot[:, c * 8 + g, :, :].rearrange("p a e -> p (a e)"),
                             hi_hot[:, :, c, 8 * g:8 * g + 8], start=(c == 0), stop=(c == NC - 1))
            ins.then_inc(diag_ps, 1)
            pe.wait_ge(diag_ready, 1)
            for b in range(8):
                lo = C16["place"][0] + 112 - 16 * b
                ins = mm(ps[4][:, 0:E], k16[:, lo:lo + P], diag[:, :, b, :], start=(b == 0), stop=(b == 7))
            ins.then_inc(slot_ps, 1)

            def trans_x(t, k, rows_sem, rows_val, r):
                pe.wait_ge(rows_sem, rows_val)
                if not (isinstance(t, int) and t < 2):
                    pe.wait_ge(xT_sb, t - 1)
                for h in range(NG):
                    ins = nc.tensor.transpose(ps[k % 2][:, h * P:(h + 1) * P], rows[:, r, h * P:(h + 1) * P], ident)
                ins.then_inc(xT_ps, 1)

            def gate_up(t, k, slot, w_sem, w_val):
                pe.wait_ge(w_sem, w_val)
                if not (isinstance(t, int) and t < 2):
                    pe.wait_ge(act_sb, t - 1)
                pe.wait_ge(xT_sb, t + 1)
                for h in range(NG):
                    ins = mm(ps[2 + k % 2][:, 0:2 * F], xT[:, k % 2, h * P:(h + 1) * P],
                             w1_sb[:, slot, h * 2 * F:(h + 1) * 2 * F], start=(h == 0), stop=(h == NG - 1))
                ins.then_inc(gu_ps, 1)

            def trans_act(t, k):
                pe.wait_ge(act_sb, t + 1)
                if not (isinstance(t, int) and t < 2):
                    pe.wait_ge(aT_sb, t - 1)
                for h in range(2):
                    ins = nc.tensor.transpose(ps[4 + k % 2][:, h * P:(h + 1) * P],
                                              act[:, k % 2, h * P:(h + 1) * P], ident)
                ins.then_inc(aT_ps, 1)

            def down(t, k, slot):
                if not (isinstance(t, int) and t < 2):
                    pe.wait_ge(y_sb, t - 1)
                pe.wait_ge(aT_sb, t + 1)
                mm(ps[6 + k % 2][:, 0:H], aT[:, k % 2, 0:P], w1_sb[:, slot, 4 * F:W1C], start=True, stop=False)
                mm(ps[6 + k % 2][:, 0:H], aT[0:F2, k % 2, P:2 * P], w2_sb[0:F2, slot, :],
                   start=False, stop=True).then_inc(y_ps, 1)

            pe.wait_ge(kv_sb, NC)
            pe.wait_ge(gcol_ready, 1)
            trans_x(0, 0, rows_in[0], 16, 0)
            gate_up(0, 0, 0, w_in[0], 32)
            trans_x(1, 1, rows_in[1], 16, 1)

            def expert_pe(i, k, ahead=2):
                t = i * RING + k
                trans_act(t, k)
                if ahead >= 2:
                    k2 = k + 2
                    trans_x(t + 2, k2, rows_in[k2 % 4], i * (16 * (RING // 4)) + 16 * (k2 // 4 + 1), k2 % 4)
                if ahead >= 1:
                    k1 = k + 1
                    gate_up(t + 1, k1, k1 % RING, w_in[k1 % RING], i * 32 + 32 * (k1 // RING + 1))
                down(t, k, k % RING)

            for k in range(4):
                expert_pe(0, k)
            with pe.Fori(0, E // RING - 1) as i:
                for k in range(4, RING + 4):
                    expert_pe(i, k)
            for k in range(4, RING):
                expert_pe(E // RING - 1, k, ahead=min(2, RING - 1 - k))

            pe.wait_ge(ov_ready, 1)
            n_ov = pe.value_load(ov_n[0:1, 0:1], min_val=0, max_val=E - 1)
            with pe.If(n_ov > 0):
                with pe.Fori(0, n_ov) as j:
                    t = j + E
                    pe.wait_ge(y_sb, t)
                    pe.wait_ge(ov_hot_ready, j + 1)
                    for c in range(NC):
                        ins = mm(ps[7][:, 0:1], ov_hot[:, c, :], k16[:, C16["tokc"][0] + c:C16["tokc"][0] + c + 1],
                                 start=(c == 0), stop=(c == NC - 1))
                    ins.then_inc(ov_list_ps, 1)
                    trans_x(t, 0, ov_rows_in, j * 16 + 16, 0)
                    gate_up(t, 0, 0, ov_w_in, j * 32 + 32)
                    trans_act(t, 0)
                    down(t, 0, 0)

            pe.wait_ge(shared_in, 48)
            for m in range(6):
                n, f = m // 3, m % 3
                fw = P if f < 2 else FS - 2 * P
                if m >= 2:
                    pe.wait_ge(sact_sb, m - 1)
                else:
                    pe.wait_ge(y_sb, E)
                for o in range(2):
                    for k in range(NG):
                        ins = mm(ps[(m % 2) * 2 + o][0:fw, :], sgu_sb[:, k, o * FS + f * P:o * FS + f * P + fw],
                                 xnT[:, k, n * 512:(n + 1) * 512], start=(k == 0), stop=(k == NG - 1))
                ins.then_inc(sgu_ps, 1)
            pe.wait_ge(kvb_ready, NC)
            pe.wait_ge(y_sb, n_ov + E)
            for c in range(NC):
                for g in range(NG):
                    ins = nc.tensor.transpose(ps[4 + 2 * g + c // 4][:, (c % 4) * P:(c % 4 + 1) * P],
                                              kv[:, c, g * P:(g + 1) * P], ident)
                if c % 4 == 3:
                    ins.then_inc(kT_ps, 1)

            def scores(u):
                c, g = u // 2, u % 2
                if u >= 2:
                    pe.wait_ge(p_sb, u - 1)
                else:
                    pe.wait_ge(sact_sb, 6)
                mm(ps[u % 2][:], kT[:, g, c * P:(c + 1) * P], qbd[:, g, c * HG:(c + 1) * HG, :].rearrange("p h i -> p (h i)"),
                   start=True, stop=True).then_inc(s_ps, 1)

            pe.wait_ge(kT_a, 2)
            pe.wait_ge(kT_v, 2)
            pe.wait_ge(qbd_ready, NG * HG)
            pe.wait_ge(qs_ready, NG)
            pe.wait_ge(ks_ready, NC)
            scores(0)
            n_state = 0
            for u in range(2 * NC):
                c, g, m = u // 2, u % 2, (u // 2) % SEQ_CHUNKS
                bank = ps[4 + c % 2]
                if u + 1 < 2 * NC:
                    scores(u + 1)
                if m < SEQ_CHUNKS - 1:
                    n_state += 1
                    if n_state >= 3:
                        pe.wait_ge(st_sb, n_state - 2)
                    mm(ps[6 + n_state % 2][:, 0:P], ks[:, c, g * P:(g + 1) * P], kv[:, c, H + g * P:H + (g + 1) * P],
                       start=True, stop=True).then_inc(st_ps, 1)
                if g == 0:
                    if c >= 2:
                        pe.wait_ge(res_sb, c - 1)
                    for f in range(3):
                        fw = P if f < 2 else FS - 2 * P
                        mm(bank[:, 0:H], sact[0:fw, f, c * P:(c + 1) * P], sdn_sb[0:fw, f, :],
                           start=(f == 0), stop=False)
                if m > 0:
                    pe.wait_ge(st_sb, (c // SEQ_CHUNKS) * 2 * (SEQ_CHUNKS - 1) + 2 * (m - 1) + g + 1)
                    mm(bank[:, g * P:(g + 1) * P], qsT[:, g, c * P:(c + 1) * P], state[:, (m - 1) % 2, g, :],
                       start=False, stop=False)
                pe.wait_ge(p_sb, u + 1)
                for h in range(HG):
                    at = g * P + h * D
                    ins = mm(bank[:, at:at + D], pT[:, u % 2, h * P:(h + 1) * P], kv[:, c, H + at:H + at + D],
                             start=False, stop=(h == HG - 1 and g == 1))
                ins.then_inc(o_ps, 1)


def _constants():
    import numpy as np
    p = np.arange(P)
    betas = np.linspace(np.log2(1.0 / 32.0), np.log2(1.0 / 512.0), HEADS).astype(np.float32)
    g = (np.float32(1.0) - np.exp2(betas).astype(np.float32)).astype(np.float64)
    a = {}
    a["ident"] = np.eye(P)
    a["mask8"] = (p[:, None] % 8 == np.arange(8)[None, :])
    a["padrow"] = (T + 1 + p)[:, None]
    a["iota_e"] = np.tile(np.arange(E), (P, 1))
    a["iota_s"] = np.tile(np.arange(P), (P, 1))
    a["hmask"] = (p[:, None] // D == np.arange(HG)[None, :])
    head = np.arange(NG)[None, :] * HG + p[:, None] // D
    a["gc"] = g[head] ** P
    a["bdmask"] = (p[:, None] // D == p[None, :] // D)
    a["kscale"] = g[np.arange(H)[None, :] // D] ** (P - 1 - p)[:, None]
    a["qscale"] = (g[head][:, :, None] ** (p + 1)[None, None, :]).reshape(P, NG * P)
    diff = p[None, None, :] - p[:, None, None]
    a["decay"] = np.where(diff >= 0, g[None, :, None] ** np.maximum(diff, 0), 0.0).reshape(P, HEADS * P)
    c32 = np.concatenate([np.asarray(a[n], np.float32) for n in C32], 1)
    b = {}
    b["tri"] = (p[:, None] < p[None, :])
    b["ones"] = np.ones((P, P))
    b["place"] = (np.arange(240)[None, :] - 112 == p[:, None] // 8)
    tok = np.arange(NC)[None, :] * P + p[:, None] + 1
    b["tok"] = np.repeat(tok, E, axis=1)
    b["tokc"] = tok
    c16 = np.concatenate([np.asarray(b[n], np.float16) for n in C16], 1)
    return c32, c16


def kernel(**inputs):
    import numpy as np
    import concourse.bacc as bacc
    from concourse.bass_utils import run_bass_kernel_spmd

    v = {n.replace("L0_attn_", "").replace("L0_ffn_", ""): np.asarray(a) for n, a in inputs.items()}

    def halves(w):
        return np.ascontiguousarray(w.reshape(NG, P, -1).transpose(1, 0, 2))

    c32, c16 = _constants()
    gu = v["w_gate_up"].transpose(0, 2, 1).reshape(E, NG, P, 2 * F).transpose(0, 2, 1, 3).reshape(E, P, NG * 2 * F)
    dn = v["w_down"].transpose(0, 2, 1)
    arrays = {
        "x": v["x"].reshape(T, H),
        "wq": halves(v["Wq"]),
        "wkv": halves(np.concatenate([v["Wk"], v["Wv"]], 1)),
        "bq": np.ascontiguousarray(v["bq"].reshape(NG, P).T),
        "bkv": np.concatenate([v["bk"], v["bv"]]),
        "gate": halves(v["gate_w"].T),
        "sgu": halves(v["ws_gate_up"].T),
        "sdn": np.ascontiguousarray(v["ws_down"].T),
        "w1": np.ascontiguousarray(np.concatenate([gu, dn[:, 0:F1, :]], 2)),
        "w2": np.ascontiguousarray(dn[:, F1:F, :]),
        "c32": c32,
        "c16": c16,
    }
    nc = bacc.Bacc("TRN2", target_bir_lowering=False, num_devices=1)
    args = [nc.dram_tensor(f"in_{n}", a.shape, mybir.dt.from_np(a.dtype), kind="ExternalInput").ap()
            for n, a in arrays.items()]
    out = nc.dram_tensor("out", (T, H), mybir.dt.float32, kind="ExternalOutput").ap()
    build(nc, *args, out)
    r = run_bass_kernel_spmd(nc, [{f"in_{n}": a for n, a in arrays.items()}], core_ids=[0])
    return r.results[0]["out"].reshape(2, T // 2, H)
```

```python
from contextlib import ExitStack

import concourse.bass as bass
from concourse import mybir

P = 128
T, H = 1024, 256
NC = T // P
E, TOPK, F = 64, 6, 176
FS = 352
HEADS, D = 8, 32
HG = P // D
NG = H // P
SEQ_CHUNKS = 4
ROW = H + E
EXTRA = 2
TILES = E + EXTRA
RING = 16
F1 = P
F2 = F - F1
W1C = 2 * 2 * F + H
ACC_ROWS = T + P
BIG = 3.0e38
UNCHOSEN = 4096.0
SKIP = 4096

C32 = {}
_at = 0
for _n, _w in (("ident", P), ("mask8", 8), ("padrow", 1), ("iota_e", E), ("iota_s", P), ("hmask", HG),
               ("gc", NG), ("bdmask", P), ("kscale", H), ("qscale", NG * P), ("decay", HEADS * P)):
    C32[_n] = (_at, _at + _w)
    _at += _w
C32W = _at
C32_LATE = C32["hmask"][0]
LATE = 4
AHEAD = 8
LOOP_PACE = 2
PACE = 3
C16 = {}
_at = 0
for _n, _w in (("tri", P), ("ones", P), ("place", 240), ("tok", NC * E), ("tokc", NC)):
    C16[_n] = (_at, _at + _w)
    _at += _w
C16W = _at


def build(nc, x, wq, wkv, bq, bkv, gate, sgu, sdn, w1, w2, c32, c16, out):
    f32, f16, i32 = mybir.dt.float32, mybir.dt.float16, mybir.dt.int32
    ALU = mybir.AluOpType
    ACT = mybir.ActivationFunctionType
    AX = mybir.AxisListType.X

    table = nc.dram_tensor("table", [T, ROW], f32, kind="Internal").ap()
    acc = [nc.dram_tensor(f"acc{k}", [ACC_ROWS, H], f32, kind="Internal").ap() for k in range(2)]

    with ExitStack() as ctx:
        def sb(name, shape, dt=f32):
            return ctx.enter_context(nc.sbuf_tensor(name, shape, dt))

        def sem(name):
            return ctx.enter_context(nc.semaphore(name))

        k32 = sb("k32", [P, C32W])
        k16 = sb("k16", [P, C16W], f16)

        def c_32(n):
            return k32[:, C32[n][0]:C32[n][1]]

        def c_16(n):
            return k16[:, C16[n][0]:C16[n][1]]

        ident = c_32("ident")

        def slab(name, words):
            return sb(name, [P, words])

        def view(s, at, *dims, dt=f32):
            n = 1
            for d in dims:
                n *= d
            v = s[:, at:at + n * mybir.dt.size(dt) // 4]
            if dt != f32:
                v = v.bitcast(dt)
            names = "abcd"[:len(dims)]
            return v.rearrange(f"p ({' '.join(names)}) -> p {' '.join(names)}", **dict(zip(names, dims)))

        tab_slab = slab("tab_slab", NC * ROW)
        tab = view(tab_slab, 0, NC, ROW)
        x_again = view(tab_slab, 0, NC, H)
        x_slab = slab("x_slab", NC * H)
        x_sb = view(x_slab, 0, NC, H)
        qT = view(x_slab, 0, NG, T)
        xnT = sb("xnT", [P, NG, T])
        stats = sb("stats", [P, NC, 6])
        mv = sb("mv", [P, NC, 2])
        rs = sb("rs", [P, 4, NC])
        gate_sb = sb("gate_sb", [P, NG, E])
        wq_sb = sb("wq_sb", [P, NG, H])
        wkv_sb = sb("wkv_sb", [P, NG, 2 * H])
        bq_sb = sb("bq_sb", [P, NG])
        bkv_sb = sb("bkv_sb", [P, 2 * H])
        sdn_sb = sb("sdn_sb", [P, 3, H])
        LG = NC * (E + 2)
        NE = NC * E
        route = slab("route", 2 * LG + 2 * NE)
        lg = view(route, 0, NC, E + 2)
        lgm = view(route, LG, NC, E + 2)
        ex = view(route, 2 * LG, NC, E)
        exm = view(route, 2 * LG + NE, NC, E)
        rank_i = sb("rank_i", [P, NE], i32)
        digits = slab("digits", AHEAD * ROW)
        lo_i = view(digits, 0, NE, dt=i32)
        hi_i = view(digits, NE, NE, dt=i32)
        lo_h = view(digits, 2 * NE, NE, dt=f16)
        hi_h = view(digits, 2 * NE + NE // 2, NE, dt=f16)
        ov_sel = view(route, NE, NC, E)
        ov_hot = view(route, 2 * NE, NC, P, dt=f16)
        state = view(route, 0, 2, NG, P)
        st_t = view(route, 3 * NE, P)
        rank_f = sb("rank_f", [P, NE])
        top8 = sb("top8", [P, NC, 8])
        neg_max = sb("neg_max", [P, NC])
        sm = sb("sm", [P, 4, NC])
        chosen = sb("chosen", [P, NC, E], f16)
        zero = sb("zero", [P, H])
        silu_try = sb("silu_try", [P, 1])
        diag = sb("diag", [P, 8, 8, 8], f16)
        slot_t = sb("slot_t", [P, 2, E])
        gidx = sb("gidx", [P, TILES], i32)
        sidx = sb("sidx", [P, TILES], i32)
        ov = sb("ov", [P, 4, E])
        ov_one = sb("ov_one", [P, EXTRA, E])
        ov_ones = sb("ov_ones", [P, E])
        ov_n = sb("ov_n", [1, 1], i32)
        ov_e = sb("ov_e", [1, EXTRA], i32)
        ov_j = sb("ov_j", [P, 1])
        ov_base = sb("ov_base", [P, 1])
        ov_s = sb("ov_s", [P, 8])
        ov_first = sb("ov_first", [P, EXTRA])
        ov_rank = sb("ov_rank", [P, NC])
        ov_adj = sb("ov_adj", [P, NC])
        ov_idx = sb("ov_idx", [P, 2], i32)
        ov_t = sb("ov_t", [P, 2])
        ov_comb = sb("ov_comb", [P, E])
        w1_slab = slab("w1_slab", RING * W1C)
        w1_sb = view(w1_slab, 0, RING, W1C)
        qbd = view(w1_slab, 0, NG, NC * HG, P)
        qsT = view(w1_slab, NG * NC * HG * P, NG, T)
        kT = view(w1_slab, NG * NC * HG * P + NG * T, NG, T)
        sact = view(w1_slab, NG * NC * HG * P + 2 * NG * T, 3, T)
        w2_slab = slab("w2_slab", RING * H)
        w2_sb = view(w2_slab, 0, RING, H)[0:F2]
        ks = view(w2_slab, 0, NC, H)
        stmp = view(w2_slab, NC * H, 2, 512)
        pT = view(w2_slab, NC * H + 1024, 2, HG * P)
        gcol = sb("gcol", [P, AHEAD], i32)
        scol = sb("scol", [P, 4], i32)
        rows = view(digits, 0, AHEAD, ROW)
        xT = sb("xT", [P, 2, H])
        xT_lo = sb("xT_lo", [P, 2, H])
        sg = sb("sg", [P, 2, F])
        act = sb("act", [P, 2, 2 * P])
        aT = sb("aT", [P, 2, 2 * P])
        y = sb("y", [P, 4, H])
        kv = sb("kv", [P, NC, 2 * H])


        with nc.sbuf_tensor("one_hots", [P, 24 * NE // 2], f32) as hots:
            lo_hot = view(hots, 0, NC * 8, 16, 8, dt=f16)
            hi_hot = view(hots, 16 * NE // 2, 8, NC, E, dt=f16)
        with nc.sbuf_tensor("routed_sums", [P, 2 * NC * H], f32) as sums:
            acc_sb = [view(sums, 0, NC, H), view(sums, NC * H, NC, H)]
        w_split = slab("w_split", 6 * 4 * F)
        w_hi = view(w_split, 0, 4, 4 * F)
        w_lo = view(w_split, 4 * 4 * F, 2, 4 * F)
        sgu_sb = sb("sgu_sb", [P, NG, 2 * FS])
        res = sb("res", [P, 2, H])

        ps = [ctx.enter_context(nc.psum_tensor(f"ps{b}", [P, 512], f32)) for b in range(8)]

        x_in = [sem(f"x_in{n}") for n in range(4)]
        ident_in = sem("ident_in")
        c16_in = sem("c16_in")
        c32_in = sem("c32_in")
        gate_in = sem("gate_in")
        wq_in = sem("wq_in")
        wkv_in = sem("wkv_in")
        bias_in = sem("bias_in")
        shared_in = sem("shared_in")
        w_in = [sem(f"w_in{s}") for s in range(RING)]
        dve_step = sem("dve_step")
        pool_step = sem("pool_step")
        var_ready, std_ready = sem("var_ready"), sem("std_ready")
        xn_ready = sem("xn_ready")
        xnT_ps, xnT_a, xnT_v = sem("xnT_ps"), sem("xnT_a"), sem("xnT_v")
        logits_ps = sem("logits_ps")
        shifted_ready, ex_ready = sem("shifted_ready"), sem("ex_ready")
        comb_ready, table_out = sem("comb_ready"), sem("table_out")
        chosen_ready, rank_ps = sem("chosen_ready"), sem("rank_ps")
        hot_ready, diag_ps, diag_ready, slot_ps = sem("hot_ready"), sem("diag_ps"), sem("diag_ready"), sem("slot_ps")
        digits_ready, counts_read = sem("digits_ready"), sem("counts_read")
        ov_ready = sem("ov_ready")
        zero_ready = sem("zero_ready")
        q_ps, q_sb = sem("q_ps"), sem("q_sb")
        kv_ps, kv_sb = sem("kv_ps"), sem("kv_sb")
        rows_in = [sem(f"rows_in{r}") for r in range(AHEAD)]
        gcol_ready, scol_ready = sem("gcol_ready"), sem("scol_ready")
        xT_ps, xT_sb, xlo_sb = sem("xT_ps"), sem("xT_sb"), sem("xlo_sb")
        whi_sb, wlo_sb = sem("whi_sb"), sem("wlo_sb")
        gu_ps, sg_sb, act_sb = sem("gu_ps"), sem("sg_sb"), sem("act_sb")
        aT_ps, aT_sb = sem("aT_ps"), sem("aT_sb")
        y_ps, y_sb = sem("y_ps"), sem("y_sb")
        acc_done = [sem("acc_done0"), sem("acc_done1")]
        act_zero, silu_zero = sem("act_zero"), sem("silu_zero")
        ov_hot_ready, ov_list_ps, ov_idx_ready, ov_expert_ready = (
            sem("ov_hot_ready"), sem("ov_list_ps"), sem("ov_idx_ready"), sem("ov_expert_ready"))
        ov_rows_in, ov_w_in = sem("ov_rows_in"), sem("ov_w_in")
        late_in = sem("late_in")
        acc_in, x_again_in = sem("acc_in"), sem("x_again_in")
        sgu_ps, stmp_sb, sact_sb = sem("sgu_ps"), sem("stmp_sb"), sem("sact_sb")
        kvb_ready, qbd_ready, qs_ready, ks_ready = sem("kvb_ready"), sem("qbd_ready"), sem("qs_ready"), sem("ks_ready")
        kT_ps, kT_a, kT_v = sem("kT_ps"), sem("kT_a"), sem("kT_v")
        s_ps, p_sb = sem("s_ps"), sem("p_sb")
        o_ps, st_ps, st_sb = sem("o_ps"), sem("st_ps"), sem("st_sb")
        xab_ready, res_sb = sem("xab_ready"), sem("res_sb")
        out_done = [sem("out_done0"), sem("out_done1")]
        sp_waited, pool_waited = sem("sp_waited"), sem("pool_waited")

        x_v = x.rearrange("(c p) h -> p c h", p=P)
        out_v = out.rearrange("(c p) h -> p c h", p=P)
        table_v = table.rearrange("(c p) h -> p c h", p=P)
        acc_v = [a.rearrange("(c p) h -> p c h", p=P) for a in acc]

        def rr(ap):
            return ap.bitcast(mybir.dt.float32r)

        def bc(ap, shape):
            return ap.unsqueeze(2).to_broadcast(shape)

        ov_steps = sem("ov_steps")
        LO_POOL = 4
        LISTED = (7, 11)

        def fetched_at(k):
            if k < RING - AHEAD:
                return k
            return k - LATE if RING - AHEAD <= k - LATE < RING + EXTRA - AHEAD else None

        block = ctx.enter_context(nc.Block())

        @block.sync
        def _(sp):
            for n in range(4):
                sp.dma_start(x_sb[:, 2 * n:2 * n + 2, :], x_v[:, 2 * n:2 * n + 2, :]).then_inc(x_in[n], 16)
            sp.dma_start(k32[:, 0:P], c32[:, 0:P]).then_inc(ident_in, 16)
            sp.dma_start(gate_sb[:], gate).then_inc(gate_in, 16)
            sp.dma_start(wq_sb[:], wq).then_inc(wq_in, 16)
            sp.dma_start(bq_sb[:], bq).then_inc(bias_in, 16)
            sp.dma_start(bkv_sb[:], bkv.partition_broadcast(P)).then_inc(bias_in, 16)
            sp.dma_start(k16[:], c16).then_inc(c16_in, 16)
            sp.dma_start(wkv_sb[:], wkv).then_inc(wkv_in, 16)
            sp.dma_start(k32[:, P:C32_LATE], c32[:, P:C32_LATE]).then_inc(c32_in, 16)

            def load_expert(slot, e):
                sp.dma_start(w1_sb[:, slot, :], w1[e, :, :]).then_inc(w_in[slot], 16)
                sp.dma_start(w2_sb[:, slot, :], w2[e, :, :]).then_inc(w_in[slot], 16)

            for s in range(RING):
                if s >= PACE:
                    sp.wait_ge(w_in[s - PACE], 32)
                load_expert(s, s)
            sp.wait_ge(rows_in[3], 16)
            sp.dma_start(sdn_sb[:, 0:2, :], sdn[0:2 * P, :].rearrange("(c p) h -> p c h", p=P)).then_inc(shared_in, 16)
            sp.dma_start(sdn_sb[0:FS - 2 * P, 2, :], sdn[2 * P:FS, :]).then_inc(shared_in, 16)
            half = (C32_LATE + C32W) // 2
            sp.dma_start(k32[:, C32_LATE:half], c32[:, C32_LATE:half]).then_inc(late_in, 16)
            sp.wait_ge(y_ps, 1)
            sp.dma_start(k32[:, half:C32W], c32[:, half:C32W]).then_inc(late_in, 16)
            for n in range(2):
                sp.wait_ge(y_ps, n + 2)
                sp.dma_start(sgu_sb[:, n, :], sgu[:, n, :]).then_inc(shared_in, 16)
            for n in range(2):
                sp.wait_ge(y_ps, n + 4)
                sp.dma_start(x_again[:, 4 * n:4 * n + 4, :], x_v[:, 4 * n:4 * n + 4, :]).then_inc(x_again_in, 16)
            with sp.Fori(0, E // RING - 1) as i:
                for s in range(RING):
                    sp.wait_ge(y_ps, i * RING + (s + 1))
                    sp.sem_inc(sp_waited, 1)
                    sp.wait_ge(w_in[(s - LOOP_PACE) % RING], i * 32 + (64 if s >= LOOP_PACE else 32))
                    e = i * RING + (RING + s)
                    sp.dma_start(w1_sb[:, s, :], w1[bass.ds(e, 1), :, :].rearrange("a p c -> p (a c)"))\
                        .then_inc(w_in[s], 16)
                    sp.dma_start(w2_sb[:, s, :], w2[bass.ds(e, 1), :, :].rearrange("a p c -> p (a c)"))\
                        .then_inc(w_in[s], 16)
            for j in range(EXTRA):
                sp.wait_ge(y_ps, E - RING + j + 1)
                sp.wait_ge(ov_expert_ready, j + 1)
                e = sp.value_load(ov_e[0:1, j:j + 1], min_val=0, max_val=E - 1)
                sp.dma_start(w1_sb[:, j, :], w1[bass.ds(e, 1), :, :].rearrange("a p c -> p (a c)"))\
                    .then_inc(w_in[j], 16)
                sp.dma_start(w2_sb[:, j, :], w2[bass.ds(e, 1), :, :].rearrange("a p c -> p (a c)"))\
                    .then_inc(w_in[j], 16)
            sp.wait_ge(ov_ready, 1)
            n_ov = sp.value_load(ov_n[0:1, 0:1], min_val=0, max_val=E - 1)
            with sp.If(n_ov > 0):
                with sp.Fori(0, n_ov) as j:
                    sp.wait_ge(y_ps, j + TILES)
                    sp.sem_inc(sp_waited, 1)
                    sp.wait_ge(ov_expert_ready, j + (EXTRA + 1))
                    sp.sem_inc(sp_waited, 1)
                    e = sp.value_load(ov_e[0:1, 0:1], min_val=0, max_val=E - 1)
                    sp.dma_start(w1_sb[:, 0, :], w1[bass.ds(e, 1), :, :].rearrange("a p c -> p (a c)"))\
                        .then_inc(ov_w_in, 16)
                    sp.dma_start(w2_sb[:, 0, :], w2[bass.ds(e, 1), :, :].rearrange("a p c -> p (a c)"))\
                        .then_inc(ov_w_in, 16)

            sp.wait_ge(acc_done[0], n_ov * 16 + 16 * (TILES // 2 + 1))
            sp.wait_ge(acc_done[1], 16 * (TILES // 2 + 1))
            for k in range(2):
                sp.dma_start(acc_sb[k], acc_v[k][:, 0:NC, :]).then_inc(acc_in, 16)
            for c in range(NC):
                sp.wait_ge(res_sb, c + 1)
                sp.dma_start(out_v[:, c, :], res[:, c % 2, :]).then_inc(out_done[c % 2], 16)
            for k in range(2):
                sp.wait_ge(out_done[k], 16 * (NC // 2))

        @block.gpsimd
        def _(pool):
            nc.gpsimd.memset(zero[:], 0.0).then_inc(zero_ready, 1)
            nc.gpsimd.memset(silu_try[:], 0.0).then_inc(silu_zero, 1)
            nc.gpsimd.memset(act[:], 0.0).then_inc(act_zero, 1)
            pool.wait_ge(xn_ready, NC)
            pool.dma_start(table_v[:, :, 0:H], tab[:, :, 0:H]).then_inc(table_out, 16)
            pool.wait_ge(zero_ready, 1)
            for k in range(2):
                pool.dma_start(acc_v[k], zero[:].unsqueeze(1).to_broadcast([P, ACC_ROWS // P, H]))\
                    .then_inc(acc_done[k], 16)
            pool.wait_ge(digits_ready, 1)
            for a in range(16 - LO_POOL, 16):
                ins = nc.gpsimd.tensor_scalar(lo_hot[:, :, a, :], lo_h.rearrange("p (n e) -> p n e", e=8), float(a),
                                              None, ALU.is_equal)
            ins.then_inc(hot_ready, 1)
            pool.wait_ge(comb_ready, 1)
            pool.dma_start(table_v[:, :, H:ROW], tab[:, :, H:ROW]).then_inc(table_out, 16)
            pool.wait_ge(hot_ready, 2)
            nc.gpsimd.memset(rows[:], 0.0).then_inc(zero_ready, 1)
            pool.wait_ge(zero_ready, 2)
            pool.wait_ge(table_out, 32)

            def gather(r):
                pool.indirect_dma_start(
                    out=rows[:, r, :], out_offset=None, in_=table,
                    in_offset=bass.IndirectOffsetOnAxis(ap=gcol[:, r:r + 1], axis=0),
                    bounds_check=T - 1, oob_is_err=False).then_inc(rows_in[r], 16)

            def scatter(k, r):
                pool.indirect_dma_start(
                    out=acc[k], out_offset=bass.IndirectOffsetOnAxis(ap=scol[:, r:r + 1], axis=0),
                    in_=y[:, r, :], in_offset=None, compute_op=ALU.add).then_inc(acc_done[k], 16)

            pool.wait_ge(gcol_ready, 1)
            for r in range(AHEAD):
                gather(r)
            def fetch(t, k):
                pool.wait_ge(gcol_ready, t + 2)
                pool.sem_inc(pool_waited, 1)
                gather(k % AHEAD)

            def store(t, k):
                pool.wait_ge(y_sb, t + 1)
                pool.wait_ge(scol_ready, t + 1)
                pool.wait_ge(acc_done[k % 2], (t - k) * 8 + 16 * (k // 2 + 1))
                pool.sem_inc(pool_waited, 1)
                scatter(k % 2, k % 4)

            fetch(0, 0)
            with pool.Fori(0, E // RING - 1) as i:
                for k in range(1, RING + 1):
                    fetch(i * RING + k, k)
                    store(i * RING + (k - 1), k - 1)
            for k in range(1, RING + EXTRA + 1):
                if fetched_at(k) is not None:
                    fetch(E - RING + fetched_at(k), fetched_at(k))
                store(E - RING + k - 1, k - 1)

            pool.wait_ge(ov_ready, 1)
            n_ov = pool.value_load(ov_n[0:1, 0:1], min_val=0, max_val=E - 1)
            with pool.If(n_ov > 0):
                with pool.Fori(0, n_ov) as j:
                    pool.wait_ge(ov_idx_ready, j + 1)
                    pool.sem_inc(pool_waited, 1)
                    pool.indirect_dma_start(
                        out=rows[:, 0, :], out_offset=None, in_=table,
                        in_offset=bass.IndirectOffsetOnAxis(ap=ov_idx[:, 0:1], axis=0),
                        bounds_check=T - 1, oob_is_err=False).then_inc(ov_rows_in, 16)
                    pool.wait_ge(y_sb, j + (TILES + 1))
                    pool.wait_ge(acc_done[0], j * 16 + 16 * (TILES // 2 + 1))
                    pool.sem_inc(pool_waited, 1)
                    pool.indirect_dma_start(
                        out=acc[0], out_offset=bass.IndirectOffsetOnAxis(ap=ov_idx[:, 1:2], axis=0),
                        in_=y[:, 0, :], in_offset=None, compute_op=ALU.add).then_inc(acc_done[0], 16)
            pool.wait_ge(acc_in, 32)
            nc.gpsimd.tensor_tensor(acc_sb[1], acc_sb[1], acc_sb[0], ALU.add).then_inc(pool_step, 1)
            pool.wait_ge(pool_step, 1)
            pool.wait_ge(x_again_in, 32)
            nc.gpsimd.tensor_tensor(acc_sb[1], acc_sb[1], x_again, ALU.add).then_inc(xab_ready, 1)

        @block.scalar
        def _(act_e):
            act_e.wait_ge(var_ready, 1)
            nc.scalar.activation(rs[:, 1, :], rs[:, 0, :], ACT.Sqrt).then_inc(std_ready, 1)
            for n in range(2):
                act_e.wait_ge(xnT_ps, n + 1)
                nc.scalar.copy(xnT[:, 0, n * 512:(n + 1) * 512], ps[n][:]).then_inc(xnT_a, 1)
            act_e.wait_ge(shifted_ready, 1)
            for c in range(NC):
                nc.scalar.activation(ex[:, c, :], lg[:, c, 0:E], ACT.Exp, bias=neg_max[:, c:c + 1],
                                     accum_out=sm[:, 0, c:c + 1]).then_inc(ex_ready, 1)
            act_e.wait_ge(bias_in, 32)
            for n in range(4):
                act_e.wait_ge(q_ps, n + 1)
                nc.scalar.activation(qT[:, n // 2, (n % 2) * 512:(n % 2 + 1) * 512], ps[n % 2][:], ACT.Identity,
                                     bias=bq_sb[:, n // 2:n // 2 + 1]).then_inc(q_sb, 1)
            act_e.wait_ge(silu_zero, 1)
            nc.scalar.activation(silu_try[:], silu_try[:], ACT.Silu)
            for c in range(NC):
                act_e.wait_ge(kv_ps, c + 1)
                nc.scalar.copy(kv[:, c, :], ps[c % 4][:]).then_inc(kv_sb, 1)

            def split_w(i, k):
                t = i * RING + k
                act_e.wait_ge(w_in[k % RING], i * 32 + 32 * (k // RING + 1))
                if not (isinstance(t, int) and t < 4):
                    act_e.wait_ge(gu_ps, t - 3)
                nc.scalar.copy(rr(w_hi[:, k % 4, :]), w1_sb[:, k % RING, 0:4 * F]).then_inc(whi_sb, 1)

            def evac_xT(t, k):
                act_e.wait_ge(xT_ps, t + 1)
                if not (isinstance(t, int) and t < 2):
                    act_e.wait_ge(gu_ps, t - 1)
                nc.scalar.copy(rr(xT[:, k % 2, :]), ps[k % 2][:, 0:H]).then_inc(xT_sb, 1)

            def silu(t, k):
                act_e.wait_ge(gu_ps, t + 1)
                if not (isinstance(t, int) and t < 2):
                    act_e.wait_ge(act_sb, t - 1)
                nc.scalar.activation(sg[:, k % 2, :], ps[2 + k % 2][:, 0:F], ACT.Silu).then_inc(sg_sb, 1)

            def evac_aT(t, k):
                act_e.wait_ge(aT_ps, t + 1)
                if not (isinstance(t, int) and t < 2):
                    act_e.wait_ge(y_ps, t - 1)
                nc.scalar.copy(aT[:, k % 2, :], ps[4 + k % 2][:, 0:2 * P]).then_inc(aT_sb, 1)

            def evac_y(t, k, first):
                act_e.wait_ge(y_ps, t + 1)
                if not first:
                    act_e.wait_ge(acc_done[k % 2], (t - k) * 8 + 16 * (k // 2))
                nc.scalar.copy(y[:, k % 4, :], ps[6 + k % 2][:, 0:H]).then_inc(y_sb, 1)

            act_e.wait_ge(diag_ps, 1)
            for k in range(3):
                split_w(0, k)
            evac_xT(0, 0)
            silu(0, 0)
            evac_xT(1, 1)

            def expert_act(i, k, ahead=3):
                t = i * RING + k
                if not (isinstance(t, int) and t < 2):
                    evac_y(t - 2, k - 2, isinstance(t, int) and t < 6)
                if ahead >= 3:
                    split_w(i, k + 3)
                if ahead >= 1:
                    silu(t + 1, k + 1)
                if ahead >= 2:
                    evac_xT(t + 2, k)
                evac_aT(t, k)

            for k in range(6):
                expert_act(0, k)
            with act_e.Fori(0, E // RING - 1) as i:
                for k in range(6, RING + 6):
                    expert_act(i, k)
            for k in range(6, RING + EXTRA):
                expert_act(E // RING - 1, k, ahead=min(3, RING + EXTRA - 1 - k))
            for k in range(RING + EXTRA - 2, RING + EXTRA):
                evac_y(E - RING + k, k, False)

            act_e.wait_ge(ov_ready, 1)
            n_ov = act_e.value_load(ov_n[0:1, 0:1], min_val=0, max_val=E - 1)
            with act_e.If(n_ov > 0):
                with act_e.Fori(0, n_ov) as j:
                    act_e.wait_ge(ov_w_in, j * 32 + 32)
                    nc.scalar.copy(rr(w_hi[:, 0, :]), w1_sb[:, 0, 0:4 * F]).then_inc(whi_sb, 1)
                    act_e.wait_ge(xT_ps, j + (TILES + 1))
                    nc.scalar.copy(rr(xT[:, 0, :]), ps[0][:, 0:H]).then_inc(xT_sb, 1)
                    act_e.wait_ge(gu_ps, j + (TILES + 1))
                    nc.scalar.activation(sg[:, 0, :], ps[2][:, 0:F], ACT.Silu).then_inc(sg_sb, 1)
                    act_e.wait_ge(aT_ps, j + (TILES + 1))
                    nc.scalar.copy(aT[:, 0, :], ps[4][:, 0:2 * P]).then_inc(aT_sb, 1)
                    act_e.wait_ge(y_ps, j + (TILES + 1))
                    act_e.wait_ge(acc_done[0], j * 16 + 16 * (TILES // 2 + 1))
                    nc.scalar.copy(y[:, 0, :], ps[6][:, 0:H]).then_inc(y_sb, 1)

            for n in range(6):
                act_e.wait_ge(sgu_ps, n + 1)
                if n >= 2:
                    act_e.wait_ge(sact_sb, n - 1)
                rows_n = P if n % 3 < 2 else FS - 2 * P
                nc.scalar.activation(stmp[0:rows_n, n % 2, :], ps[(n % 2) * 2][0:rows_n, :], ACT.Silu)\
                    .then_inc(stmp_sb, 1)
            for n in range(2):
                act_e.wait_ge(kT_ps, n + 1)
                nc.scalar.copy(kT[:, 0, n * 512:(n + 1) * 512], ps[4 + n][:]).then_inc(kT_a, 1)

        @block.vector
        def _(dve):
            step = [0]

            def link(ins):
                step[0] += 1
                ins.then_inc(dve_step, 1)
                dve.wait_ge(dve_step, step[0])

            V = nc.vector
            for c in range(NC):
                if c % 2 == 0:
                    dve.wait_ge(x_in[c // 2], 16)
                ins = V.bn_stats(stats[:, c, :], x_sb[:, c, :])
            link(ins)
            for c in range(NC):
                ins = V.bn_aggr(mv[:, c, :], stats[:, c, :])
            link(ins)
            V.tensor_scalar(rs[:, 0, :], mv[:, :, 1], 1e-5, None, ALU.add).then_inc(var_ready, 1)
            dve.wait_ge(std_ready, 1)
            link(V.reciprocal(rs[:, 2, :], rs[:, 1, :]))
            link(V.tensor_tensor(rs[:, 3, :], rs[:, 2, :], rs[:, 2, :], ALU.mult))
            link(V.scalar_tensor_tensor(rs[:, 3, :], rs[:, 3, :], -0.5, rs[:, 0, :], ALU.mult, ALU.mult))
            link(V.scalar_tensor_tensor(rs[:, 2, :], rs[:, 3, :], 1.5, rs[:, 2, :], ALU.add, ALU.mult))
            for c in range(NC):
                V.tensor_scalar(tab[:, c, 0:H], x_sb[:, c, :], mv[:, c, 0:1], rs[:, 2, c:c + 1],
                                ALU.subtract, ALU.mult).then_inc(xn_ready, 1)
            V.memset(lg[:, :, E:E + 2], BIG)
            V.memset(ov_ones[:], 1.0)
            V.memset(ov_j[:], 0.0)
            V.memset(ov_base[:], P - UNCHOSEN)
            for n in range(2):
                dve.wait_ge(xnT_ps, n + 1)
                V.tensor_copy(xnT[:, 1, n * 512:(n + 1) * 512], ps[2 + n][:]).then_inc(xnT_v, 1)

            dve.wait_ge(logits_ps, 1)
            link(V.tensor_copy(lg[:, :, 0:E], ps[4][:].rearrange("p (c e) -> p c e", e=E)))
            for c in range(NC):
                ins = V.max(top8[:, c, :], lg[:, c, 0:E])
            link(ins)
            link(V.tensor_scalar(neg_max[:], top8[:, :, 0], -1.0, None, ALU.mult))
            V.memset(top8[:, :, TOPK:8], BIG).then_inc(shifted_ready, 1)
            dve.wait_ge(shifted_ready, 1)
            for c in range(NC):
                ins = V.match_replace(lgm[:, c, :], top8[:, c, :], lg[:, c, :], -BIG)
            link(ins)
            V.tensor_tensor(chosen[:], lg[:, :, 0:E], lgm[:, :, 0:E], ALU.not_equal).then_inc(chosen_ready, 1)
            dve.wait_ge(chosen_ready, 1)
            dve.wait_ge(ex_ready, NC)
            link(V.tensor_tensor(exm[:], ex[:], chosen[:], ALU.mult))
            V.tensor_reduce(sm[:, 1, :], exm[:], AX, ALU.add)
            link(V.reciprocal(sm[:, 2, :], sm[:, 0, :]))
            link(V.tensor_tensor(sm[:, 1, :], sm[:, 1, :], sm[:, 2, :], ALU.mult))
            link(V.tensor_scalar(sm[:, 1, :], sm[:, 1, :], 1e-20, None, ALU.add))
            link(V.reciprocal(sm[:, 3, :], sm[:, 1, :]))
            link(V.tensor_tensor(sm[:, 3, :], sm[:, 3, :], sm[:, 2, :], ALU.mult))
            V.tensor_tensor(tab[:, :, H:ROW], exm[:], bc(sm[:, 3, :], [P, NC, E]), ALU.mult).then_inc(comb_ready, 1)

            dve.wait_ge(rank_ps, 1)
            link(V.scalar_tensor_tensor(rank_i[:], chosen[:].rearrange("p c e -> p (c e)"), -UNCHOSEN, ps[5][:],
                                        ALU.mult, ALU.add))
            V.tensor_scalar(lo_i[:], rank_i[:], 15, None, ALU.bitwise_and)
            link(V.tensor_scalar(hi_i[:], rank_i[:], 4, None, ALU.arith_shift_right))
            V.tensor_copy(lo_h[:], lo_i[:])
            V.tensor_copy(hi_h[:], hi_i[:]).then_inc(digits_ready, 1)
            dve.wait_ge(digits_ready, 1)
            dve.wait_ge(c16_in, 16)
            for b in range(8):
                V.scalar_tensor_tensor(hi_hot[:, b, :, :].rearrange("p c e -> p (c e)"), hi_h[:],
                                       float(b) - UNCHOSEN / 16, c_16("tok"), ALU.is_equal, ALU.mult)
            for a in range(16 - LO_POOL):
                ins = V.tensor_scalar(lo_hot[:, :, a, :], lo_h.rearrange("p (n e) -> p n e", e=8), float(a), None,
                                      ALU.is_equal)
            ins.then_inc(hot_ready, 1)
            dve.wait_ge(c32_in, 16)
            dve.wait_ge(diag_ps, 1)
            V.tensor_tensor(diag[:].rearrange("p g b e -> p (g b) e"), ps[7][:].rearrange("p (gb e) -> p gb e", e=8),
                            c_32("mask8").unsqueeze(1).to_broadcast([P, 64, 8]), ALU.mult).then_inc(diag_ready, 1)
            dve.wait_ge(slot_ps, 1)

            def indices(lst, tmp, g_out, s_out):
                V.tensor_scalar(tmp[0], lst, 0.0, float(SKIP + 1), ALU.is_equal, ALU.mult)
                link(V.tensor_scalar(tmp[1], lst, 0.0, c_32("padrow"), ALU.is_equal, ALU.mult))
                V.scalar_tensor_tensor(g_out, lst, -1.0, tmp[0], ALU.add, ALU.add)
                return V.scalar_tensor_tensor(s_out, lst, -1.0, tmp[1], ALU.add, ALU.add)

            link(indices(ps[4][:, 0:E], (slot_t[:, 0, :], slot_t[:, 1, :]), gidx[:, 0:E], sidx[:, 0:E]))
            V.tensor_copy(gcol[:], gidx[:, 0:AHEAD]).then_inc(gcol_ready, 1)

            V.tensor_copy(rank_f[:], rank_i[:])
            dve.wait_ge(rank_ps, 2)
            link(V.tensor_scalar(ov[:, 0, :], ps[6][:, 0:E], float(P), None, ALU.is_gt))
            for j in range(2, T // P):
                link(V.scalar_tensor_tensor(ov[:, 0, :], ps[6][:, 0:E], float(P * j), ov[:, 0, :],
                                            ALU.is_gt, ALU.add))
            link(V.tensor_tensor_scan(ov[:, 1, :], ov_ones[:], ov[:, 0, :], 0.0, ALU.mult, ALU.add))
            V.tensor_scalar(ov_n[:], ov[0:1, 1, E - 1:E], float(-EXTRA), 0.0, ALU.add, ALU.max).then_inc(ov_ready, 1)
            V.tensor_tensor(ov[:, 2, :], ov[:, 1, :], ov[:, 0, :], ALU.subtract).then_inc(counts_read, 1)
            dve.wait_ge(counts_read, 1)

            def gate_up(t, k, comb):
                dve.wait_ge(sg_sb, t + 1)
                if not (isinstance(t, int) and t < 2):
                    dve.wait_ge(aT_ps, t - 1)
                V.scalar_tensor_tensor(act[:, k % 2, 0:F], ps[2 + k % 2][:, F:2 * F], comb, sg[:, k % 2, :],
                                       ALU.mult, ALU.mult).then_inc(act_sb, 1)

            def w_low(t, k):
                dve.wait_ge(whi_sb, t + 1)
                if not (isinstance(t, int) and t < 2):
                    dve.wait_ge(gu_ps, t - 1)
                V.tensor_tensor(rr(w_lo[:, k % 2, :]), w1_sb[:, k % RING, 0:4 * F], w_hi[:, k % 4, :],
                                ALU.subtract).then_inc(wlo_sb, 1)

            def x_low(t, k):
                dve.wait_ge(xT_sb, t + 1)
                V.tensor_tensor(rr(xT_lo[:, k % 2, :]), ps[k % 2][:, 0:H], xT[:, k % 2, :], ALU.subtract)\
                    .then_inc(xlo_sb, 1)

            def extra_expert(n, chained):
                chained(V.tensor_scalar(ov_one[:, n, :], ov[:, 1, :], ov_j[:], None, ALU.is_gt))
                chained(V.scalar_tensor_tensor(ov_one[:, n, :], ov[:, 2, :], ov_j[:], ov_one[:, n, :],
                                               ALU.is_le, ALU.mult))
                chained(V.tensor_tensor(ov[:, 3, :], ov_one[:, n, :], c_32("iota_e"), ALU.mult))
                chained(V.tensor_reduce(ov_s[:, 0:1], ov[:, 3, :], AX, ALU.add))
                V.tensor_copy(ov_e[:, n:n + 1], ov_s[0:1, 0:1]).then_inc(ov_expert_ready, 1)

            def extra_base(n, chained):
                chained(V.tensor_tensor(ov[:, 3, :], ov_one[:, n, :], ov[:, 2, :], ALU.mult))
                chained(V.tensor_reduce(ov_s[:, 1:2], ov[:, 3, :], AX, ALU.add))
                chained(V.scalar_tensor_tensor(ov_first[:, n:n + 1], ov_s[:, 1:2], float(-P), ov_base[:],
                                               ALU.mult, ALU.add))
                V.tensor_scalar(ov_j[:], ov_j[:], 1.0, None, ALU.add)
                chained(V.tensor_scalar(ov_base[:], ov_base[:], float(P), None, ALU.add))

            def extra_ranks(n, chained):
                chained(V.tensor_tensor(ov_sel[:], rank_f[:].rearrange("p (c e) -> p c e", e=E),
                                        ov_one[:, n, :].unsqueeze(1).to_broadcast([P, NC, E]), ALU.mult))
                chained(V.tensor_reduce(ov_rank[:], ov_sel[:], AX, ALU.add))
                chained(V.tensor_scalar(ov_adj[:], ov_rank[:], ov_first[:, n:n + 1], None, ALU.subtract))

            def extra_hot(n, chained):
                for c in range(NC):
                    ins = V.tensor_scalar(ov_hot[:, c, :], c_32("iota_s"), ov_adj[:, c:c + 1], None, ALU.is_equal)
                ins.then_inc(ov_hot_ready, 1)

            def extra_weight(r, n, chained):
                chained(V.tensor_tensor(ov_comb[:], rows[:, r, H:ROW], ov_one[:, n, :], ALU.mult))
                chained(V.tensor_reduce(ov_s[:, 4:5], ov_comb[:], AX, ALU.add))

            def extra_indices(n, bank):
                dve.wait_ge(ov_list_ps, n + 1)
                lst = bank[:, H:H + 1]
                link(indices(lst, (ov_t[:, 0:1], ov_t[:, 1:2]), gidx[:, E + n:E + n + 1], sidx[:, E + n:E + n + 1]))

            pieces = (extra_expert, extra_base, extra_ranks, extra_hot)
            w_low(0, 0)
            x_low(0, 0)
            dve.wait_ge(act_zero, 1)
            w_low(1, 1)
            gate_up(0, 0, rows[:, 0, H:H + 1])
            x_low(1, 1)

            def expert_dve(t, k, first=False, last=False):
                if not first:
                    dve.wait_ge(acc_done[k % 2], (t - k) * 8 + 16 * (k // 2))
                V.tensor_copy(scol[:, k % 4:k % 4 + 1], sidx[:, bass.ds(t, 1)]).then_inc(scol_ready, 1)
                nxt = fetched_at(k) if last else k
                if nxt is not None:
                    r = nxt % AHEAD
                    V.tensor_copy(gcol[:, r:r + 1], gidx[:, bass.ds(t - k + nxt + AHEAD, 1)]).then_inc(gcol_ready, 1)
                ahead = not (last and k >= RING + EXTRA - 2)
                if ahead:
                    w_low(t + 2, k + 2)
                if last and k >= RING - 1:
                    if k < RING + EXTRA - 1:
                        j = k - (RING - 1)
                        dve.wait_ge(sg_sb, E + j + 1)
                        extra_weight((k + 1) % AHEAD, j, link)
                        gate_up(E + j, k + 1, ov_s[:, 4:5])
                else:
                    gate_up(t + 1, k + 1, rows[:, (k + 1) % AHEAD, bass.ds(t + (H + 1), 1)])
                if ahead:
                    x_low(t + 2, k)

            pieces_at = {0: (extra_expert, 0), 1: (extra_base, 0), 2: (extra_expert, 1), 3: (extra_base, 1),
                         4: (extra_ranks, 0), 6: (extra_hot, 0), 8: (extra_ranks, 1), 10: (extra_hot, 1)}
            for k in range(4):
                expert_dve(k, k, first=True)
                piece, n = pieces_at[k]
                piece(n, link)
            with dve.Fori(0, E // RING - 1) as i:
                for k in range(4, RING + 4):
                    expert_dve(i * RING + k, k)
            for k in range(4, RING + EXTRA):
                if k - 1 in LISTED:
                    dve.wait_ge(y_sb, E - RING + k - 1)
                    extra_indices(LISTED.index(k - 1), ps[6 + (k - 2) % 2])
                expert_dve(E - RING + k, k, last=True)
                if k in pieces_at:
                    piece, n = pieces_at[k]
                    piece(n, link)

            n_ov = dve.value_load(ov_n[0:1, 0:1], min_val=0, max_val=E - 1)

            def ov_body(j):
                count = [0]

                def olink(ins):
                    count[0] += 1
                    ins.then_inc(ov_steps, 1)
                    dve.wait_ge(ov_steps, j * OV_LINKS + count[0])

                for piece in pieces:
                    piece(0, olink)
                dve.wait_ge(ov_list_ps, j + (EXTRA + 1))
                lst = ps[7][:, H:H + 1]
                V.tensor_scalar(ov_t[:, 0:1], lst, 0.0, float(SKIP + 1), ALU.is_equal, ALU.mult)
                olink(V.tensor_scalar(ov_t[:, 1:2], lst, 0.0, c_32("padrow"), ALU.is_equal, ALU.mult))
                dve.wait_ge(acc_done[0], j * 16 + 16 * (TILES // 2 + 1))
                V.scalar_tensor_tensor(ov_idx[:, 0:1], lst, -1.0, ov_t[:, 0:1], ALU.add, ALU.add)
                V.scalar_tensor_tensor(ov_idx[:, 1:2], lst, -1.0, ov_t[:, 1:2], ALU.add, ALU.add)\
                    .then_inc(ov_idx_ready, 1)
                dve.wait_ge(ov_rows_in, j * 16 + 16)
                extra_weight(0, 0, olink)
                w_low(j + TILES, 0)
                x_low(j + TILES, 0)
                dve.wait_ge(sg_sb, j + (TILES + 1))
                V.scalar_tensor_tensor(act[:, 0, 0:F], ps[2][:, F:2 * F], ov_s[:, 4:5], sg[:, 0, :],
                                       ALU.mult, ALU.mult).then_inc(act_sb, 1)
                assert count[0] == OV_LINKS, count

            OV_LINKS = 14
            with dve.If(n_ov > 0):
                with dve.Fori(0, n_ov) as j:
                    ov_body(j)

            dve.wait_ge(late_in, 32)
            def bias_kv(c):
                V.tensor_tensor(kv[:, c, :], kv[:, c, :], bkv_sb[:], ALU.add).then_inc(kvb_ready, 1)

            def split_heads(g, h):
                V.tensor_scalar(qbd[:, g, h::HG, :], qT[:, g, :].rearrange("p (c i) -> p c i", i=P),
                                c_32("hmask")[:, h:h + 1], None, ALU.mult).then_inc(qbd_ready, 1)

            dve.wait_ge(kv_sb, NC)
            dve.wait_ge(q_sb, 4)
            dve.wait_ge(y_ps, n_ov + TILES)
            extra = [lambda c=c: bias_kv(c) for c in range(NC)]
            heads = [lambda g=g, h=h: split_heads(g, h) for g in range(NG) for h in range(HG)]
            for f in extra[0:4]:
                f()
            for n in range(6):
                rows_n = P if n % 3 < 2 else FS - 2 * P
                dve.wait_ge(stmp_sb, n + 1)
                V.tensor_tensor(sact[0:rows_n, n % 3, (n // 3) * 512:(n // 3 + 1) * 512],
                                ps[(n % 2) * 2 + 1][0:rows_n, :], stmp[0:rows_n, n % 2, :], ALU.mult)\
                    .then_inc(sact_sb, 1)
                if n < 2:
                    for f in extra[4 + 2 * n:6 + 2 * n]:
                        f()
                    if n == 1:
                        dve.wait_ge(kvb_ready, NC)
                        for c in range(NC):
                            V.tensor_tensor(ks[:, c, :], kv[:, c, 0:H], c_32("kscale"), ALU.mult).then_inc(ks_ready, 1)
                elif n < 4:
                    for f in heads[4 * (n - 2):4 * (n - 1)]:
                        f()
                elif n == 4:
                    for g in range(NG):
                        V.tensor_tensor(qsT[:, g, :].rearrange("p (c i) -> p c i", i=P),
                                        qT[:, g, :].rearrange("p (c i) -> p c i", i=P),
                                        c_32("qscale")[:, g * P:(g + 1) * P].unsqueeze(1).to_broadcast([P, NC, P]),
                                        ALU.mult).then_inc(qs_ready, 1)
            for n in range(2):
                dve.wait_ge(kT_ps, n + 1)
                V.tensor_copy(kT[:, 1, n * 512:(n + 1) * 512], ps[6 + n][:]).then_inc(kT_v, 1)

            n_state = 0
            for u in range(2 * NC):
                c, g = u // 2, u % 2
                dve.wait_ge(s_ps, u + 1)
                if u >= 2:
                    dve.wait_ge(o_ps, u - 1)
                V.tensor_tensor(pT[:, u % 2, :], ps[u % 2][:],
                                c_32("decay")[:, g * HG * P:(g + 1) * HG * P], ALU.mult).then_inc(p_sb, 1)
                if u >= 2 and u % 2 == 0:
                    finish = c - 1
                    if finish == 0:
                        dve.wait_ge(xab_ready, 1)
                    dve.wait_ge(o_ps, 2 * (finish + 1))
                    if finish >= 2:
                        dve.wait_ge(out_done[finish % 2], 16 * (finish // 2))
                    V.tensor_tensor(res[:, finish % 2, :], ps[4 + finish % 2][:, 0:H], acc_sb[1][:, finish, :],
                                    ALU.add).then_inc(res_sb, 1)
                if c % SEQ_CHUNKS < SEQ_CHUNKS - 1:
                    m = c % SEQ_CHUNKS
                    n_state += 1
                    dve.wait_ge(st_ps, n_state)
                    if m == 0:
                        V.tensor_tensor(state[:, 0, g, :], ps[6 + n_state % 2][:, 0:P], c_32("bdmask"), ALU.mult)\
                            .then_inc(st_sb, 1)
                    else:
                        dve.wait_ge(st_sb, n_state - 1)
                        link(V.tensor_tensor(st_t[:], ps[6 + n_state % 2][:, 0:P], c_32("bdmask"), ALU.mult))
                        V.scalar_tensor_tensor(state[:, m % 2, g, :], state[:, (m - 1) % 2, g, :],
                                               c_32("gc")[:, g:g + 1], st_t[:], ALU.mult, ALU.add).then_inc(st_sb, 1)
            dve.wait_ge(o_ps, 2 * NC)
            dve.wait_ge(out_done[(NC - 1) % 2], 16 * ((NC - 1) // 2))
            V.tensor_tensor(res[:, (NC - 1) % 2, :], ps[4 + (NC - 1) % 2][:, 0:H], acc_sb[1][:, NC - 1, :],
                            ALU.add).then_inc(res_sb, 1)

        @block.tensor
        def _(pe):
            mm = nc.tensor.matmul
            pe.wait_ge(ident_in, 16)
            for c in range(NC):
                pe.wait_ge(xn_ready, c + 1)
                for k in range(NG):
                    ins = nc.tensor.transpose(ps[2 * k + c // 4][:, (c % 4) * P:(c % 4 + 1) * P],
                                              tab[:, c, k * P:(k + 1) * P], ident)
                if c % 4 == 3:
                    ins.then_inc(xnT_ps, 1)
            pe.wait_ge(gate_in, 16)
            for c in range(NC):
                pe.wait_ge(xnT_a, c // 4 + 1)
                pe.wait_ge(xnT_v, c // 4 + 1)
                for k in range(NG):
                    ins = mm(ps[4][:, c * E:(c + 1) * E], xnT[:, k, c * P:(c + 1) * P], gate_sb[:, k, :],
                             start=(k == 0), stop=(k == NG - 1))
            ins.then_inc(logits_ps, 1)
            pe.wait_ge(wq_in, 16)

            def q_unit(m):
                g, n = m // 2, m % 2
                if m >= 2:
                    pe.wait_ge(q_sb, m - 1)
                for k in range(NG):
                    ins = mm(ps[m % 2][:], wq_sb[:, k, g * P:(g + 1) * P], xnT[:, k, n * 512:(n + 1) * 512],
                             start=(k == 0), stop=(k == NG - 1))
                ins.then_inc(q_ps, 1)

            q_unit(0)
            q_unit(1)
            pe.wait_ge(c16_in, 16)
            pe.wait_ge(chosen_ready, 1)
            mm(ps[5][:], c_16("tri"), chosen[:].rearrange("p c e -> p (c e)"), start=True, stop=False)
            for c in range(NC - 1):
                ins = mm(ps[5][:, (c + 1) * E:].rearrange("p (c e) -> p c e", e=E), c_16("ones"),
                   chosen[:, c:c + 1, :].to_broadcast([P, NC - 1 - c, E]), start=False, stop=(c == NC - 2))
            ins.then_inc(rank_ps, 1)
            for c in range(NC):
                ins = mm(ps[6][:, 0:E], c_16("ones"), chosen[:, c, :], start=(c == 0), stop=(c == NC - 1))
            ins.then_inc(rank_ps, 1)
            q_unit(2)
            q_unit(3)
            pe.wait_ge(wkv_in, 16)
            pe.wait_ge(q_sb, 4)

            def kv_chunk(c):
                if c >= 4:
                    pe.wait_ge(kv_sb, c - 3)
                for k in range(NG):
                    ins = mm(ps[c % 4][:], xnT[:, k, c * P:(c + 1) * P], wkv_sb[:, k, :],
                             start=(k == 0), stop=(k == NG - 1))
                ins.then_inc(kv_ps, 1)

            for c in range(5):
                kv_chunk(c)
            pe.wait_ge(hot_ready, 2)
            for g in range(8):
                for c in range(NC):
                    ins = mm(ps[7][:, g * 64:(g + 1) * 64], lo_hot[:, c * 8 + g, :, :].rearrange("p a e -> p (a e)"),
                             hi_hot[:, :, c, 8 * g:8 * g + 8], start=(c == 0), stop=(c == NC - 1))
            ins.then_inc(diag_ps, 1)
            kv_chunk(5)
            pe.wait_ge(diag_ready, 1)
            for b in range(8):
                lo = C16["place"][0] + 112 - 16 * b
                ins = mm(ps[4][:, 0:E], k16[:, lo:lo + P], diag[:, :, b, :], start=(b == 0), stop=(b == 7))
            ins.then_inc(slot_ps, 1)
            for c in range(6, NC):
                kv_chunk(c)

            def trans_x(t, k, rows_sem, rows_val, r):
                pe.wait_ge(rows_sem, rows_val)
                if not (isinstance(t, int) and t < 2):
                    pe.wait_ge(xlo_sb, t - 1)
                for h in range(NG):
                    ins = nc.tensor.transpose(ps[k % 2][:, h * P:(h + 1) * P], rows[:, r, h * P:(h + 1) * P], ident)
                ins.then_inc(xT_ps, 1)

            def gate_up(t, k, slot, w_sem, w_val):
                pe.wait_ge(w_sem, w_val)
                if not (isinstance(t, int) and t < 2):
                    pe.wait_ge(act_sb, t - 1)
                pe.wait_ge(whi_sb, t + 1)
                pe.wait_ge(xT_sb, t + 1)
                for n, (a, b, ready) in enumerate(((xT, w_hi, None), (xT_lo, w_hi, xlo_sb), (xT, w_lo, wlo_sb))):
                    if ready is not None:
                        pe.wait_ge(ready, t + 1)
                    for h in range(NG):
                        ins = mm(ps[2 + k % 2][:, 0:2 * F], rr(a[:, k % 2, h * P:(h + 1) * P]),
                                 rr(b[:, k % (2 if b is w_lo else 4), h * 2 * F:(h + 1) * 2 * F]),
                                 start=(n == 0 and h == 0), stop=(n == 2 and h == NG - 1))
                ins.then_inc(gu_ps, 1)

            def trans_act(t, k):
                pe.wait_ge(act_sb, t + 1)
                if not (isinstance(t, int) and t < 2):
                    pe.wait_ge(aT_sb, t - 1)
                for h in range(2):
                    ins = nc.tensor.transpose(ps[4 + k % 2][:, h * P:(h + 1) * P],
                                              act[:, k % 2, h * P:(h + 1) * P], ident)
                ins.then_inc(aT_ps, 1)

            def token_list(bank):
                for c in range(NC):
                    ins = mm(bank[:, H:H + 1], ov_hot[:, c, :], k16[:, C16["tokc"][0] + c:C16["tokc"][0] + c + 1],
                             start=(c == 0), stop=(c == NC - 1))
                ins.then_inc(ov_list_ps, 1)

            def down(t, k, slot, listed=None):
                if not (isinstance(t, int) and t < 2):
                    pe.wait_ge(y_sb, t - 1)
                if listed is not None:
                    pe.wait_ge(ov_hot_ready, listed + 1)
                    token_list(ps[6 + k % 2])
                pe.wait_ge(aT_sb, t + 1)
                mm(ps[6 + k % 2][:, 0:H], aT[:, k % 2, 0:P], w1_sb[:, slot, 4 * F:W1C], start=True, stop=False)
                mm(ps[6 + k % 2][:, 0:H], aT[0:F2, k % 2, P:2 * P], w2_sb[0:F2, slot, :],
                   start=False, stop=True).then_inc(y_ps, 1)

            pe.wait_ge(kv_sb, NC)
            pe.wait_ge(gcol_ready, 1)
            trans_x(0, 0, rows_in[0], 16, 0)
            gate_up(0, 0, 0, w_in[0], 32)
            trans_x(1, 1, rows_in[1], 16, 1)

            def expert_pe(i, k, ahead=2, first=False, listed=None):
                t = i * RING + k
                if ahead >= 1:
                    k1 = k + 1
                    gate_up(t + 1, k1, k1 % RING, w_in[k1 % RING], i * 32 + 32 * (k1 // RING + 1))
                if ahead >= 2:
                    k2 = k + 2
                    trans_x(t + 2, k2, rows_in[k2 % AHEAD], i * (16 * (RING // AHEAD)) + 16 * (k2 // AHEAD + 1),
                            k2 % AHEAD)
                trans_act(t, k)
                if not first:
                    down(t - 1, k - 1, (k - 1) % RING, listed)

            for k in range(4):
                expert_pe(0, k, first=(k == 0))
            with pe.Fori(0, E // RING - 1) as i:
                for k in range(4, RING + 4):
                    expert_pe(i, k)
            for k in range(4, RING + EXTRA):
                expert_pe(E // RING - 1, k, ahead=min(2, RING + EXTRA - 1 - k), listed=LISTED.index(k) if k in LISTED else None)
            down(TILES - 1, RING + EXTRA - 1, EXTRA - 1)

            pe.wait_ge(ov_ready, 1)
            n_ov = pe.value_load(ov_n[0:1, 0:1], min_val=0, max_val=E - 1)
            with pe.If(n_ov > 0):
                with pe.Fori(0, n_ov) as j:
                    t = j + TILES
                    pe.wait_ge(y_sb, t)
                    pe.wait_ge(ov_hot_ready, j + (EXTRA + 1))
                    token_list(ps[7])
                    trans_x(t, 0, ov_rows_in, j * 16 + 16, 0)
                    gate_up(t, 0, 0, ov_w_in, j * 32 + 32)
                    trans_act(t, 0)
                    down(t, 0, 0)

            pe.wait_ge(shared_in, 64)
            for m in range(6):
                n, f = m // 3, m % 3
                fw = P if f < 2 else FS - 2 * P
                if m >= 2:
                    pe.wait_ge(sact_sb, m - 1)
                else:
                    pe.wait_ge(y_sb, TILES)
                for o in range(2):
                    for k in range(NG):
                        ins = mm(ps[(m % 2) * 2 + o][0:fw, :], sgu_sb[:, k, o * FS + f * P:o * FS + f * P + fw],
                                 xnT[:, k, n * 512:(n + 1) * 512], start=(k == 0), stop=(k == NG - 1))
                ins.then_inc(sgu_ps, 1)
            pe.wait_ge(kvb_ready, NC)
            pe.wait_ge(y_sb, n_ov + TILES)
            for c in range(NC):
                for g in range(NG):
                    ins = nc.tensor.transpose(ps[4 + 2 * g + c // 4][:, (c % 4) * P:(c % 4 + 1) * P],
                                              kv[:, c, g * P:(g + 1) * P], ident)
                if c % 4 == 3:
                    ins.then_inc(kT_ps, 1)

            def scores(u):
                c, g = u // 2, u % 2
                if u >= 2:
                    pe.wait_ge(p_sb, u - 1)
                else:
                    pe.wait_ge(sact_sb, 6)
                mm(ps[u % 2][:], kT[:, g, c * P:(c + 1) * P], qbd[:, g, c * HG:(c + 1) * HG, :].rearrange("p h i -> p (h i)"),
                   start=True, stop=True).then_inc(s_ps, 1)

            pe.wait_ge(kT_a, 2)
            pe.wait_ge(kT_v, 2)
            pe.wait_ge(qbd_ready, NG * HG)
            pe.wait_ge(qs_ready, NG)
            pe.wait_ge(ks_ready, NC)
            scores(0)
            n_state = 0
            for u in range(2 * NC):
                c, g, m = u // 2, u % 2, (u // 2) % SEQ_CHUNKS
                bank = ps[4 + c % 2]
                if u + 1 < 2 * NC:
                    scores(u + 1)
                if m < SEQ_CHUNKS - 1:
                    n_state += 1
                    if n_state >= 3:
                        pe.wait_ge(st_sb, n_state - 2)
                    mm(ps[6 + n_state % 2][:, 0:P], ks[:, c, g * P:(g + 1) * P], kv[:, c, H + g * P:H + (g + 1) * P],
                       start=True, stop=True).then_inc(st_ps, 1)
                if g == 0:
                    if c >= 2:
                        pe.wait_ge(res_sb, c - 1)
                    for f in range(3):
                        fw = P if f < 2 else FS - 2 * P
                        mm(bank[:, 0:H], sact[0:fw, f, c * P:(c + 1) * P], sdn_sb[0:fw, f, :],
                           start=(f == 0), stop=False)
                if m > 0:
                    pe.wait_ge(st_sb, (c // SEQ_CHUNKS) * 2 * (SEQ_CHUNKS - 1) + 2 * (m - 1) + g + 1)
                    mm(bank[:, g * P:(g + 1) * P], qsT[:, g, c * P:(c + 1) * P], state[:, (m - 1) % 2, g, :],
                       start=False, stop=False)
                pe.wait_ge(p_sb, u + 1)
                for h in range(HG):
                    at = g * P + h * D
                    ins = mm(bank[:, at:at + D], pT[:, u % 2, h * P:(h + 1) * P], kv[:, c, H + at:H + at + D],
                             start=False, stop=(h == HG - 1 and g == 1))
                ins.then_inc(o_ps, 1)


def _constants():
    import numpy as np
    p = np.arange(P)
    betas = np.linspace(np.log2(1.0 / 32.0), np.log2(1.0 / 512.0), HEADS).astype(np.float32)
    g = (np.float32(1.0) - np.exp2(betas).astype(np.float32)).astype(np.float64)
    a = {}
    a["ident"] = np.eye(P)
    a["mask8"] = (p[:, None] % 8 == np.arange(8)[None, :])
    a["padrow"] = (T + 1 + p)[:, None]
    a["iota_e"] = np.tile(np.arange(E), (P, 1))
    a["iota_s"] = np.tile(np.arange(P), (P, 1))
    a["hmask"] = (p[:, None] // D == np.arange(HG)[None, :])
    head = np.arange(NG)[None, :] * HG + p[:, None] // D
    a["gc"] = g[head] ** P
    a["bdmask"] = (p[:, None] // D == p[None, :] // D)
    a["kscale"] = g[np.arange(H)[None, :] // D] ** (P - 1 - p)[:, None]
    a["qscale"] = (g[head][:, :, None] ** (p + 1)[None, None, :]).reshape(P, NG * P)
    diff = p[None, None, :] - p[:, None, None]
    a["decay"] = np.where(diff >= 0, g[None, :, None] ** np.maximum(diff, 0), 0.0).reshape(P, HEADS * P)
    c32 = np.concatenate([np.asarray(a[n], np.float32) for n in C32], 1)
    b = {}
    b["tri"] = (p[:, None] < p[None, :])
    b["ones"] = np.ones((P, P))
    b["place"] = (np.arange(240)[None, :] - 112 == p[:, None] // 8)
    tok = np.arange(NC)[None, :] * P + p[:, None] + 1
    b["tok"] = np.repeat(tok, E, axis=1)
    b["tokc"] = tok
    c16 = np.concatenate([np.asarray(b[n], np.float16) for n in C16], 1)
    return c32, c16


def kernel(**inputs):
    import numpy as np
    import concourse.bacc as bacc
    from concourse.bass_utils import run_bass_kernel_spmd

    v = {n.replace("L0_attn_", "").replace("L0_ffn_", ""): np.asarray(a) for n, a in inputs.items()}

    def halves(w):
        return np.ascontiguousarray(w.reshape(NG, P, -1).transpose(1, 0, 2))

    c32, c16 = _constants()
    gu = v["w_gate_up"].transpose(0, 2, 1).reshape(E, NG, P, 2 * F).transpose(0, 2, 1, 3).reshape(E, P, NG * 2 * F)
    dn = v["w_down"].transpose(0, 2, 1)
    arrays = {
        "x": v["x"].reshape(T, H),
        "wq": halves(v["Wq"]),
        "wkv": halves(np.concatenate([v["Wk"], v["Wv"]], 1)),
        "bq": np.ascontiguousarray(v["bq"].reshape(NG, P).T),
        "bkv": np.concatenate([v["bk"], v["bv"]]),
        "gate": halves(v["gate_w"].T),
        "sgu": halves(v["ws_gate_up"].T),
        "sdn": np.ascontiguousarray(v["ws_down"].T),
        "w1": np.ascontiguousarray(np.concatenate([gu, dn[:, 0:F1, :]], 2)),
        "w2": np.ascontiguousarray(dn[:, F1:F, :]),
        "c32": c32,
        "c16": c16,
    }
    nc = bacc.Bacc("TRN2", target_bir_lowering=False, num_devices=1)
    args = [nc.dram_tensor(f"in_{n}", a.shape, mybir.dt.from_np(a.dtype), kind="ExternalInput").ap()
            for n, a in arrays.items()]
    out = nc.dram_tensor("out", (T, H), mybir.dt.float32, kind="ExternalOutput").ap()
    build(nc, *args, out)
    r = run_bass_kernel_spmd(nc, [{f"in_{n}": a for n, a in arrays.items()}], core_ids=[0])
    return r.results[0]["out"].reshape(2, T // 2, H)
```

```python
from contextlib import ExitStack

import concourse.bass as bass
from concourse import mybir

P = 128
T, H = 1024, 256
NC = T // P
E, TOPK, F = 64, 6, 176
FS = 352
HEADS, D = 8, 32
HG = P // D
NG = H // P
SEQ_CHUNKS = 4
ROW = H + E
EXTRA = 2
TILES = E + EXTRA
RING = 16
TILE_BITS = 7
F1 = P
F2 = F - F1
W1C = 2 * 2 * F + H
ACC_ROWS = T + P
BIG = 3.0e38
UNCHOSEN = 4096.0
SKIP = 4096

C32 = {}
_at = 0
for _n, _w in (("ident", P), ("mask8", 8), ("padrow", 1), ("iota_e", E), ("iota_s", P), ("hmask", HG),
               ("gc", NG), ("bdmask", P), ("kscale", H), ("qscale", NG * P), ("decay", HEADS * P)):
    C32[_n] = (_at, _at + _w)
    _at += _w
C32W = _at
C32_LATE = C32["hmask"][0]
LATE = 4
AHEAD = 8
FIRST_LOADS = 12
WARM_UP = 14
PACE = 3
LOOP_PACE = 2
C16 = {}
_at = 0
for _n, _w in (("tri", P), ("ones", P), ("place", 240), ("tok", NC * E), ("tokc", NC)):
    C16[_n] = (_at, _at + _w)
    _at += _w
C16W = _at


def build(nc, x, wq, wkv, bq, bkv, gate, sgu, sdn, w1, w2, c32, c16, out):
    f32, f16, i32 = mybir.dt.float32, mybir.dt.float16, mybir.dt.int32
    ALU = mybir.AluOpType
    ACT = mybir.ActivationFunctionType
    AX = mybir.AxisListType.X

    table = nc.dram_tensor("table", [T, ROW], f32, kind="Internal").ap()
    acc = [nc.dram_tensor(f"acc{k}", [ACC_ROWS, H], f32, kind="Internal").ap() for k in range(2)]

    with ExitStack() as ctx:
        def sb(name, shape, dt=f32):
            return ctx.enter_context(nc.sbuf_tensor(name, shape, dt))

        def sem(name):
            return ctx.enter_context(nc.semaphore(name))

        k32 = sb("k32", [P, C32W])
        k16 = sb("k16", [P, C16W], f16)

        def c_32(n):
            return k32[:, C32[n][0]:C32[n][1]]

        def c_16(n):
            return k16[:, C16[n][0]:C16[n][1]]

        ident = c_32("ident")

        def slab(name, words):
            return sb(name, [P, words])

        def view(s, at, *dims, dt=f32):
            n = 1
            for d in dims:
                n *= d
            v = s[:, at:at + n * mybir.dt.size(dt) // 4]
            if dt != f32:
                v = v.bitcast(dt)
            names = "abcd"[:len(dims)]
            return v.rearrange(f"p ({' '.join(names)}) -> p {' '.join(names)}", **dict(zip(names, dims)))

        tab_slab = slab("tab_slab", NC * ROW)
        tab = view(tab_slab, 0, NC, ROW)
        x_again = view(tab_slab, 0, NC, H)
        x_slab = slab("x_slab", NC * H)
        x_sb = view(x_slab, 0, NC, H)
        qT = view(x_slab, 0, NG, T)
        xnT = sb("xnT", [P, NG, T])
        stats = sb("stats", [P, NC, 6])
        mv = sb("mv", [P, NC, 2])
        rs = sb("rs", [P, 4, NC])
        gate_sb = sb("gate_sb", [P, NG, E])
        wq_sb = sb("wq_sb", [P, NG, H])
        wkv_sb = sb("wkv_sb", [P, NG, 2 * H])
        bq_sb = sb("bq_sb", [P, NG])
        bkv_sb = sb("bkv_sb", [P, 2 * H])
        sdn_sb = sb("sdn_sb", [P, 3, H])
        LG = NC * (E + 2)
        NE = NC * E
        route = slab("route", 2 * LG + 2 * NE)
        lg = view(route, 0, NC, E + 2)
        lgm = view(route, LG, NC, E + 2)
        ex = view(route, 2 * LG, NC, E)
        exm = view(route, 2 * LG + NE, NC, E)
        rank_i = sb("rank_i", [P, NE], i32)
        digits = slab("digits", AHEAD * ROW)
        qT_lo = view(digits, 0, NG, T)
        lo_i = view(digits, 0, NE, dt=i32)
        hi_i = view(digits, NE, NE, dt=i32)
        lo_h = view(digits, 2 * NE, NE, dt=f16)
        hi_h = view(digits, 2 * NE + NE // 2, NE, dt=f16)
        ov_sel = view(route, NE, NC, E)
        ov_hot = view(route, 2 * NE, NC, P, dt=f16)
        state = view(route, 0, 2, NG, P)
        st_t = view(route, 3 * NE, P)
        rank_f = sb("rank_f", [P, NE])
        top8 = sb("top8", [P, NC, 8])
        neg_max = sb("neg_max", [P, NC])
        sm = sb("sm", [P, 4, NC])
        chosen = sb("chosen", [P, NC, E], f16)
        zero = sb("zero", [P, H])
        silu_try = sb("silu_try", [P, 1])
        diag = sb("diag", [P, 8, 8, 8], f16)
        slot_t = sb("slot_t", [P, 2, E])
        gidx = sb("gidx", [P, TILES], i32)
        sidx = sb("sidx", [P, TILES], i32)
        ov = sb("ov", [P, 4, E])
        ov_one = sb("ov_one", [P, EXTRA, E])
        ov_ones = sb("ov_ones", [P, E])
        ov_i = sb("ov_i", [P, E], i32)
        ov_n = sb("ov_n", [1, 1], i32)
        ov_e = sb("ov_e", [1, EXTRA], i32)
        ov_j = sb("ov_j", [P, 1])
        ov_base = sb("ov_base", [P, 1])
        ov_s = sb("ov_s", [P, 8])
        ov_first = sb("ov_first", [P, EXTRA])
        ov_rank = sb("ov_rank", [P, NC])
        ov_adj = sb("ov_adj", [P, NC])
        ov_idx = sb("ov_idx", [P, 2], i32)
        ov_t = sb("ov_t", [P, 2])
        ov_comb = sb("ov_comb", [P, E])
        with nc.sbuf_tensor("w1_ring", [P, RING * W1C], f32) as ring:
            w1_sb = view(ring, 0, RING, W1C)
        with nc.sbuf_tensor("first_slots", [P, FIRST_LOADS * W1C], f32), \
                nc.sbuf_tensor("xn_hi", [P, NG, T], f32) as xn_hi, nc.sbuf_tensor("xn_lo0", [P, T], f32) as xn_lo0:
            pass
        qsT = sb("qsT", [P, NG, T])
        kT_hi, kT_lo = sb("kT_hi", [P, NG, T]), sb("kT_lo", [P, NG, T])
        sact_hi, sact_lo = sb("sact_hi", [P, 3, T]), sb("sact_lo", [P, 3, T])
        qbd_hi, qbd_lo = sb("qbd_hi", [P, 2, HG, P]), sb("qbd_lo", [P, 2, HG, P])
        sdn_hi = sb("sdn_hi", [P, 3, H])
        slab("end_of_ring", RING * W1C - 3 * NG * T - 6 * T - 4 * HG * P - 3 * H)
        q_round = kT_lo
        with nc.sbuf_tensor("first_w2_slots", [P, FIRST_LOADS * H], f32), \
                nc.sbuf_tensor("wkv_lo", [P, NG, 2 * H], f32) as wkv_lo:
            pass
        w2_slab = slab("w2_slab", RING * H)
        w2_sb = view(w2_slab, 0, RING, H)[0:F2]
        ks = view(w2_slab, 0, NC, H)
        stmp = view(w2_slab, NC * H, 2, 512)
        pT = view(w2_slab, NC * H + 1024, 2, HG * P)
        gcol = sb("gcol", [P, AHEAD], i32)
        scol = sb("scol", [P, 8], i32)
        rows = view(digits, 0, AHEAD, ROW)
        xT_both = sb("xT_both", [P, 4, H])
        xT, xT_lo = xT_both[:, 0:2, :], xT_both[:, 2:4, :]
        wkv_hi = xT_both.rearrange("p (k a) h -> p k (a h)", k=NG)
        sdn_lo = xT_both[:, 0:3, :]
        sg = sb("sg", [P, 2, F])
        act = sb("act", [P, 2, 2 * P])
        aT = sb("aT", [P, 2, 2 * P])
        with nc.sbuf_tensor("xn_lo1", [P, T], f32) as xn_lo1:
            xn_lo = (xn_lo0, xn_lo1)
        y = sb("y", [P, 4, H])
        sprod = y.rearrange("p (a b) h -> p a (b h)", a=2)
        kv = sb("kv", [P, NC, 2 * H])


        with nc.sbuf_tensor("one_hots", [P, 24 * NE // 2], f32) as hots:
            lo_hot = view(hots, 0, NC * 8, 16, 8, dt=f16)
            hi_hot = view(hots, 16 * NE // 2, 8, NC, E, dt=f16)
        with nc.sbuf_tensor("routed_sums", [P, 2 * NC * H], f32) as sums:
            acc_sb = [view(sums, 0, NC, H), view(sums, NC * H, NC, H)]
        w_split = slab("w_split", 6 * 4 * F)
        w_hi = view(w_split, 0, 4, 4 * F)
        w_lo = view(w_split, 4 * 4 * F, 2, 4 * F)
        sgu_sb = sb("sgu_sb", [P, NG, 2 * FS])
        res = sb("res", [P, 2, H])

        ps = [ctx.enter_context(nc.psum_tensor(f"ps{b}", [P, 512], f32)) for b in range(8)]

        x_in = [sem(f"x_in{n}") for n in range(4)]
        ident_in = sem("ident_in")
        c16_in = sem("c16_in")
        c32_in = sem("c32_in")
        gate_in = sem("gate_in")
        wq_in = sem("wq_in")
        wkv_in = sem("wkv_in")
        bias_in = sem("bias_in")
        shared_in = sem("shared_in")
        w_in = [sem(f"w_in{s}") for s in range(RING)]
        dve_step = sem("dve_step")
        pool_step = sem("pool_step")
        var_ready, std_ready = sem("var_ready"), sem("std_ready")
        xn_ready = sem("xn_ready")
        xnT_ps, xnT_a, xnT_v = sem("xnT_ps"), sem("xnT_a"), sem("xnT_v")
        logits_ps = sem("logits_ps")
        shifted_ready, ex_ready = sem("shifted_ready"), sem("ex_ready")
        comb_ready, table_out = sem("comb_ready"), sem("table_out")
        exm_ready, sums_ready, share_ready = sem("exm_ready"), sem("sums_ready"), sem("share_ready")
        chosen_ready, rank_ps = sem("chosen_ready"), sem("rank_ps")
        hot_ready, diag_ps, diag_ready, slot_ps = sem("hot_ready"), sem("diag_ps"), sem("diag_ready"), sem("slot_ps")
        digits_ready, counts_read = sem("digits_ready"), sem("counts_read")
        ov_ready = sem("ov_ready")
        zero_ready = sem("zero_ready")
        xhi_ready, wkv_hi_ready, xlo_ready, wkv_lo_ready = (
            sem("xhi_ready"), sem("wkv_hi_ready"), sem("xlo_ready"), sem("wkv_lo_ready"))
        q_ps, q_sb = sem("q_ps"), sem("q_sb")
        kv_ps, kv_sb = sem("kv_ps"), sem("kv_sb")
        rows_in = [sem(f"rows_in{r}") for r in range(AHEAD)]
        gcol_ready, scol_ready = sem("gcol_ready"), sem("scol_ready")
        xT_ps, xT_sb, xlo_sb = sem("xT_ps"), sem("xT_sb"), sem("xlo_sb")
        whi_sb, wlo_sb = sem("whi_sb"), sem("wlo_sb")
        gu_ps, sg_sb, act_sb = sem("gu_ps"), sem("sg_sb"), sem("act_sb")
        aT_ps, aT_sb = sem("aT_ps"), sem("aT_sb")
        y_ps, y_sb = sem("y_ps"), sem("y_sb")
        acc_done = [sem("acc_done0"), sem("acc_done1")]
        act_zero, silu_zero = sem("act_zero"), sem("silu_zero")
        ov_hot_ready, ov_list_ps, ov_idx_ready, ov_expert_ready = (
            sem("ov_hot_ready"), sem("ov_list_ps"), sem("ov_idx_ready"), sem("ov_expert_ready"))
        ov_rows_in, ov_w_in = sem("ov_rows_in"), sem("ov_w_in")
        late_in = sem("late_in")
        acc_in, x_again_in = sem("acc_in"), sem("x_again_in")
        sgu_ps, stmp_sb = sem("sgu_ps"), sem("stmp_sb")
        kvb_ready, qs_ready, ks_ready = sem("kvb_ready"), sem("qs_ready"), sem("ks_ready")
        prod_sb, shi_sb, slo_sb = sem("prod_sb"), sem("shi_sb"), sem("slo_sb")
        q_rounded, q_low, sdn_hi_ready, sdn_lo_ready = (
            sem("q_rounded"), sem("q_low"), sem("sdn_hi_ready"), sem("sdn_lo_ready"))
        qhi_sb, qlo_sb = sem("qhi_sb"), sem("qlo_sb")
        kT_ps, kT_a, kT_v = sem("kT_ps"), sem("kT_a"), sem("kT_v")
        s_ps, p_sb = sem("s_ps"), sem("p_sb")
        o_ps, st_ps, st_sb = sem("o_ps"), sem("st_ps"), sem("st_sb")
        xab_ready, res_sb = sem("xab_ready"), sem("res_sb")
        out_done = [sem("out_done0"), sem("out_done1")]
        sp_waited, pool_waited = sem("sp_waited"), sem("pool_waited")

        x_v = x.rearrange("(c p) h -> p c h", p=P)
        out_v = out.rearrange("(c p) h -> p c h", p=P)
        table_v = table.rearrange("(c p) h -> p c h", p=P)
        acc_v = [a.rearrange("(c p) h -> p c h", p=P) for a in acc]

        def rr(ap):
            return ap.bitcast(mybir.dt.float32r)

        def bc(ap, shape):
            return ap.unsqueeze(2).to_broadcast(shape)

        ov_steps = sem("ov_steps")
        LO_POOL = 3
        LISTED = (8, 12)

        def fetched_at(k):
            if k < RING - AHEAD:
                return k
            return k - LATE if RING - AHEAD <= k - LATE < RING + EXTRA - AHEAD else None

        block = ctx.enter_context(nc.Block())

        @block.sync
        def _(sp):
            for n in range(4):
                sp.dma_start(x_sb[:, 2 * n:2 * n + 2, :], x_v[:, 2 * n:2 * n + 2, :]).then_inc(x_in[n], 16)
            sp.dma_start(k32[:, 0:P], c32[:, 0:P]).then_inc(ident_in, 16)
            sp.dma_start(gate_sb[:], gate).then_inc(gate_in, 16)
            sp.dma_start(wq_sb[:], wq).then_inc(wq_in, 16)
            sp.dma_start(bq_sb[:], bq).then_inc(bias_in, 16)
            sp.dma_start(bkv_sb[:], bkv.partition_broadcast(P)).then_inc(bias_in, 16)
            sp.dma_start(k16[:], c16).then_inc(c16_in, 16)
            sp.dma_start(wkv_sb[:], wkv).then_inc(wkv_in, 16)
            sp.dma_start(k32[:, P:C32_LATE], c32[:, P:C32_LATE]).then_inc(c32_in, 16)

            def load_expert(slot, e):
                sp.dma_start(w1_sb[:, slot, :], w1[e, :, :]).then_inc(w_in[slot], 16)
                sp.dma_start(w2_sb[:, slot, :], w2[e, :, :]).then_inc(w_in[slot], 16)

            for s in range(RING):
                if s == FIRST_LOADS:
                    sp.wait_ge(rows_in[1], 16)
                    sp.wait_ge(kv_ps, NC)
                if s >= PACE:
                    sp.wait_ge(w_in[s - PACE], 32)
                load_expert(s, s)
            with sp.Fori(0, E // RING - 1) as i:
                for s in range(RING):
                    sp.wait_ge(y_ps, i * RING + (s + 1))
                    sp.sem_inc(sp_waited, 1)
                    sp.wait_ge(w_in[(s - LOOP_PACE) % RING], i * 32 + (64 if s >= LOOP_PACE else 32))
                    e = i * RING + (RING + s)
                    sp.dma_start(w1_sb[:, s, :], w1[bass.ds(e, 1), :, :].rearrange("a p c -> p (a c)"))\
                        .then_inc(w_in[s], 16)
                    sp.dma_start(w2_sb[:, s, :], w2[bass.ds(e, 1), :, :].rearrange("a p c -> p (a c)"))\
                        .then_inc(w_in[s], 16)
            for j in range(EXTRA):
                sp.wait_ge(y_ps, E - RING + j + 1)
                sp.wait_ge(ov_expert_ready, j + 1)
                e = sp.value_load(ov_e[0:1, j:j + 1], min_val=0, max_val=E - 1)
                sp.dma_start(w1_sb[:, j, :], w1[bass.ds(e, 1), :, :].rearrange("a p c -> p (a c)"))\
                    .then_inc(w_in[j], 16)
                sp.dma_start(w2_sb[:, j, :], w2[bass.ds(e, 1), :, :].rearrange("a p c -> p (a c)"))\
                    .then_inc(w_in[j], 16)
            late = [(sdn_sb[:, 0:2, :], sdn[0:2 * P, :].rearrange("(c p) h -> p c h", p=P), shared_in),
                    (sdn_sb[0:FS - 2 * P, 2, :], sdn[2 * P:FS, :], shared_in)]
            late += [(sgu_sb[:, n, :], sgu[:, n, :], shared_in) for n in range(NG)]
            half = (C32_LATE + C32W) // 2
            late += [(k32[:, lo:hi], c32[:, lo:hi], late_in) for lo, hi in ((C32_LATE, half), (half, C32W))]
            late += [(x_again[:, 4 * n:4 * n + 4, :], x_v[:, 4 * n:4 * n + 4, :], x_again_in) for n in range(2)]
            for n, (dst, src, done) in enumerate(late):
                sp.wait_ge(y_ps, E - RING + EXTRA + n + 1)
                sp.dma_start(dst, src).then_inc(done, 16)
            sp.wait_ge(ov_ready, 1)
            n_ov = sp.value_load(ov_n[0:1, 0:1], min_val=0, max_val=E - 1)
            with sp.If(n_ov > 0):
                with sp.Fori(0, n_ov) as j:
                    sp.wait_ge(y_ps, j + TILES)
                    sp.sem_inc(sp_waited, 1)
                    sp.wait_ge(ov_expert_ready, j + (EXTRA + 1))
                    sp.sem_inc(sp_waited, 1)
                    e = sp.value_load(ov_e[0:1, 0:1], min_val=0, max_val=E - 1)
                    sp.dma_start(w1_sb[:, 0, :], w1[bass.ds(e, 1), :, :].rearrange("a p c -> p (a c)"))\
                        .then_inc(ov_w_in, 16)
                    sp.dma_start(w2_sb[:, 0, :], w2[bass.ds(e, 1), :, :].rearrange("a p c -> p (a c)"))\
                        .then_inc(ov_w_in, 16)

            sp.wait_ge(acc_done[0], n_ov * 16 + 16 * (TILES // 2 + 1))
            sp.wait_ge(acc_done[1], 16 * (TILES // 2 + 1))
            for k in range(2):
                sp.dma_start(acc_sb[k], acc_v[k][:, 0:NC, :]).then_inc(acc_in, 16)
            for c in range(NC):
                sp.wait_ge(res_sb, c + 1)
                sp.dma_start(out_v[:, c, :], res[:, c % 2, :]).then_inc(out_done[c % 2], 16)
            for k in range(2):
                sp.wait_ge(out_done[k], 16 * (NC // 2))

        @block.gpsimd
        def _(pool):
            nc.gpsimd.memset(zero[:], 0.0).then_inc(zero_ready, 1)
            nc.gpsimd.memset(silu_try[:], 0.0).then_inc(silu_zero, 1)
            nc.gpsimd.memset(act[:], 0.0).then_inc(act_zero, 1)
            pool.wait_ge(xn_ready, NC)
            pool.dma_start(table_v[:, :, 0:H], tab[:, :, 0:H]).then_inc(table_out, 16)
            pool.wait_ge(zero_ready, 1)
            for k in range(2):
                pool.dma_start(acc_v[k], zero[:].unsqueeze(1).to_broadcast([P, ACC_ROWS // P, H]))\
                    .then_inc(acc_done[k], 16)
            G = nc.gpsimd
            for k in range(NG):
                pool.wait_ge(xhi_ready, k + 1)
                G.tensor_tensor(rr(xn_lo[k][:]), xnT[:, k, :], xn_hi[:, k, :], ALU.subtract).then_inc(xlo_ready, 1)
            pool.wait_ge(wkv_hi_ready, 1)
            G.tensor_tensor(rr(wkv_lo[:]), wkv_sb[:], wkv_hi, ALU.subtract).then_inc(wkv_lo_ready, 1)
            pool.wait_ge(chosen_ready, 1)
            pool.wait_ge(ex_ready, NC)
            G.tensor_tensor(exm[:], ex[:], chosen[:], ALU.mult).then_inc(exm_ready, 1)
            pool.wait_ge(digits_ready, 1)
            for a in range(16 - LO_POOL, 16):
                ins = nc.gpsimd.tensor_scalar(lo_hot[:, :, a, :], lo_h.rearrange("p (n e) -> p n e", e=8), float(a),
                                              None, ALU.is_equal)
            ins.then_inc(hot_ready, 1)
            pool.wait_ge(share_ready, 1)
            pool.wait_ge(exm_ready, 1)
            G.tensor_tensor(tab[:, :, H:ROW], exm[:], bc(sm[:, 3, :], [P, NC, E]), ALU.mult).then_inc(comb_ready, 1)
            pool.wait_ge(comb_ready, 1)
            pool.dma_start(table_v[:, :, H:ROW], tab[:, :, H:ROW]).then_inc(table_out, 16)
            pool.wait_ge(hot_ready, 2)
            nc.gpsimd.memset(rows[:], 0.0).then_inc(zero_ready, 1)
            pool.wait_ge(zero_ready, 2)
            pool.wait_ge(table_out, 32)

            def gather(r):
                pool.indirect_dma_start(
                    out=rows[:, r, :], out_offset=None, in_=table,
                    in_offset=bass.IndirectOffsetOnAxis(ap=gcol[:, r:r + 1], axis=0),
                    bounds_check=T - 1, oob_is_err=False).then_inc(rows_in[r], 16)

            def scatter(k):
                pool.indirect_dma_start(
                    out=acc[k % 2], out_offset=bass.IndirectOffsetOnAxis(ap=scol[:, k % 8:k % 8 + 1], axis=0),
                    in_=y[:, k % 4, :], in_offset=None, compute_op=ALU.add).then_inc(acc_done[k % 2], 16)

            pool.wait_ge(gcol_ready, 1)
            for r in range(AHEAD):
                gather(r)
            def fetch(t, k):
                pool.wait_ge(gcol_ready, t + 2)
                pool.sem_inc(pool_waited, 1)
                gather(k % AHEAD)

            def store(t, k):
                pool.wait_ge(y_sb, t + 1)
                pool.wait_ge(scol_ready, t + 1)
                pool.wait_ge(acc_done[k % 2], (t - k) * 8 + 16 * (k // 2 + 1))
                pool.sem_inc(pool_waited, 1)
                scatter(k)

            fetch(0, 0)
            with pool.Fori(0, E // RING - 1) as i:
                for k in range(1, RING + 1):
                    fetch(i * RING + k, k)
                    store(i * RING + (k - 1), k - 1)
            for k in range(1, RING + EXTRA + 1):
                if fetched_at(k) is not None:
                    fetch(E - RING + fetched_at(k), fetched_at(k))
                store(E - RING + k - 1, k - 1)

            pool.wait_ge(ov_ready, 1)
            n_ov = pool.value_load(ov_n[0:1, 0:1], min_val=0, max_val=E - 1)
            with pool.If(n_ov > 0):
                with pool.Fori(0, n_ov) as j:
                    pool.wait_ge(ov_idx_ready, j + 1)
                    pool.sem_inc(pool_waited, 1)
                    pool.indirect_dma_start(
                        out=rows[:, 0, :], out_offset=None, in_=table,
                        in_offset=bass.IndirectOffsetOnAxis(ap=ov_idx[:, 0:1], axis=0),
                        bounds_check=T - 1, oob_is_err=False).then_inc(ov_rows_in, 16)
                    pool.wait_ge(y_sb, j + (TILES + 1))
                    pool.wait_ge(acc_done[0], j * 16 + 16 * (TILES // 2 + 1))
                    pool.sem_inc(pool_waited, 1)
                    pool.indirect_dma_start(
                        out=acc[0], out_offset=bass.IndirectOffsetOnAxis(ap=ov_idx[:, 1:2], axis=0),
                        in_=y[:, 0, :], in_offset=None, compute_op=ALU.add).then_inc(acc_done[0], 16)
            pool.wait_ge(y_ps, n_ov + TILES)
            pool.sem_inc(pool_waited, 1)
            pool.wait_ge(q_rounded, 1)
            for g in range(NG):
                ins = G.tensor_tensor(qT_lo[:, g, :], qT[:, g, :], q_round[:, g, :], ALU.subtract)
                ins.then_inc(q_low, 1)
            pool.wait_ge(sdn_hi_ready, 2)
            G.tensor_tensor(rr(sdn_lo[:, 0:2, :]), sdn_sb[:, 0:2, :], sdn_hi[:, 0:2, :], ALU.subtract)\
                .then_inc(sdn_lo_ready, 1)
            last = FS - 2 * P
            G.tensor_tensor(rr(sdn_lo[0:last, 2, :]), sdn_sb[0:last, 2, :], sdn_hi[0:last, 2, :], ALU.subtract)\
                .then_inc(sdn_lo_ready, 1)
            pool.wait_ge(late_in, 32)
            pool.wait_ge(q_low, NG)

            def q_low_heads(u):
                c, g = u // 2, u % 2
                if u >= 2:
                    pool.wait_ge(s_ps, u - 1)
                G.tensor_tensor(rr(qbd_lo[:, u % 2, :, :]),
                                qT_lo[:, g, c * P:(c + 1) * P].unsqueeze(1).to_broadcast([P, HG, P]),
                                bc(c_32("hmask"), [P, HG, P]), ALU.mult).then_inc(qlo_sb, 1)

            def low_product(n):
                rows_n = P if n % 3 < 2 else last
                cols = slice((n // 3) * 512, (n // 3 + 1) * 512)
                pool.wait_ge(shi_sb, n + 1)
                G.tensor_tensor(rr(sact_lo[0:rows_n, n % 3, cols]), sprod[0:rows_n, n % 2, :],
                                sact_hi[0:rows_n, n % 3, cols], ALU.subtract).then_inc(slo_sb, 1)

            for n in range(5):
                low_product(n)
                if n in (1, 2):
                    q_low_heads(n - 1)
            for c in range(NC):
                if c < NC - 1:
                    q_low_heads(2 * c + 2)
                    q_low_heads(2 * c + 3)
                if c == 0:
                    low_product(5)
                    pool.wait_ge(acc_in, 32)
                    pool.wait_ge(x_again_in, 32)
                G.tensor_tensor(acc_sb[1][:, c, :], acc_sb[1][:, c, :], acc_sb[0][:, c, :], ALU.add)\
                    .then_inc(pool_step, 1)
                pool.wait_ge(pool_step, c + 1)
                G.tensor_tensor(acc_sb[1][:, c, :], acc_sb[1][:, c, :], x_again[:, c, :], ALU.add)\
                    .then_inc(xab_ready, 1)

        @block.scalar
        def _(act_e):
            act_e.wait_ge(var_ready, 1)
            nc.scalar.activation(rs[:, 1, :], rs[:, 0, :], ACT.Sqrt).then_inc(std_ready, 1)
            for n in range(2):
                act_e.wait_ge(xnT_ps, n + 1)
                nc.scalar.copy(xnT[:, 0, n * 512:(n + 1) * 512], ps[n][:]).then_inc(xnT_a, 1)
            for k, ready in enumerate((xnT_a, xnT_v)):
                act_e.wait_ge(ready, 2)
                nc.scalar.copy(rr(xn_hi[:, k, :]), xnT[:, k, :]).then_inc(xhi_ready, 1)
            act_e.wait_ge(wkv_in, 16)
            nc.scalar.copy(rr(wkv_hi), wkv_sb[:]).then_inc(wkv_hi_ready, 1)
            act_e.wait_ge(shifted_ready, 1)
            for c in range(NC):
                nc.scalar.activation(ex[:, c, :], lg[:, c, 0:E], ACT.Exp, bias=neg_max[:, c:c + 1],
                                     accum_out=sm[:, 0, c:c + 1]).then_inc(ex_ready, 1)
            act_e.wait_ge(bias_in, 32)
            for n in range(4):
                if n == 2:
                    act_e.wait_ge(exm_ready, 1)
                    for c in range(NC):
                        nc.scalar.activation(lgm[:, c, 0:E], exm[:, c, :], ACT.Identity,
                                             accum_out=sm[:, 1, c:c + 1]).then_inc(sums_ready, 1)
                act_e.wait_ge(q_ps, n + 1)
                nc.scalar.activation(qT[:, n // 2, (n % 2) * 512:(n % 2 + 1) * 512], ps[n % 2][:], ACT.Identity,
                                     bias=bq_sb[:, n // 2:n // 2 + 1]).then_inc(q_sb, 1)
            act_e.wait_ge(silu_zero, 1)
            nc.scalar.activation(silu_try[:], silu_try[:], ACT.Silu)
            def split_w(i, k):
                t = i * RING + k
                act_e.wait_ge(w_in[k % RING], i * 32 + 32 * (k // RING + 1))
                if not (isinstance(t, int) and t < 4):
                    act_e.wait_ge(gu_ps, t - 3)
                nc.scalar.copy(rr(w_hi[:, k % 4, :]), w1_sb[:, k % RING, 0:4 * F]).then_inc(whi_sb, 1)

            def evac_xT(t, k):
                act_e.wait_ge(xT_ps, t + 1)
                if not (isinstance(t, int) and t < 2):
                    act_e.wait_ge(gu_ps, t - 1)
                nc.scalar.copy(rr(xT[:, k % 2, :]), ps[k % 2][:, 0:H]).then_inc(xT_sb, 1)

            def silu(t, k):
                act_e.wait_ge(gu_ps, t + 1)
                if not (isinstance(t, int) and t < 2):
                    act_e.wait_ge(act_sb, t - 1)
                nc.scalar.activation(sg[:, k % 2, :], ps[2 + k % 2][:, 0:F], ACT.Silu).then_inc(sg_sb, 1)

            def evac_aT(t, k):
                act_e.wait_ge(aT_ps, t + 1)
                if not (isinstance(t, int) and t < 2):
                    act_e.wait_ge(y_ps, t - 1)
                nc.scalar.copy(aT[:, k % 2, :], ps[4 + k % 2][:, 0:2 * P]).then_inc(aT_sb, 1)

            def evac_y(t, k, first):
                act_e.wait_ge(y_ps, t + 1)
                if not first:
                    act_e.wait_ge(acc_done[k % 2], (t - k) * 8 + 16 * (k // 2))
                nc.scalar.copy(y[:, k % 4, :], ps[6 + k % 2][:, 0:H]).then_inc(y_sb, 1)

            for c in range(NC):
                act_e.wait_ge(kv_ps, c + 1)
                nc.scalar.copy(kv[:, c, :], ps[c % 4][:]).then_inc(kv_sb, 1)
                if c == NC - 3:
                    act_e.wait_ge(diag_ps, 1)
                if c >= NC - 3 and c < NC - 1:
                    split_w(0, c - (NC - 3))
            evac_xT(0, 0)
            split_w(0, 2)
            silu(0, 0)
            evac_xT(1, 1)

            def expert_act(i, k, ahead=3):
                t = i * RING + k
                if not (isinstance(t, int) and t < 2):
                    evac_y(t - 2, k - 2, isinstance(t, int) and t < 6)
                if ahead >= 3:
                    split_w(i, k + 3)
                if ahead >= 1:
                    silu(t + 1, k + 1)
                if ahead >= 2:
                    evac_xT(t + 2, k)
                evac_aT(t, k)

            for k in range(6):
                expert_act(0, k)
            with act_e.Fori(0, E // RING - 1) as i:
                for k in range(6, RING + 6):
                    expert_act(i, k)
            for k in range(6, RING + EXTRA):
                expert_act(E // RING - 1, k, ahead=min(3, RING + EXTRA - 1 - k))
            for k in range(RING + EXTRA - 2, RING + EXTRA):
                evac_y(E - RING + k, k, False)

            act_e.wait_ge(ov_ready, 1)
            n_ov = act_e.value_load(ov_n[0:1, 0:1], min_val=0, max_val=E - 1)
            with act_e.If(n_ov > 0):
                with act_e.Fori(0, n_ov) as j:
                    act_e.wait_ge(ov_w_in, j * 32 + 32)
                    nc.scalar.copy(rr(w_hi[:, 0, :]), w1_sb[:, 0, 0:4 * F]).then_inc(whi_sb, 1)
                    act_e.wait_ge(xT_ps, j + (TILES + 1))
                    nc.scalar.copy(rr(xT[:, 0, :]), ps[0][:, 0:H]).then_inc(xT_sb, 1)
                    act_e.wait_ge(gu_ps, j + (TILES + 1))
                    nc.scalar.activation(sg[:, 0, :], ps[2][:, 0:F], ACT.Silu).then_inc(sg_sb, 1)
                    act_e.wait_ge(aT_ps, j + (TILES + 1))
                    nc.scalar.copy(aT[:, 0, :], ps[4][:, 0:2 * P]).then_inc(aT_sb, 1)
                    act_e.wait_ge(y_ps, j + (TILES + 1))
                    act_e.wait_ge(acc_done[0], j * 16 + 16 * (TILES // 2 + 1))
                    nc.scalar.copy(y[:, 0, :], ps[6][:, 0:H]).then_inc(y_sb, 1)

            act_e.wait_ge(y_ps, n_ov + TILES)
            nc.scalar.copy(rr(q_round[:]), qT[:]).then_inc(q_rounded, 1)
            act_e.wait_ge(shared_in, 64)
            last = FS - 2 * P
            nc.scalar.copy(rr(sdn_hi[:, 0:2, :]), sdn_sb[:, 0:2, :]).then_inc(sdn_hi_ready, 1)
            nc.scalar.copy(rr(sdn_hi[0:last, 2, :]), sdn_sb[0:last, 2, :]).then_inc(sdn_hi_ready, 1)

            def high_product(n):
                rows_n = P if n % 3 < 2 else last
                act_e.wait_ge(prod_sb, n + 1)
                nc.scalar.copy(rr(sact_hi[0:rows_n, n % 3, (n // 3) * 512:(n // 3 + 1) * 512]),
                               sprod[0:rows_n, n % 2, :]).then_inc(shi_sb, 1)

            def q_high_heads(u):
                c, g = u // 2, u % 2
                if u >= 2:
                    act_e.wait_ge(s_ps, u - 1)
                for h in range(HG):
                    ins = nc.scalar.activation(rr(qbd_hi[:, u % 2, h, :]), qT[:, g, c * P:(c + 1) * P], ACT.Identity,
                                               scale=c_32("hmask")[:, h:h + 1])
                ins.then_inc(qhi_sb, 1)

            act_e.wait_ge(late_in, 32)
            for n in range(6):
                act_e.wait_ge(sgu_ps, n + 1)
                if n >= 2:
                    act_e.wait_ge(prod_sb, n - 1)
                rows_n = P if n % 3 < 2 else last
                nc.scalar.activation(stmp[0:rows_n, n % 2, :], ps[(n % 2) * 2][0:rows_n, :], ACT.Silu)\
                    .then_inc(stmp_sb, 1)
                if n >= 1:
                    high_product(n - 1)
                if n in (1, 2):
                    q_high_heads(n - 1)
                if n in (3, 4):
                    half = n - 3
                    act_e.wait_ge(kT_ps, half + 1)
                    for g in range(NG):
                        nc.scalar.copy(rr(kT_hi[:, g, half * 512:(half + 1) * 512]), ps[4 + 2 * g + half][:])\
                            .then_inc(kT_a, 1)
            for u in range(2, 2 * NC):
                q_high_heads(u)
                if u == 2:
                    high_product(5)

        @block.vector
        def _(dve):
            step = [0]

            def link(ins):
                step[0] += 1
                ins.then_inc(dve_step, 1)
                dve.wait_ge(dve_step, step[0])

            V = nc.vector
            for c in range(NC):
                if c % 2 == 0:
                    dve.wait_ge(x_in[c // 2], 16)
                ins = V.bn_stats(stats[:, c, :], x_sb[:, c, :])
            link(ins)
            for c in range(NC):
                ins = V.bn_aggr(mv[:, c, :], stats[:, c, :])
            link(ins)
            V.tensor_scalar(rs[:, 0, :], mv[:, :, 1], 1e-5, None, ALU.add).then_inc(var_ready, 1)
            dve.wait_ge(std_ready, 1)
            link(V.reciprocal(rs[:, 2, :], rs[:, 1, :]))
            link(V.tensor_tensor(rs[:, 3, :], rs[:, 2, :], rs[:, 2, :], ALU.mult))
            link(V.scalar_tensor_tensor(rs[:, 3, :], rs[:, 3, :], -0.5, rs[:, 0, :], ALU.mult, ALU.mult))
            link(V.scalar_tensor_tensor(rs[:, 2, :], rs[:, 3, :], 1.5, rs[:, 2, :], ALU.add, ALU.mult))
            for c in range(NC):
                V.tensor_scalar(tab[:, c, 0:H], x_sb[:, c, :], mv[:, c, 0:1], rs[:, 2, c:c + 1],
                                ALU.subtract, ALU.mult).then_inc(xn_ready, 1)
            V.memset(lg[:, :, E:E + 2], BIG)
            V.memset(ov_ones[:], 1.0)
            V.memset(ov_j[:], 0.0)
            V.memset(ov_base[:], P - UNCHOSEN)
            for n in range(2):
                dve.wait_ge(xnT_ps, n + 1)
                V.tensor_copy(xnT[:, 1, n * 512:(n + 1) * 512], ps[2 + n][:]).then_inc(xnT_v, 1)

            dve.wait_ge(logits_ps, 1)
            link(V.tensor_copy(lg[:, :, 0:E], ps[4][:].rearrange("p (c e) -> p c e", e=E)))
            for c in range(NC):
                ins = V.max(top8[:, c, :], lg[:, c, 0:E])
            link(ins)
            link(V.tensor_scalar(neg_max[:], top8[:, :, 0], -1.0, None, ALU.mult))
            V.memset(top8[:, :, TOPK:8], BIG).then_inc(shifted_ready, 1)
            dve.wait_ge(shifted_ready, 1)
            for c in range(NC):
                ins = V.match_replace(lgm[:, c, :], top8[:, c, :], lg[:, c, :], -BIG)
            link(ins)
            V.tensor_tensor(chosen[:], lg[:, :, 0:E], lgm[:, :, 0:E], ALU.not_equal).then_inc(chosen_ready, 1)
            dve.wait_ge(chosen_ready, 1)
            dve.wait_ge(rank_ps, 1)
            link(V.scalar_tensor_tensor(rank_i[:], chosen[:].rearrange("p c e -> p (c e)"), -UNCHOSEN, ps[5][:],
                                        ALU.mult, ALU.add))
            V.tensor_scalar(lo_i[:], rank_i[:], 15, None, ALU.bitwise_and)
            link(V.tensor_scalar(hi_i[:], rank_i[:], 4, None, ALU.arith_shift_right))
            V.tensor_copy(lo_h[:], lo_i[:])
            V.tensor_copy(hi_h[:], hi_i[:]).then_inc(digits_ready, 1)
            dve.wait_ge(digits_ready, 1)
            dve.wait_ge(c16_in, 16)
            for b in range(8):
                V.scalar_tensor_tensor(hi_hot[:, b, :, :].rearrange("p c e -> p (c e)"), hi_h[:],
                                       float(b) - UNCHOSEN / 16, c_16("tok"), ALU.is_equal, ALU.mult)
            dve.wait_ge(sums_ready, NC)
            link(V.reciprocal(sm[:, 2, :], sm[:, 0, :]))
            link(V.tensor_tensor(sm[:, 1, :], sm[:, 1, :], sm[:, 2, :], ALU.mult))
            link(V.tensor_scalar(sm[:, 1, :], sm[:, 1, :], 1e-20, None, ALU.add))
            link(V.reciprocal(sm[:, 3, :], sm[:, 1, :]))
            V.tensor_tensor(sm[:, 3, :], sm[:, 3, :], sm[:, 2, :], ALU.mult).then_inc(share_ready, 1)
            for a in range(16 - LO_POOL):
                ins = V.tensor_scalar(lo_hot[:, :, a, :], lo_h.rearrange("p (n e) -> p n e", e=8), float(a), None,
                                      ALU.is_equal)
            ins.then_inc(hot_ready, 1)
            dve.wait_ge(c32_in, 16)
            dve.wait_ge(diag_ps, 1)
            V.tensor_tensor(diag[:].rearrange("p g b e -> p (g b) e"), ps[7][:].rearrange("p (gb e) -> p gb e", e=8),
                            c_32("mask8").unsqueeze(1).to_broadcast([P, 64, 8]), ALU.mult).then_inc(diag_ready, 1)
            dve.wait_ge(slot_ps, 1)

            def indices(lst, tmp, g_out, s_out):
                V.tensor_scalar(tmp[0], lst, 0.0, float(SKIP + 1), ALU.is_equal, ALU.mult)
                link(V.tensor_scalar(tmp[1], lst, 0.0, c_32("padrow"), ALU.is_equal, ALU.mult))
                V.scalar_tensor_tensor(g_out, lst, -1.0, tmp[0], ALU.add, ALU.add)
                return V.scalar_tensor_tensor(s_out, lst, -1.0, tmp[1], ALU.add, ALU.add)

            link(indices(ps[4][:, 0:E], (slot_t[:, 0, :], slot_t[:, 1, :]), gidx[:, 0:E], sidx[:, 0:E]))
            V.tensor_copy(gcol[:], gidx[:, 0:AHEAD]).then_inc(gcol_ready, 1)

            V.tensor_copy(rank_f[:], rank_i[:])
            dve.wait_ge(rank_ps, 2)
            link(V.tensor_scalar(ov_i[:], ps[6][:, 0:E], -1.0, 0.0, ALU.add, ALU.max))
            link(V.tensor_scalar(ov_i[:], ov_i[:], TILE_BITS, None, ALU.arith_shift_right))
            link(V.tensor_copy(ov[:, 0, :], ov_i[:]))
            link(V.tensor_tensor_scan(ov[:, 1, :], ov_ones[:], ov[:, 0, :], 0.0, ALU.mult, ALU.add))
            V.tensor_scalar(ov_n[:], ov[0:1, 1, E - 1:E], float(-EXTRA), 0.0, ALU.add, ALU.max).then_inc(ov_ready, 1)
            V.tensor_tensor(ov[:, 2, :], ov[:, 1, :], ov[:, 0, :], ALU.subtract).then_inc(counts_read, 1)
            dve.wait_ge(counts_read, 1)

            def gate_up(t, k, comb):
                dve.wait_ge(sg_sb, t + 1)
                if not (isinstance(t, int) and t < 2):
                    dve.wait_ge(aT_ps, t - 1)
                V.scalar_tensor_tensor(act[:, k % 2, 0:F], ps[2 + k % 2][:, F:2 * F], comb, sg[:, k % 2, :],
                                       ALU.mult, ALU.mult).then_inc(act_sb, 1)

            def w_low(t, k):
                dve.wait_ge(whi_sb, t + 1)
                if not (isinstance(t, int) and t < 2):
                    dve.wait_ge(gu_ps, t - 1)
                V.tensor_tensor(rr(w_lo[:, k % 2, :]), w1_sb[:, k % RING, 0:4 * F], w_hi[:, k % 4, :],
                                ALU.subtract).then_inc(wlo_sb, 1)

            def x_low(t, k):
                dve.wait_ge(xT_sb, t + 1)
                V.tensor_tensor(rr(xT_lo[:, k % 2, :]), ps[k % 2][:, 0:H], xT[:, k % 2, :], ALU.subtract)\
                    .then_inc(xlo_sb, 1)

            def extra_expert(n, chained):
                chained(V.tensor_scalar(ov_one[:, n, :], ov[:, 1, :], ov_j[:], None, ALU.is_gt))
                chained(V.scalar_tensor_tensor(ov_one[:, n, :], ov[:, 2, :], ov_j[:], ov_one[:, n, :],
                                               ALU.is_le, ALU.mult))
                chained(V.tensor_tensor(ov[:, 3, :], ov_one[:, n, :], c_32("iota_e"), ALU.mult))
                chained(V.tensor_reduce(ov_s[:, 0:1], ov[:, 3, :], AX, ALU.add))
                V.tensor_copy(ov_e[:, n:n + 1], ov_s[0:1, 0:1]).then_inc(ov_expert_ready, 1)

            def extra_base(n, chained):
                chained(V.tensor_tensor(ov[:, 3, :], ov_one[:, n, :], ov[:, 2, :], ALU.mult))
                chained(V.tensor_reduce(ov_s[:, 1:2], ov[:, 3, :], AX, ALU.add))
                chained(V.scalar_tensor_tensor(ov_first[:, n:n + 1], ov_s[:, 1:2], float(-P), ov_base[:],
                                               ALU.mult, ALU.add))
                V.tensor_scalar(ov_j[:], ov_j[:], 1.0, None, ALU.add)
                chained(V.tensor_scalar(ov_base[:], ov_base[:], float(P), None, ALU.add))

            def extra_select(n, chained):
                chained(V.tensor_tensor(ov_sel[:], rank_f[:].rearrange("p (c e) -> p c e", e=E),
                                        ov_one[:, n, :].unsqueeze(1).to_broadcast([P, NC, E]), ALU.mult))

            def extra_place(n, chained):
                chained(V.tensor_reduce(ov_rank[:], ov_sel[:], AX, ALU.add))
                chained(V.tensor_scalar(ov_adj[:], ov_rank[:], ov_first[:, n:n + 1], None, ALU.subtract))

            def hot_half(n):
                part, shape = slice(n * (NC // 2), (n + 1) * (NC // 2)), [P, NC // 2, P]
                return V.tensor_tensor(ov_hot[:, part, :], c_32("iota_s").unsqueeze(1).to_broadcast(shape),
                                       bc(ov_adj[:, part], shape), ALU.is_equal)

            def extra_hot(n, chained):
                hot_half(0)

            def extra_hot_rest(n, chained):
                hot_half(1).then_inc(ov_hot_ready, 1)

            def extra_weight(r, n, chained):
                chained(V.tensor_tensor(ov_comb[:], rows[:, r, H:ROW], ov_one[:, n, :], ALU.mult))
                chained(V.tensor_reduce(ov_s[:, 4:5], ov_comb[:], AX, ALU.add))

            def extra_indices(n, bank):
                dve.wait_ge(ov_list_ps, n + 1)
                lst = bank[:, H:H + 1]
                link(indices(lst, (ov_t[:, 0:1], ov_t[:, 1:2]), gidx[:, E + n:E + n + 1], sidx[:, E + n:E + n + 1]))

            pieces = (extra_expert, extra_base, extra_select, extra_place, extra_hot, extra_hot_rest)
            w_low(0, 0)
            x_low(0, 0)
            dve.wait_ge(act_zero, 1)
            w_low(1, 1)
            gate_up(0, 0, rows[:, 0, H:H + 1])
            x_low(1, 1)

            def expert_dve(t, k, first=False, last=False):
                ahead = not (last and k >= RING + EXTRA - 2)
                if ahead:
                    w_low(t + 2, k + 2)
                if last and k >= RING - 1:
                    if k < RING + EXTRA - 1:
                        j = k - (RING - 1)
                        dve.wait_ge(sg_sb, E + j + 1)
                        extra_weight((k + 1) % AHEAD, j, link)
                        gate_up(E + j, k + 1, ov_s[:, 4:5])
                else:
                    gate_up(t + 1, k + 1, rows[:, (k + 1) % AHEAD, bass.ds(t + (H + 1), 1)])
                if ahead:
                    x_low(t + 2, k)
                if not first:
                    dve.wait_ge(acc_done[k % 2], (t - k) * 8 + 16 * (k // 2 - 1))
                V.tensor_copy(scol[:, k % 8:k % 8 + 1], sidx[:, bass.ds(t, 1)]).then_inc(scol_ready, 1)
                nxt = fetched_at(k) if last else k
                if nxt is not None:
                    r = nxt % AHEAD
                    V.tensor_copy(gcol[:, r:r + 1], gidx[:, bass.ds(t - k + nxt + AHEAD, 1)]).then_inc(gcol_ready, 1)

            pieces_at = {0: (extra_expert, 0), 1: (extra_base, 0), 2: (extra_expert, 1), 3: (extra_base, 1),
                         4: (extra_select, 0), 5: (extra_place, 0), 6: (extra_hot, 0), 7: (extra_hot_rest, 0),
                         8: (extra_select, 1), 9: (extra_place, 1), 10: (extra_hot, 1), 11: (extra_hot_rest, 1)}
            for k in range(4):
                expert_dve(k, k, first=True)
                piece, n = pieces_at[k]
                piece(n, link)
            with dve.Fori(0, E // RING - 1) as i:
                for k in range(4, RING + 4):
                    expert_dve(i * RING + k, k)
            for k in range(4, RING + EXTRA):
                if k - 1 in LISTED:
                    dve.wait_ge(y_sb, E - RING + k - 1)
                    extra_indices(LISTED.index(k - 1), ps[6 + (k - 2) % 2])
                expert_dve(E - RING + k, k, last=True)
                if k in pieces_at:
                    piece, n = pieces_at[k]
                    piece(n, link)

            n_ov = dve.value_load(ov_n[0:1, 0:1], min_val=0, max_val=E - 1)

            def ov_body(j):
                count = [0]

                def olink(ins):
                    count[0] += 1
                    ins.then_inc(ov_steps, 1)
                    dve.wait_ge(ov_steps, j * OV_LINKS + count[0])

                for piece in pieces:
                    piece(0, olink)
                dve.wait_ge(ov_list_ps, j + (EXTRA + 1))
                lst = ps[7][:, H:H + 1]
                V.tensor_scalar(ov_t[:, 0:1], lst, 0.0, float(SKIP + 1), ALU.is_equal, ALU.mult)
                olink(V.tensor_scalar(ov_t[:, 1:2], lst, 0.0, c_32("padrow"), ALU.is_equal, ALU.mult))
                dve.wait_ge(acc_done[0], j * 16 + 16 * (TILES // 2 + 1))
                V.scalar_tensor_tensor(ov_idx[:, 0:1], lst, -1.0, ov_t[:, 0:1], ALU.add, ALU.add)
                V.scalar_tensor_tensor(ov_idx[:, 1:2], lst, -1.0, ov_t[:, 1:2], ALU.add, ALU.add)\
                    .then_inc(ov_idx_ready, 1)
                dve.wait_ge(ov_rows_in, j * 16 + 16)
                extra_weight(0, 0, olink)
                w_low(j + TILES, 0)
                x_low(j + TILES, 0)
                dve.wait_ge(sg_sb, j + (TILES + 1))
                V.scalar_tensor_tensor(act[:, 0, 0:F], ps[2][:, F:2 * F], ov_s[:, 4:5], sg[:, 0, :],
                                       ALU.mult, ALU.mult).then_inc(act_sb, 1)
                assert count[0] == OV_LINKS, count

            OV_LINKS = 14
            with dve.If(n_ov > 0):
                with dve.Fori(0, n_ov) as j:
                    ov_body(j)

            dve.wait_ge(late_in, 32)
            def bias_kv(c):
                V.tensor_tensor(kv[:, c, :], kv[:, c, :], bkv_sb[:], ALU.add).then_inc(kvb_ready, 1)

            dve.wait_ge(kv_sb, NC)
            dve.wait_ge(q_sb, 4)
            dve.wait_ge(y_ps, n_ov + TILES)
            extra = [lambda c=c: bias_kv(c) for c in range(NC)]
            for f in extra[0:4]:
                f()
            for n in range(6):
                rows_n = P if n % 3 < 2 else FS - 2 * P
                dve.wait_ge(stmp_sb, n + 1)
                if n == 0:
                    dve.wait_ge(acc_done[0], n_ov * 16 + 16 * (TILES // 2 + 1))
                    dve.wait_ge(acc_done[1], 16 * (TILES // 2 + 1))
                if n >= 2:
                    dve.wait_ge(slo_sb, n - 1)
                V.tensor_tensor(sprod[0:rows_n, n % 2, :], ps[(n % 2) * 2 + 1][0:rows_n, :], stmp[0:rows_n, n % 2, :],
                                ALU.mult).then_inc(prod_sb, 1)
                if n < 2:
                    for f in extra[4 + 2 * n:6 + 2 * n]:
                        f()
                    if n == 1:
                        dve.wait_ge(kvb_ready, NC)
                        for c in range(NC):
                            V.tensor_tensor(ks[:, c, :], kv[:, c, 0:H], c_32("kscale"), ALU.mult).then_inc(ks_ready, 1)
                elif n in (3, 4):
                    dve.wait_ge(q_low, NG)
                    half = n - 3
                    for g in range(NG):
                        dve.wait_ge(kT_a, NG * half + g + 1)
                        part = slice(half * 512, (half + 1) * 512)
                        V.tensor_tensor(rr(kT_lo[:, g, part]), ps[4 + 2 * g + half][:], kT_hi[:, g, part],
                                        ALU.subtract).then_inc(kT_v, 1)
                elif n == 2:
                    for g in range(NG):
                        V.tensor_tensor(qsT[:, g, :].rearrange("p (c i) -> p c i", i=P),
                                        qT[:, g, :].rearrange("p (c i) -> p c i", i=P),
                                        c_32("qscale")[:, g * P:(g + 1) * P].unsqueeze(1).to_broadcast([P, NC, P]),
                                        ALU.mult).then_inc(qs_ready, 1)

            n_state = 0
            for u in range(2 * NC):
                c, g = u // 2, u % 2
                dve.wait_ge(s_ps, u + 1)
                if u >= 2:
                    dve.wait_ge(o_ps, u - 1)
                V.tensor_tensor(pT[:, u % 2, :], ps[u % 2][:],
                                c_32("decay")[:, g * HG * P:(g + 1) * HG * P], ALU.mult).then_inc(p_sb, 1)
                if u >= 2 and u % 2 == 0:
                    finish = c - 1
                    dve.wait_ge(xab_ready, finish + 1)
                    dve.wait_ge(o_ps, 2 * (finish + 1))
                    if finish >= 2:
                        dve.wait_ge(out_done[finish % 2], 16 * (finish // 2))
                    V.tensor_tensor(res[:, finish % 2, :], ps[4 + finish % 2][:, 0:H], acc_sb[1][:, finish, :],
                                    ALU.add).then_inc(res_sb, 1)
                if c % SEQ_CHUNKS < SEQ_CHUNKS - 1:
                    m = c % SEQ_CHUNKS
                    n_state += 1
                    dve.wait_ge(st_ps, n_state)
                    if m == 0:
                        V.tensor_tensor(state[:, 0, g, :], ps[6 + n_state % 2][:, 0:P], c_32("bdmask"), ALU.mult)\
                            .then_inc(st_sb, 1)
                    else:
                        dve.wait_ge(st_sb, n_state - 1)
                        link(V.tensor_tensor(st_t[:], ps[6 + n_state % 2][:, 0:P], c_32("bdmask"), ALU.mult))
                        V.scalar_tensor_tensor(state[:, m % 2, g, :], state[:, (m - 1) % 2, g, :],
                                               c_32("gc")[:, g:g + 1], st_t[:], ALU.mult, ALU.add).then_inc(st_sb, 1)
            dve.wait_ge(xab_ready, NC)
            dve.wait_ge(o_ps, 2 * NC)
            dve.wait_ge(out_done[(NC - 1) % 2], 16 * ((NC - 1) // 2))
            V.tensor_tensor(res[:, (NC - 1) % 2, :], ps[4 + (NC - 1) % 2][:, 0:H], acc_sb[1][:, NC - 1, :],
                            ALU.add).then_inc(res_sb, 1)

        @block.tensor
        def _(pe):
            mm = nc.tensor.matmul
            pe.wait_ge(zero_ready, 1)
            for _ in range(WARM_UP):
                mm(ps[7][:, 0:H], zero[:, 0:P], zero[:], start=True, stop=True)
            pe.wait_ge(ident_in, 16)
            for c in range(NC):
                pe.wait_ge(xn_ready, c + 1)
                for k in range(NG):
                    ins = nc.tensor.transpose(ps[2 * k + c // 4][:, (c % 4) * P:(c % 4 + 1) * P],
                                              tab[:, c, k * P:(k + 1) * P], ident)
                if c % 4 == 3:
                    ins.then_inc(xnT_ps, 1)
            pe.wait_ge(gate_in, 16)
            for c in range(NC):
                pe.wait_ge(xnT_a, c // 4 + 1)
                pe.wait_ge(xnT_v, c // 4 + 1)
                for k in range(NG):
                    ins = mm(ps[4][:, c * E:(c + 1) * E], xnT[:, k, c * P:(c + 1) * P], gate_sb[:, k, :],
                             start=(k == 0), stop=(k == NG - 1))
            ins.then_inc(logits_ps, 1)
            pe.wait_ge(wq_in, 16)

            def q_unit(m):
                g, n = m // 2, m % 2
                if m >= 2:
                    pe.wait_ge(q_sb, m - 1)
                for k in range(NG):
                    ins = mm(ps[m % 2][:], wq_sb[:, k, g * P:(g + 1) * P], xnT[:, k, n * 512:(n + 1) * 512],
                             start=(k == 0), stop=(k == NG - 1))
                ins.then_inc(q_ps, 1)

            q_unit(0)
            q_unit(1)
            pe.wait_ge(c16_in, 16)
            pe.wait_ge(chosen_ready, 1)
            mm(ps[5][:], c_16("tri"), chosen[:].rearrange("p c e -> p (c e)"), start=True, stop=False)
            for c in range(NC - 1):
                ins = mm(ps[5][:, (c + 1) * E:].rearrange("p (c e) -> p c e", e=E), c_16("ones"),
                   chosen[:, c:c + 1, :].to_broadcast([P, NC - 1 - c, E]), start=False, stop=(c == NC - 2))
            ins.then_inc(rank_ps, 1)
            for c in range(NC):
                ins = mm(ps[6][:, 0:E], c_16("ones"), chosen[:, c, :], start=(c == 0), stop=(c == NC - 1))
            ins.then_inc(rank_ps, 1)
            q_unit(2)
            q_unit(3)
            pe.wait_ge(xlo_ready, NG)
            pe.wait_ge(wkv_lo_ready, 1)
            pe.wait_ge(q_sb, 4)

            def kv_chunk(c):
                if c >= 4:
                    pe.wait_ge(kv_sb, c - 3)
                part = slice(c * P, (c + 1) * P)
                for k in range(NG):
                    passes = ((xn_hi[:, k, part], wkv_hi), (xn_lo[k][:, part], wkv_hi), (xn_hi[:, k, part], wkv_lo))
                    for n, (a, b) in enumerate(passes):
                        ins = mm(ps[c % 4][:], rr(a), rr(b[:, k, :]), start=(k == 0 and n == 0),
                                 stop=(k == NG - 1 and n == 2))
                ins.then_inc(kv_ps, 1)

            for c in range(4):
                kv_chunk(c)
            pe.wait_ge(hot_ready, 2)
            for g in range(8):
                for c in range(NC):
                    ins = mm(ps[7][:, g * 64:(g + 1) * 64], lo_hot[:, c * 8 + g, :, :].rearrange("p a e -> p (a e)"),
                             hi_hot[:, :, c, 8 * g:8 * g + 8], start=(c == 0), stop=(c == NC - 1))
            ins.then_inc(diag_ps, 1)
            kv_chunk(4)
            pe.wait_ge(diag_ready, 1)
            for b in range(8):
                lo = C16["place"][0] + 112 - 16 * b
                ins = mm(ps[4][:, 0:E], k16[:, lo:lo + P], diag[:, :, b, :], start=(b == 0), stop=(b == 7))
            ins.then_inc(slot_ps, 1)
            for c in range(5, NC):
                kv_chunk(c)

            def trans_x(t, k, rows_sem, rows_val, r):
                pe.wait_ge(rows_sem, rows_val)
                if not (isinstance(t, int) and t < 2):
                    pe.wait_ge(xlo_sb, t - 1)
                for h in range(NG):
                    ins = nc.tensor.transpose(ps[k % 2][:, h * P:(h + 1) * P], rows[:, r, h * P:(h + 1) * P], ident)
                ins.then_inc(xT_ps, 1)

            def gate_up(t, k, slot, w_sem, w_val):
                pe.wait_ge(w_sem, w_val)
                if not (isinstance(t, int) and t < 2):
                    pe.wait_ge(act_sb, t - 1)
                pe.wait_ge(whi_sb, t + 1)
                pe.wait_ge(xT_sb, t + 1)
                for n, (a, b, ready) in enumerate(((xT, w_hi, None), (xT_lo, w_hi, xlo_sb), (xT, w_lo, wlo_sb))):
                    if ready is not None:
                        pe.wait_ge(ready, t + 1)
                    for h in range(NG):
                        ins = mm(ps[2 + k % 2][:, 0:2 * F], rr(a[:, k % 2, h * P:(h + 1) * P]),
                                 rr(b[:, k % (2 if b is w_lo else 4), h * 2 * F:(h + 1) * 2 * F]),
                                 start=(n == 0 and h == 0), stop=(n == 2 and h == NG - 1))
                ins.then_inc(gu_ps, 1)

            def trans_act(t, k):
                pe.wait_ge(act_sb, t + 1)
                if not (isinstance(t, int) and t < 2):
                    pe.wait_ge(aT_sb, t - 1)
                for h in range(2):
                    ins = nc.tensor.transpose(ps[4 + k % 2][:, h * P:(h + 1) * P],
                                              act[:, k % 2, h * P:(h + 1) * P], ident)
                ins.then_inc(aT_ps, 1)

            def token_list(bank):
                for c in range(NC):
                    ins = mm(bank[:, H:H + 1], ov_hot[:, c, :], k16[:, C16["tokc"][0] + c:C16["tokc"][0] + c + 1],
                             start=(c == 0), stop=(c == NC - 1))
                ins.then_inc(ov_list_ps, 1)

            def down(t, k, slot, listed=None):
                if not (isinstance(t, int) and t < 2):
                    pe.wait_ge(y_sb, t - 1)
                if listed is not None:
                    pe.wait_ge(ov_hot_ready, listed + 1)
                    token_list(ps[6 + k % 2])
                pe.wait_ge(aT_sb, t + 1)
                mm(ps[6 + k % 2][:, 0:H], aT[:, k % 2, 0:P], w1_sb[:, slot, 4 * F:W1C], start=True, stop=False)
                mm(ps[6 + k % 2][:, 0:H], aT[0:F2, k % 2, P:2 * P], w2_sb[0:F2, slot, :],
                   start=False, stop=True).then_inc(y_ps, 1)

            pe.wait_ge(kv_sb, NC)
            pe.wait_ge(gcol_ready, 1)
            trans_x(0, 0, rows_in[0], 16, 0)
            gate_up(0, 0, 0, w_in[0], 32)
            trans_x(1, 1, rows_in[1], 16, 1)

            def expert_pe(i, k, ahead=2, first=False, listed=None):
                t = i * RING + k
                if ahead >= 1:
                    k1 = k + 1
                    gate_up(t + 1, k1, k1 % RING, w_in[k1 % RING], i * 32 + 32 * (k1 // RING + 1))
                if ahead >= 2:
                    k2 = k + 2
                    trans_x(t + 2, k2, rows_in[k2 % AHEAD], i * (16 * (RING // AHEAD)) + 16 * (k2 // AHEAD + 1),
                            k2 % AHEAD)
                trans_act(t, k)
                if not first:
                    down(t - 1, k - 1, (k - 1) % RING, listed)

            for k in range(4):
                expert_pe(0, k, first=(k == 0))
            with pe.Fori(0, E // RING - 1) as i:
                for k in range(4, RING + 4):
                    expert_pe(i, k)
            for k in range(4, RING + EXTRA):
                expert_pe(E // RING - 1, k, ahead=min(2, RING + EXTRA - 1 - k), listed=LISTED.index(k) if k in LISTED else None)
            down(TILES - 1, RING + EXTRA - 1, EXTRA - 1)

            pe.wait_ge(ov_ready, 1)
            n_ov = pe.value_load(ov_n[0:1, 0:1], min_val=0, max_val=E - 1)
            with pe.If(n_ov > 0):
                with pe.Fori(0, n_ov) as j:
                    t = j + TILES
                    pe.wait_ge(y_sb, t)
                    pe.wait_ge(ov_hot_ready, j + (EXTRA + 1))
                    token_list(ps[7])
                    trans_x(t, 0, ov_rows_in, j * 16 + 16, 0)
                    gate_up(t, 0, 0, ov_w_in, j * 32 + 32)
                    trans_act(t, 0)
                    down(t, 0, 0)

            pe.wait_ge(shared_in, 64)
            for m in range(6):
                n, f = m // 3, m % 3
                fw = P if f < 2 else FS - 2 * P
                if m in (3, 4):
                    if m == 3:
                        pe.wait_ge(kvb_ready, NC)
                        pe.wait_ge(y_sb, n_ov + TILES)
                    half = m - 3
                    for c in range(4 * half, 4 * half + 4):
                        for g in range(NG):
                            ins = nc.tensor.transpose(ps[4 + 2 * g + half][:, (c % 4) * P:(c % 4 + 1) * P],
                                                      kv[:, c, g * P:(g + 1) * P], ident)
                    ins.then_inc(kT_ps, 1)
                if m >= 2:
                    pe.wait_ge(prod_sb, m - 1)
                else:
                    pe.wait_ge(y_sb, TILES)
                for o in range(2):
                    for k in range(NG):
                        ins = mm(ps[(m % 2) * 2 + o][0:fw, :], sgu_sb[:, k, o * FS + f * P:o * FS + f * P + fw],
                                 xnT[:, k, n * 512:(n + 1) * 512], start=(k == 0), stop=(k == NG - 1))
                ins.then_inc(sgu_ps, 1)
            def scores(u):
                c, g = u // 2, u % 2
                if u >= 2:
                    pe.wait_ge(p_sb, u - 1)
                else:
                    pe.wait_ge(prod_sb, 5)
                pe.wait_ge(qhi_sb, u + 1)
                pe.wait_ge(qlo_sb, u + 1)
                passes = ((kT_hi, qbd_hi), (kT_lo, qbd_hi), (kT_hi, qbd_lo))
                for n, (a, b) in enumerate(passes):
                    ins = mm(ps[u % 2][:], rr(a[:, g, c * P:(c + 1) * P]),
                             rr(b[:, u % 2, :, :].rearrange("p h i -> p (h i)")), start=(n == 0), stop=(n == 2))
                ins.then_inc(s_ps, 1)

            pe.wait_ge(kT_a, 2 * NG)
            pe.wait_ge(kT_v, 2 * NG)
            pe.wait_ge(qs_ready, NG)
            pe.wait_ge(ks_ready, NC)
            scores(0)
            n_state = 0
            for u in range(2 * NC):
                c, g, m = u // 2, u % 2, (u // 2) % SEQ_CHUNKS
                bank = ps[4 + c % 2]
                if u + 1 < 2 * NC:
                    scores(u + 1)
                if m < SEQ_CHUNKS - 1:
                    n_state += 1
                    if n_state >= 3:
                        pe.wait_ge(st_sb, n_state - 2)
                    mm(ps[6 + n_state % 2][:, 0:P], ks[:, c, g * P:(g + 1) * P], kv[:, c, H + g * P:H + (g + 1) * P],
                       start=True, stop=True).then_inc(st_ps, 1)
                if g == 0:
                    if c == 0:
                        pe.wait_ge(sdn_lo_ready, 2)
                    if c % 4 == 0:
                        pe.wait_ge(slo_sb, 3 if c < 4 else 6)
                    if c >= 2:
                        pe.wait_ge(res_sb, c - 1)
                    for f in range(3):
                        fw = P if f < 2 else FS - 2 * P
                        for n, (a, b) in enumerate(((sact_hi, sdn_hi), (sact_lo, sdn_hi), (sact_hi, sdn_lo))):
                            mm(bank[:, 0:H], rr(a[0:fw, f, c * P:(c + 1) * P]), rr(b[0:fw, f, :]),
                               start=(f == 0 and n == 0), stop=False)
                if m > 0:
                    pe.wait_ge(st_sb, (c // SEQ_CHUNKS) * 2 * (SEQ_CHUNKS - 1) + 2 * (m - 1) + g + 1)
                    mm(bank[:, g * P:(g + 1) * P], qsT[:, g, c * P:(c + 1) * P], state[:, (m - 1) % 2, g, :],
                       start=False, stop=False)
                pe.wait_ge(p_sb, u + 1)
                for h in range(HG):
                    at = g * P + h * D
                    ins = mm(bank[:, at:at + D], pT[:, u % 2, h * P:(h + 1) * P], kv[:, c, H + at:H + at + D],
                             start=False, stop=(h == HG - 1 and g == 1))
                ins.then_inc(o_ps, 1)


def _constants():
    import numpy as np
    p = np.arange(P)
    betas = np.linspace(np.log2(1.0 / 32.0), np.log2(1.0 / 512.0), HEADS).astype(np.float32)
    g = (np.float32(1.0) - np.exp2(betas).astype(np.float32)).astype(np.float64)
    a = {}
    a["ident"] = np.eye(P)
    a["mask8"] = (p[:, None] % 8 == np.arange(8)[None, :])
    a["padrow"] = (T + 1 + p)[:, None]
    a["iota_e"] = np.tile(np.arange(E), (P, 1))
    a["iota_s"] = np.tile(np.arange(P), (P, 1))
    a["hmask"] = (p[:, None] // D == np.arange(HG)[None, :])
    head = np.arange(NG)[None, :] * HG + p[:, None] // D
    a["gc"] = g[head] ** P
    a["bdmask"] = (p[:, None] // D == p[None, :] // D)
    a["kscale"] = g[np.arange(H)[None, :] // D] ** (P - 1 - p)[:, None]
    a["qscale"] = (g[head][:, :, None] ** (p + 1)[None, None, :]).reshape(P, NG * P)
    diff = p[None, None, :] - p[:, None, None]
    a["decay"] = np.where(diff >= 0, g[None, :, None] ** np.maximum(diff, 0), 0.0).reshape(P, HEADS * P)
    c32 = np.concatenate([np.asarray(a[n], np.float32) for n in C32], 1)
    b = {}
    b["tri"] = (p[:, None] < p[None, :])
    b["ones"] = np.ones((P, P))
    b["place"] = (np.arange(240)[None, :] - 112 == p[:, None] // 8)
    tok = np.arange(NC)[None, :] * P + p[:, None] + 1
    b["tok"] = np.repeat(tok, E, axis=1)
    b["tokc"] = tok
    c16 = np.concatenate([np.asarray(b[n], np.float16) for n in C16], 1)
    return c32, c16


def kernel(**inputs):
    import numpy as np
    import concourse.bacc as bacc
    from concourse.bass_utils import run_bass_kernel_spmd

    v = {n.replace("L0_attn_", "").replace("L0_ffn_", ""): np.asarray(a) for n, a in inputs.items()}

    def halves(w):
        return np.ascontiguousarray(w.reshape(NG, P, -1).transpose(1, 0, 2))

    c32, c16 = _constants()
    gu = v["w_gate_up"].transpose(0, 2, 1).reshape(E, NG, P, 2 * F).transpose(0, 2, 1, 3).reshape(E, P, NG * 2 * F)
    dn = v["w_down"].transpose(0, 2, 1)
    arrays = {
        "x": v["x"].reshape(T, H),
        "wq": halves(v["Wq"]),
        "wkv": halves(np.concatenate([v["Wk"], v["Wv"]], 1)),
        "bq": np.ascontiguousarray(v["bq"].reshape(NG, P).T),
        "bkv": np.concatenate([v["bk"], v["bv"]]),
        "gate": halves(v["gate_w"].T),
        "sgu": halves(v["ws_gate_up"].T),
        "sdn": np.ascontiguousarray(v["ws_down"].T),
        "w1": np.ascontiguousarray(np.concatenate([gu, dn[:, 0:F1, :]], 2)),
        "w2": np.ascontiguousarray(dn[:, F1:F, :]),
        "c32": c32,
        "c16": c16,
    }
    nc = bacc.Bacc("TRN2", target_bir_lowering=False, num_devices=1)
    args = [nc.dram_tensor(f"in_{n}", a.shape, mybir.dt.from_np(a.dtype), kind="ExternalInput").ap()
            for n, a in arrays.items()]
    out = nc.dram_tensor("out", (T, H), mybir.dt.float32, kind="ExternalOutput").ap()
    build(nc, *args, out)
    r = run_bass_kernel_spmd(nc, [{f"in_{n}": a for n, a in arrays.items()}], core_ids=[0])
    return r.results[0]["out"].reshape(2, T // 2, H)
```
